# Optimizing a Trainium2 kernel written in Bass

```python
import numpy as np
import jax
import jax.numpy as jnp

def _softmax(x, axis=-1):
    return jax.nn.softmax(x, axis=axis)

def _gelu(x):
    return jax.nn.gelu(x, approximate=True)

def _silu(x):
    return jax.nn.silu(x)

def _sigmoid(x):
    return jax.nn.sigmoid(x)

def _layernorm(x, axis=-1, eps=1e-05):
    m = jnp.mean(x, axis=axis, keepdims=True)
    v = jnp.var(x, axis=axis, keepdims=True)
    return (x - m) / jnp.sqrt(v + eps)

def _scatter_add(tgt, idx, src, axis=0):
    return tgt.at[idx].add(src)

def _segment_sum(src, seg, n):
    return jax.ops.segment_sum(src, seg, n)
kernel_name = 'mk_recurrent_d2_jaxref_r8_1ba477'

def setup_inputs(seed: int=0):
    np.random.seed(seed)
    _w = jnp.asarray

    def _L0_attn_setup():
        import jax, jax.numpy as jnp
        import numpy as np
        B, L, D, H = (4, 512, 256, 16)
        HD = D // H
        EPS = 1e-09

        def phi(x):
            return jax.nn.elu(x) + 1.0
        key = jax.random.key(seed)
        k1, k2, k3 = jax.random.split(key, 3)
        x = jax.random.normal(k1, (B, L, D), dtype=jnp.float32)
        W_qkv = jax.random.normal(k2, (3 * D, D), dtype=jnp.float32) * D ** (-0.5)
        W_out = jax.random.normal(k3, (D, D), dtype=jnp.float32) * D ** (-0.5)
        return {'x': x, 'W_qkv': W_qkv, 'W_out': W_out}
    _L0_attn_in = _L0_attn_setup()

    def _L0_ffn_setup():
        import jax, jax.numpy as jnp
        import numpy as np
        EPS = 1e-08

        def ternary_quantize(w):
            threshold = 0.7 * jnp.mean(jnp.abs(w), axis=-1, keepdims=True)
            q = jnp.where(w > threshold, 1.0, jnp.where(w < -threshold, -1.0, 0.0)).astype(w.dtype)
            return w + jax.lax.stop_gradient(q - w)
        key = jax.random.key(seed)
        k1, k2, k3 = jax.random.split(key, 3)
        B, S, D_in, D_out = (4, 256, 256, 256)
        x = jax.random.normal(k1, (B, S, D_in), dtype=jnp.float32)
        bound = np.sqrt(6.0 / D_in)
        weight = jax.random.uniform(k2, (D_out, D_in), dtype=jnp.float32, minval=-bound, maxval=bound)
        bias = jax.random.normal(k3, (D_out,), dtype=jnp.float32) * 0.01
        return {'x': x, 'weight': weight, 'bias': bias}
    _L0_ffn_in = _L0_ffn_setup()

    def _L1_attn_setup():
        import jax, jax.numpy as jnp
        import numpy as np
        B, S, D, H = (2, 256, 256, 16)
        HD = D // H
        NEG = jnp.float32(-1000000000.0)
        key = jax.random.key(seed)
        ks = jax.random.split(key, 6)
        slopes = np.array([2 ** (-8.0 * (i + 1) / H) for i in range(H)], dtype=np.float32)
        return {'hidden_states': jax.random.normal(ks[0], (B, S, D), jnp.float32), 'qkv_w': jax.random.normal(ks[1], (3 * D, D), jnp.float32) * (1.0 / np.sqrt(D)), 'qkv_b': jax.random.normal(ks[2], (3 * D,), jnp.float32) * 0.01, 'out_w': jax.random.normal(ks[3], (D, D), jnp.float32) * (1.0 / np.sqrt(D)), 'out_b': jax.random.normal(ks[4], (D,), jnp.float32) * 0.01, 'alibi_slopes': jnp.asarray(slopes)}
    _L1_attn_in = _L1_attn_setup()

    def _L1_ffn_setup():
        import jax, jax.numpy as jnp
        import numpy as np
        NUM_EXPERTS = 8
        TOP_K = 2
        key = jax.random.key(seed)
        ks = jax.random.split(key, 7)
        B, S, H, I, E = (4, 256, 256, 256, NUM_EXPERTS)
        sc = 0.02
        return {'hidden_states': jax.random.normal(ks[0], (B, S, H), dtype=jnp.float32), 'gate_w': jax.random.normal(ks[1], (E, H), dtype=jnp.float32) * sc, 'gate_b': jax.random.normal(ks[2], (E,), dtype=jnp.float32) * sc, 'w1': jax.random.normal(ks[3], (E, 2 * I, H), dtype=jnp.float32) * sc, 'b1': jax.random.normal(ks[4], (E, 2 * I), dtype=jnp.float32) * sc, 'w2': jax.random.normal(ks[5], (E, H, I), dtype=jnp.float32) * sc, 'b2': jax.random.normal(ks[6], (E, H), dtype=jnp.float32) * sc}
    _L1_ffn_in = _L1_ffn_setup()
    _d = {'L0_attn_x': _L0_attn_in['x'], 'L0_attn_W_qkv': _L0_attn_in['W_qkv'], 'L0_attn_W_out': _L0_attn_in['W_out'], 'L0_ffn_weight': _L0_ffn_in['weight'], 'L0_ffn_bias': _L0_ffn_in['bias'], 'L1_attn_qkv_w': _L1_attn_in['qkv_w'], 'L1_attn_qkv_b': _L1_attn_in['qkv_b'], 'L1_attn_out_w': _L1_attn_in['out_w'], 'L1_attn_out_b': _L1_attn_in['out_b'], 'L1_attn_alibi_slopes': _L1_attn_in['alibi_slopes'], 'L1_ffn_gate_w': _L1_ffn_in['gate_w'], 'L1_ffn_gate_b': _L1_ffn_in['gate_b'], 'L1_ffn_w1': _L1_ffn_in['w1'], 'L1_ffn_b1': _L1_ffn_in['b1'], 'L1_ffn_w2': _L1_ffn_in['w2'], 'L1_ffn_b2': _L1_ffn_in['b2']}
    _x0 = _d['L0_attn_x']
    _d['L0_attn_x'] = jax.random.normal(jax.random.fold_in(jax.random.key(seed), 1), (1, 2048, 256), dtype=_x0.dtype)
    del _x0
    return _d

def reference(L0_attn_x, L0_attn_W_qkv, L0_attn_W_out, L0_ffn_weight, L0_ffn_bias, L1_attn_qkv_w, L1_attn_qkv_b, L1_attn_out_w, L1_attn_out_b, L1_attn_alibi_slopes, L1_ffn_gate_w, L1_ffn_gate_b, L1_ffn_w1, L1_ffn_b1, L1_ffn_w2, L1_ffn_b2):

    def _L0_attn_ref(x, W_qkv, W_out):
        import jax, jax.numpy as jnp
        import numpy as np
        B, L, D, H = (4, 512, 256, 16)
        HD = D // H
        EPS = 1e-09

        def phi(x):
            return jax.nn.elu(x) + 1.0
        b, l, d = x.shape
        qkv = x @ W_qkv.T
        q, k, v = jnp.split(qkv, 3, axis=-1)
        q = q.reshape(b, l, H, HD).transpose(0, 2, 1, 3)
        k = k.reshape(b, l, H, HD).transpose(0, 2, 1, 3)
        v = v.reshape(b, l, H, HD).transpose(0, 2, 1, 3)
        q = phi(q)
        k = phi(k)
        kv_cumsum = jnp.cumsum(k * v, axis=2)
        k_cumsum = jnp.cumsum(k, axis=2)
        out = q * kv_cumsum / (q * k_cumsum + EPS)
        out = out.transpose(0, 2, 1, 3).reshape(b, l, d)
        return out @ W_out.T * HD ** (-0.5)

    def _L0_ffn_ref(x, weight, bias):
        import jax, jax.numpy as jnp
        import numpy as np
        EPS = 1e-08

        def ternary_quantize(w):
            threshold = 0.7 * jnp.mean(jnp.abs(w), axis=-1, keepdims=True)
            q = jnp.where(w > threshold, 1.0, jnp.where(w < -threshold, -1.0, 0.0)).astype(w.dtype)
            return w + jax.lax.stop_gradient(q - w)
        q_weight = ternary_quantize(weight)
        return jnp.einsum('bsi,oi->bso', x, q_weight) + bias

    def _L1_attn_ref(hidden_states, qkv_w, qkv_b, out_w, out_b, alibi_slopes):
        import jax, jax.numpy as jnp
        import numpy as np
        B, S, D, H = (2, 256, 256, 16)
        HD = D // H
        NEG = jnp.float32(-1000000000.0)
        b, s, d = hidden_states.shape
        qkv = hidden_states @ qkv_w.T + qkv_b
        q, k, v = jnp.split(qkv, 3, axis=-1)
        q = q.reshape(b, s, H, HD)
        k = k.reshape(b, s, H, HD)
        v = v.reshape(b, s, H, HD)
        scale = 1.0 / np.sqrt(HD)
        scores = jnp.einsum('bqhd,bkhd->bhqk', q, k) * scale
        pos = jnp.arange(s)
        rel = (pos[None, :] - pos[:, None]).astype(jnp.float32)
        bias = alibi_slopes[:, None, None] * rel
        causal = pos[None, :] <= pos[:, None]
        scores = jnp.where(causal[None, None], scores + bias[None], NEG)
        attn = jax.nn.softmax(scores, axis=-1)
        out = jnp.einsum('bhqk,bkhd->bqhd', attn, v).reshape(b, s, d)
        out = out @ out_w.T + out_b
        return out

    def _L1_ffn_ref(hidden_states, gate_w, gate_b, w1, b1, w2, b2):
        import jax, jax.numpy as jnp
        import numpy as np
        NUM_EXPERTS = 8
        TOP_K = 2
        B, S, H = hidden_states.shape
        x = hidden_states.reshape(-1, H)
        logits = x @ gate_w.T + gate_b
        top_vals, top_idx = jax.lax.top_k(logits, TOP_K)
        routing = jax.nn.softmax(top_vals.astype(jnp.float32), axis=-1).astype(x.dtype)
        out = jnp.zeros_like(x)
        E = w1.shape[0]
        for e in range(E):
            h = x @ w1[e].T + b1[e]
            x_glu = h[:, 0::2]
            x_lin = h[:, 1::2]
            y = x_glu * jax.nn.sigmoid(1.702 * x_glu) * (x_lin + 1.0)
            ye = y @ w2[e].T + b2[e]
            we = jnp.sum(routing * (top_idx == e), axis=-1)
            out = out + ye * we[:, None]
        return out.reshape(B, S, H)
    x = L0_attn_x
    xn = _layernorm(x, axis=-1)
    s = _L0_attn_ref(xn, L0_attn_W_qkv, L0_attn_W_out)
    g = _silu(_L0_ffn_ref(xn, L0_ffn_weight, L0_ffn_bias))
    x = x + s * g
    xn = _layernorm(x, axis=-1)
    s = _L1_attn_ref(xn, L1_attn_qkv_w, L1_attn_qkv_b, L1_attn_out_w, L1_attn_out_b, L1_attn_alibi_slopes)
    g = _silu(_L1_ffn_ref(xn, L1_ffn_gate_w, L1_ffn_gate_b, L1_ffn_w1, L1_ffn_b1, L1_ffn_w2, L1_ffn_b2))
    x = x + s * g
    return x

_drawn_inputs = setup_inputs


def setup_inputs(seed=0):
    import zlib

    import numpy as np

    out = dict(_drawn_inputs(seed))
    spreads = {}
    factors = {'L0_ffn_bias': 8.0,
     'L1_attn_qkv_w': 6.798,
     'L1_attn_qkv_b': 8.0,
     'L1_attn_out_w': 6.313,
     'L1_attn_out_b': 200.0,
     'L1_attn_alibi_slopes': 8.0,
     'L1_ffn_gate_w': 7.262,
     'L1_ffn_gate_b': 8.0,
     'L1_ffn_w1': 6.836,
     'L1_ffn_b1': 8.0,
     'L1_ffn_w2': 6.656,
     'L1_ffn_b2': 8.0}
    for name, (base, spread) in spreads.items():
        noise = np.random.default_rng([zlib.crc32(name.encode()), seed]).standard_normal(out[name].shape)
        drawn = base * np.exp(spread * noise) if base else spread * noise
        out[name] = jnp.asarray(drawn.astype(out[name].dtype))
    for name, factor in factors.items():
        out[name] = (out[name] * factor).astype(out[name].dtype)
    return out
```

```python
from contextlib import ExitStack

import concourse.bass as bass
from concourse import mybir

F32, F16, BF16 = mybir.dt.float32, mybir.dt.float16, mybir.dt.bfloat16
ALU = mybir.AluOpType
ACT = mybir.ActivationFunctionType
AX = mybir.AxisListType

P = 128
S, D = 2048, 256
H, HD = 16, 16
KK = D // P
NT = S // P
CH = 512
NC = S // CH
TC = CH // P
E, I = 8, 256
WS = 16.0
LN_EPS = 1e-5
L0_EPS = 1e-9

POS = 12
SPLITS = ((0, 0, 0, 1, 1, 2), (0, 1, 2, 0, 1, 0))
ROWS_A = POS + 6 * HD
ROWS_B = ROWS_A + 3

A_ORDER = (3, 0, 1, 2)
B_ORDER = (0, 3, 2, 1)
N_A = [TC * (a + 1) for a in A_ORDER]
N_B = [TC * (b + 1) for b in B_ORDER]
OFF_A = [sum(N_A[:s]) for s in range(NC)]
OFF_B = [sum(N_B[:s]) for s in range(NC)]
PER_HEAD = sum(N_A)
RING = 5
LAG = 3
STEPS = 16

UNITS = (((0, 0, 0, 0, 4, 2, 4, 6, 7), (1, 1, 0, 8, 12, 2, 12, 14, 15)),
         ((2, 0, 1, 1, 7, 1, 7, 9, 13),),
         ((3, 1, 1, 1, 7, 1, 7, 9, 13),),
         ())
FILLS = ((), ((0, 0, 0, 14, 15),), ((1, 0, 1, 14, 15),), ((2, 1, 0, 8, 9), (3, 1, 1, 12, 13)))
T_HEADS, T_RCP, T_NORM, T_MAXT, T_MAXC = 2, 3, 4, 6, 7


def share(n, t, steps):
    return range(min(n, n * t // steps), min(n, n * (t + 1) // steps))


def ds(start, size):
    return bass.ds(start, size)


def build(nc, x, w_qkv0, w_out0, w_ffn, b_ffn, w_qkv1, b_qk1, b_v1, w_out1, b_out1, slopes, pos_rows, pick,
          masks, ident, sel, gate_w, gate_b, w1, b1, w2, b2, out):
    ctx = ExitStack()
    with ctx:
        def sb(name, shape, dt=F32):
            return ctx.enter_context(nc.sbuf_tensor(name, shape, dt))

        def sem(name):
            return ctx.enter_context(nc.semaphore(name))

        XO = sb("XO", [P, NT, D])
        ACC = sb("ACC", [P, NT, D])
        XTH = sb("XTH", [P, KK, S], F16)
        XTL = sb("XTL", [P, KK, S], F16)
        W1H = sb("W1H", [P, E * 1024], F16)
        W1L = sb("W1L", [P, E * 1024], F16)
        W2 = sb("W2", [P, E, KK, D])
        VV = sb("VV", [P, NT, D])
        OPS = sb("OPS", [P, 4, 2, S], BF16)
        PR = sb("PR", [P, RING, CH])
        YT = sb("YT", [P, 2, KK, CH])
        U = sb("U", [P, 2, CH])
        VS = sb("VS", [P, 2, NT, 32])
        STG = sb("STG", [P, 2048])
        WO1 = sb("WO1", [P, KK, D])
        POSR = sb("POSR", [POS, 2, S], BF16)
        PICK = sb("PICK", [POS, 2, 4])
        SLB = sb("SLB", [POS, H])
        SLR = sb("SLR", [POS, H])
        SLP = sb("SLP", [POS, 3, H], BF16)
        SCL = sb("SCL", [POS, 2, H])
        MASK = sb("MASK", [P, 3, P], BF16)
        IDN = sb("IDN", [P, P])
        SEL = sb("SEL", [P, HD + 1])
        MV = sb("MV", [P, NT, 2])
        BST = sb("BST", [P, TC, 6])
        RSTD = sb("RSTD", [P, NT])
        VEPS = sb("VEPS", [P, NT])
        HALF = sb("HALF", [P, NT])
        ONE1 = sb("ONE1", [1, 2, P])
        ONES = sb("ONES", [P, 1])
        ZERO = sb("ZERO", [P, P], BF16)
        NIL = sb("NIL", [P, 1])
        ONEB = sb("ONEB", [P, CH], BF16)
        BROW = sb("BROW", [1, 3, D])
        GBR = sb("GBR", [1, E])
        BQK = sb("BQK", [P, 4])
        CAR = sb("CAR", [P, 4, 1])
        TH = sb("TH", [P, 2, CH])
        GT = sb("GT", [P, 2, CH])
        PM = sb("PM", [P, 2, TC, NC])
        NM = sb("NM", [P, 2, TC])
        NR = sb("NR", [P, 2, 2, TC])
        NP = sb("NP", [P, 2, 3, TC], BF16)
        MT = sb("MT", [12, 2, P], BF16)
        RC = sb("RC", [P, 2, TC])
        GW = sb("GW", [P, KK, E])
        GWH = sb("GWH", [P, KK, E], F16)
        GWL = sb("GWL", [P, KK, E], F16)
        LG = sb("LG", [P, NT, E])
        TOP = sb("TOP", [P, 4, NT])
        WE = sb("WE", [P, NT, E])
        WES = sb("WES", [P, NT, E])
        B1 = sb("B1", [P, E, 2, 2])
        B1S = sb("B1S", [P, E, 2, 2])
        B1T = sb("B1T", [P, E, 2])

        ops32 = OPS[:, :, :, :].rearrange("p a b s -> p (a b s)").bitcast(F32)
        EX = ops32[:, 0:2048].rearrange("p (m n) -> p m n", m=4)
        RE = ops32[:, 2048:4096].rearrange("p (m n) -> p m n", m=4)
        PH = ops32[:, 4096:6144].rearrange("p (m n) -> p m n", m=4)
        KV = ops32[:, 6144:7168].rearrange("p (m n) -> p m n", m=2)
        KC = ops32[:, 7168:8192].rearrange("p (m n) -> p m n", m=2)
        pr32 = PR[:, :, :].rearrange("p r n -> p (r n)")
        NUM = pr32[:, 0:1024].rearrange("p (m n) -> p m n", m=2)
        DEN = pr32[:, 1024:2048].rearrange("p (m n) -> p m n", m=2)
        yt32 = YT[:, :, :, :].rearrange("p a b n -> p (a b n)")
        WQH = yt32[:, 0:768].bitcast(F16).rearrange("p (k n) -> p k n", k=KK)
        RT = yt32[:, 768:1280].rearrange("p (a t e) -> p a t e", a=4, t=NT)
        WQL = U[:, :, :].rearrange("p a n -> p (a n)")[:, 0:768].bitcast(F16).rearrange("p (k n) -> p k n", k=KK)
        WET = pr32[0:E, 0:S]
        B2 = pr32[0:E, S:S + D]
        TQ = pr32[:, 0:2 * CH].rearrange("p (m n) -> p m n", m=2)
        KVC = YT[:, 0]
        XN = ACC[:, 0:TC, :]
        OT0 = YT[:, 1]
        vv32 = VV[:, :, :].rearrange("p a b -> p (a b)")
        W0H = vv32[:, 0:768].bitcast(F16).rearrange("p (k n) -> p k n", k=KK)
        W0L = vv32[:, 768:1536].bitcast(F16).rearrange("p (k n) -> p k n", k=KK)
        FH = vv32[:, 1536:1792].bitcast(F16).rearrange("p (k n) -> p k n", k=KK)
        FL = vv32[:, 1792:2048].bitcast(F16).rearrange("p (k n) -> p k n", k=KK)
        WO0 = vv32[:, 2048:2560].rearrange("p (k n) -> p k n", k=KK)
        WF = vv32[:, 2560:3072].rearrange("p (k n) -> p k n", k=KK)
        QF = vv32[:, 3072:3584].rearrange("p (k n) -> p k n", k=KK)
        NF = vv32[:, 3584:4096].rearrange("p (k n) -> p k n", k=KK)
        QV = ops32[:, 0:2048].rearrange("p (m n) -> p m n", m=4)
        QR = ops32[:, 2048:4096].rearrange("p (m n) -> p m n", m=4)
        QP = ops32[:, 4096:7168].bitcast(BF16).rearrange("p (m j n) -> p m j n", m=4, j=3)

        parts = nc.dram_tensor("qk_parts", (2, 3, D, S), BF16, kind="Internal").ap()
        x1_dram = nc.dram_tensor("x1_rows", (P, NT, D), F32, kind="Internal").ap()

        PS = [ctx.enter_context(nc.psum_tensor(f"bank{i}", [P, CH], F32)) for i in range(8)]
        MTP = PS[7][0:3 * TC, 256:256 + P // 2].bitcast(BF16)

        w_in0, cast_in, w_ffn_in, w_out_in, w_q1_in = (
            sem("w_in0"), sem("cast_in"), sem("w_ffn_in"), sem("w_out_in"), sem("w_q1_in"))
        small_in, const_in, w2_in, memset_done, w0h = (
            sem("small_in"), sem("const_in"), sem("w2_in"), sem("memset_done"), sem("w0h"))
        w0l, ffn_thr, ffn_q, ffn_t, ffn_h = (
            sem("w0l"), sem("ffn_thr"), sem("ffn_q"), sem("ffn_t"), sem("ffn_h"))
        ffn_split, w1h_done, w1l_done, wq1h, wq1l = (
            sem("ffn_split"), sem("w1h_done"), sem("w1l_done"), sem("wq1h"), sem("wq1l"))
        stats, var_eps, rstd_done, xn, xt_ps = (
            sem("stats"), sem("var_eps"), sem("rstd_done"), sem("xn"), sem("xt_ps"))
        xth, xtl, proj, exps, relus = (
            sem("xth"), sem("xtl"), sem("proj"), sem("exps"), sem("relus"))
        phi_k, phi_q, scan_k, v_read, scan_kv = (
            sem("phi_k"), sem("phi_q"), sem("scan_k"), sem("v_read"), sem("scan_kv"))
        nd, nd2, numden, rcp, outT = (
            sem("nd"), sem("nd2"), sem("numden"), sem("rcp"), sem("outT"))
        z_ps, s_ps, gate_th, gate_a, gate_mid = (
            sem("z_ps"), sem("s_ps"), sem("gate_th"), sem("gate_a"), sem("gate_mid"))
        x1_add, x1_spill, qk_ps, qk_v, qk_p0 = (
            sem("x1_add"), sem("x1_spill"), sem("qk_ps"), sem("qk_v"), sem("qk_p0"))
        qk_r1, qk_p1, qk_p2, parts_out, v_ps = (
            sem("qk_r1"), sem("qk_p1"), sem("qk_p2"), sem("parts_out"), sem("v_ps"))
        v_copied, lg_ps, lg_copied, gsplit, route = (
            sem("v_copied"), sem("lg_ps"), sem("lg_copied"), sem("gsplit"), sem("route"))
        expd, rstep, ones_rows, we_done, wet_ps = (
            sem("expd"), sem("rstep"), sem("ones_rows"), sem("we_done"), sem("wet_ps"))
        wet_copied, b2_ps, acc_init, b1_prep, slope_part = (
            sem("wet_copied"), sem("b2_ps"), sem("acc_init"), sem("b1_prep"), sem("slope_part"))
        scl, opa_rows, vs_ready, a_scored, a_reduced = (
            sem("scl"), sem("opa_rows"), sem("vs_ready"), sem("a_scored"), sem("a_reduced"))
        row_max, max_part, mt_ps, mt_copied, b_scored = (
            sem("row_max"), sem("max_part"), sem("mt_ps"), sem("mt_copied"), sem("b_scored"))
        b_exped, pv_done, u_ready, o_ps, o_rc = (
            sem("b_exped"), sem("pv_done"), sem("u_ready"), sem("o_ps"), sem("o_rc"))
        o_normed, up_ps, th_done, th1, glu_read = (
            sem("o_normed"), sem("up_ps"), sem("th_done"), sem("th1"), sem("glu_read"))
        y_ready, ye_ps, ye_added, carry, ot_ps = (
            sem("y_ready"), sem("ye_ps"), sem("ye_added"), sem("carry"), sem("ot_ps"))
        ot_copied, fin_ps, fin_th, fin_a, fin_b = (
            sem("ot_copied"), sem("fin_ps"), sem("fin_th"), sem("fin_a"), sem("fin_b"))
        fin_x, x1_in, out_st = (
            sem("fin_x"), sem("x1_in"), sem("out_st"))
        opa_in = [sem("opa_in0"), sem("opa_in1")]
        stage_in = [sem("stage_in0"), sem("stage_in1")]
        opb_in = [sem("opb_in0"), sem("opb_in1")]
        mrow = [sem(f"mrow{s}") for s in range(NC)]
        x_in = [sem(f"x_in{c}") for c in range(NC)]

        block = ctx.enter_context(nc.Block())

        def wait(eng, semaphore, count):
            if not (isinstance(count, int) and count <= 0):
                eng.wait_ge(semaphore, count)

        def slots_of_loop(run, eng):
            def fresh(value, least):
                return eng.snap(eng.to_reg(value), min_val=least, max_val=H // 2 - 2 + least)

            run(0, 0, 0)
            with eng.Fori(0, H // 2 - 1) as i:
                for u in range(2):
                    for s in range(NC):
                        if (u, s) != (0, 0):
                            run(fresh(i, 0), u, s)
                run(fresh(i + 1, 1), 0, 0)
            for u in range(2):
                for s in range(NC):
                    if (u, s) != (0, 0):
                        run(H // 2 - 1, u, s)

        def prev_of(i, u, s):
            if s:
                return i, u, s - 1
            if u:
                return i, 0, NC - 1
            if isinstance(i, int) and i == 0:
                return None
            return i - 1, 1, NC - 1

        def finds_maxima(i, u):
            return not (isinstance(i, int) and 2 * i + u == H - 1)

        @block.sync
        def _(sp):
            for c in range(NC):
                sp.dma_start(XO[:, TC * c:TC * c + TC, :],
                             x[0].rearrange("(t p) d -> p t d", p=P)[:, TC * c:TC * c + TC, :]).then_inc(x_in[c], 16)
                if c == 0:
                    sp.dma_start(STG[:, 0:1536], w_qkv0.rearrange("p k n -> p (k n)")).then_inc(w_in0, 16)
            sp.wait_ge(w0l, 1)
            sp.dma_start(STG[:, 0:1536], w_qkv1.rearrange("p k n -> p (k n)")).then_inc(w_q1_in, 16)
            sp.dma_start(W2[:, :, :, :], w2).then_inc(w2_in, 16)
            with sp.Fori(0, NC) as c:
                sp.wait_ge(x1_add, 2 * c + 2)
                sp.dma_start(x1_dram[:, ds(TC * c, TC), :], XO[:, ds(TC * c, TC), :]).then_inc(x1_spill, 16)
            with sp.Fori(0, NC) as c:
                for m in range(4):
                    side, half = m // 2, m % 2
                    sp.wait_ge(qk_p2, 4 * c + m + 1)
                    sp.dma_start(parts[side, :, half * P:half * P + P, ds(c * CH, CH)].rearrange("j f t -> f j t"),
                                 QP[:, m, :, :]).then_inc(parts_out, 16)

            def load_a(h, par):
                for side in range(2):
                    row = POS
                    for part in SPLITS[side]:
                        sp.dma_start(OPS[row:row + HD, par, side, :],
                                     parts[side, part, ds(HD * h, HD), :]).then_inc(opa_in[par], 16)
                        row += HD

            def copy_b(h, par, times):
                sp.wait_ge(opa_in[par], 16 * 12 * times)
                sp.wait_ge(ones_rows, 2)
                sp.wait_ge(opa_rows, 2 * h + 2)
                sp.dma_start(OPS[0:ROWS_A, 2 + par, :, :], OPS[0:ROWS_A, par, :, :]).then_inc(opb_in[par], 16)

            def rows_out(par, s, k):
                sp.wait_ge(mt_copied, k)
                a = A_ORDER[s]
                sp.dma_start(OPS[ROWS_A:ROWS_B, 2 + par, 0, CH * a:CH * a + CH].rearrange("j (q t) -> j q t", q=TC),
                             MT[:, s % 2, :]).then_inc(mrow[s], 16)

            sp.wait_ge(parts_out, 16 * 16)
            load_a(0, 0)
            load_a(1, 1)
            copy_b(0, 0, 1)
            for s in range(NC):
                rows_out(0, s, s + 1)

            def slot(i, u, s):
                h = 2 * i + u
                prev = prev_of(i, u, s)
                if prev and finds_maxima(*prev[:2]):
                    rows_out((prev[1] + 1) % 2, prev[2], NC + NC * (2 * prev[0] + prev[1]) + prev[2] + 1)
                if s == 1:
                    if not (isinstance(i, int) and h + 2 >= H):
                        load_a(h + 2, u)
                    if not (isinstance(i, int) and h + 1 >= H):
                        copy_b(h + 1, 1 - u, i + 1 + u)

            slots_of_loop(slot, sp)
            sp.wait_ge(a_scored, PER_HEAD * H)
            sp.wait_ge(x1_spill, 16 * NC)
            sp.dma_start(ops32[:, 0:4096], x1_dram.rearrange("p t d -> p (t d)")).then_inc(x1_in, 16)
            with sp.Fori(0, NT // 2) as r:
                sp.wait_ge(fin_x, r + 1)
                sp.dma_start(out[0].rearrange("(t p) d -> p t d", p=P)[:, ds(2 * r, 2), :],
                             ops32[:, ds(CH * r, CH)].rearrange("p (t d) -> p t d", d=D)).then_inc(out_st, 16)
            sp.wait_ge(out_st, 16 * (NT // 2))

        @block.gpsimd
        def _(pool):
            pool.dma_start(MASK[:, :, :], masks).then_inc(cast_in, 16)
            pool.dma_start(POSR[:, :, :], pos_rows, max_dma_last_dim=4096).then_inc(cast_in, 16)
            pool.memset(ONES[:, :], 1.0).then_inc(memset_done, 1)
            pool.memset(HALF[:, :], -0.5).then_inc(memset_done, 1)
            pool.memset(ONE1[:, 0, :], 1.0).then_inc(memset_done, 1)
            pool.memset(ONE1[:, 1, :], WS).then_inc(memset_done, 1)
            pool.memset(ZERO[:, :], 0.0).then_inc(memset_done, 1)
            pool.memset(ONEB[:, :], 1.0).then_inc(memset_done, 1)
            pool.memset(NIL[:, :], 0.0).then_inc(memset_done, 1)
            pool.memset(CAR[:, :, :], 0.0).then_inc(memset_done, 1)
            pool.memset(VS[:, :, :, HD + 1:32], 0.0).then_inc(memset_done, 1)
            pool.memset(VS[:, :, :, HD:HD + 1], 1.0).then_inc(memset_done, 1)

            def rstd(k, tiles):
                pool.wait_ge(var_eps, k)
                pool.tensor_tensor(RSTD[:, tiles], VEPS[:, tiles], HALF[:, 0:TC], ALU.pow).then_inc(rstd_done, 1)

            pool.wait_ge(memset_done, 10)
            for c in range(NC):
                rstd(c + 1, slice(TC * c, TC * c + TC))

            def front(c):
                for m in range(2):
                    wait(pool, phi_q, 2 * c + m + 1)
                    wait(pool, scan_k, 2 * c + m + 1)
                    wait(pool, outT, 2 * c)
                    pool.tensor_tensor(DEN[:, m, :], PH[:, 2 + m, :], KC[:, m, :], ALU.mult).then_inc(nd, 1)
                    wait(pool, nd, 2 * c + m + 1)
                    pool.tensor_scalar(DEN[:, m, :], DEN[:, m, :], L0_EPS, None, ALU.add).then_inc(nd2, 1)
                    wait(pool, scan_kv, 2 * c + m + 1)
                    pool.tensor_tensor(NUM[:, m, :], PH[:, 2 + m, :], KVC[:, m, :], ALU.mult).then_inc(numden, 1)

            def back(c):
                for r in range(2):
                    wait(pool, gate_mid, 2 * c + r + 1)
                    xs = XO[:, ds(TC * c + 2 * r, 2), :].rearrange("p t d -> p (t d)")
                    pool.tensor_tensor(xs, xs, GT[:, r, :], ALU.add).then_inc(x1_add, 1)
                rstd(NC + c + 1, ds(TC * c, TC))

            front(0)
            for c in range(NC - 1):
                front(c + 1)
                back(c)
            back(NC - 1)

            def fetch(e, half):
                pool.dma_start(STG[:, 1024 * half:1024 * half + 1024], w1[:, ds(1024 * e, 1024)])\
                    .then_inc(stage_in[half], 16)

            def split(e, half, turn):
                st = STG[:, 1024 * half:1024 * half + 1024]
                pool.wait_ge(stage_in[half], 16 * turn + 16)
                pool.tensor_scalar(st, st, WS, 0.0, ALU.mult, ALU.add).then_inc(w1h_done, 1)
                pool.wait_ge(w1h_done, 2 * e + 1)
                pool.tensor_copy(W1H[:, ds(1024 * e, 1024)], st).then_inc(w1h_done, 1)
                pool.wait_ge(w1h_done, 2 * e + 2)
                pool.tensor_tensor(W1L[:, ds(1024 * e, 1024)], st, W1H[:, ds(1024 * e, 1024)],
                                   ALU.subtract).then_inc(w1l_done, 1)

            pool.wait_ge(wq1l, 2)
            for half in range(2):
                fetch(half, half)
            for q in range(E // 2 - 1):
                for half in range(2):
                    split(2 * q + half, half, q)
                    wait(pool, w1l_done, 2 * q + half + 1)
                    fetch(2 * q + 2 + half, half)
            for half in range(2):
                split(E - 2 + half, half, E // 2 - 1)

            def rows(h, par):
                for side in range(2):
                    pool.tensor_tensor(OPS[0:POS, par, side, :], POSR[:, side, :],
                                       SCL[:, side, ds(h, 1)].broadcast_to([POS, S]), ALU.mult).then_inc(opa_rows, 1)

            def values(h, par):
                pool.tensor_copy(VS[:, par, :, 0:HD], VV[:, :, ds(HD * h, HD)]).then_inc(vs_ready, 1)

            nought = NIL[:, 0:1].broadcast_to([P, TC])

            def maxima(par, k):
                pool.wait_ge(row_max, k)
                pool.tensor_tensor(NP[:, par, 0, :], NM[:, par, :], nought, ALU.add).then_inc(max_part, 1)
                pool.wait_ge(max_part, 5 * k - 4)
                pool.tensor_tensor(NR[:, par, 0, :], NM[:, par, :], NP[:, par, 0, :], ALU.subtract).then_inc(max_part, 1)
                pool.wait_ge(max_part, 5 * k - 3)
                pool.tensor_tensor(NP[:, par, 1, :], NR[:, par, 0, :], nought, ALU.add).then_inc(max_part, 1)
                pool.wait_ge(max_part, 5 * k - 2)
                pool.tensor_tensor(NR[:, par, 1, :], NR[:, par, 0, :], NP[:, par, 1, :], ALU.subtract).then_inc(max_part, 1)
                pool.wait_ge(max_part, 5 * k - 1)
                pool.tensor_tensor(NP[:, par, 2, :], NR[:, par, 1, :], nought, ALU.add).then_inc(max_part, 1)

            pool.wait_ge(scl, 8)
            pool.wait_ge(cast_in, 32)
            pool.wait_ge(parts_out, 16 * 16)
            pool.wait_ge(w1l_done, E)
            for par in range(2):
                pool.memset(OPS[96:P, 2 + par, 1, :], 1.0).then_inc(ones_rows, 1)
            pool.wait_ge(ones_rows, 2)
            rows(0, 0)
            rows(1, 1)
            pool.wait_ge(v_copied, 2 * NC)
            values(0, 0)
            for s in range(NC):
                maxima(s % 2, s + 1)

            def slot(i, u, s):
                h = 2 * i + u
                for unit, _, _, _, _, _, _, _, _ in UNITS[s]:
                    m = NC * h + unit
                    pool.wait_ge(th_done, m + 1)
                    pool.tensor_tensor(TH[:, unit % 2, :], TH[:, unit % 2, :], ONES[:, 0:1].broadcast_to([P, CH]), ALU.add)\
                        .then_inc(th1, 1)
                if s == 1:
                    if not (isinstance(i, int) and h + 2 >= H):
                        rows(h + 2, u)
                    if not (isinstance(i, int) and h + 1 >= H):
                        values(h + 1, 1 - u)
                if finds_maxima(i, u):
                    maxima(s % 2, NC * (h + 1) + s + 1)

            slots_of_loop(slot, pool)

            pool.wait_ge(x1_in, 16)
            for q in range(NT // 4):
                for r in range(2):
                    wait(pool, fin_b, 2 * q + r + 1)
                    xs = ops32[:, ds(2 * CH * q + CH * r, CH)]
                    pool.tensor_tensor(xs, xs, GT[:, r, :], ALU.add).then_inc(fin_x, 1)

        @block.scalar
        def _(act):
            act.dma_start(IDN[:, :], ident).then_inc(const_in, 16)
            act.dma_start(SEL[:, :], sel).then_inc(const_in, 16)
            act.dma_start(WF[:, :, :], w_ffn).then_inc(w_ffn_in, 16)
            act.dma_start(WO0[:, :, :], w_out0).then_inc(w_out_in, 16)
            act.dma_start(BROW[0:1, 0, :], b_ffn).then_inc(small_in, 16)
            act.dma_start(BROW[0:1, 1, :], b_v1).then_inc(small_in, 16)
            act.dma_start(BROW[0:1, 2, :], b_out1).then_inc(small_in, 16)
            act.dma_start(GBR[0:1, :], gate_b).then_inc(small_in, 16)
            act.dma_start(GW[:, :, :], gate_w).then_inc(small_in, 16)
            act.dma_start(BQK[:, :], b_qk1).then_inc(small_in, 16)
            act.dma_start(WO1[:, :, :], w_out1).then_inc(small_in, 16)
            act.dma_start(B2[:, :], b2).then_inc(small_in, 16)
            act.dma_start(B1[:, :, :, :], b1).then_inc(small_in, 16)
            act.dma_start(SLB[:, :], slopes.broadcast_to([POS, H])).then_inc(small_in, 16)
            act.dma_start(PICK[:, :, :], pick).then_inc(small_in, 16)
            act.wait_ge(w_in0, 16)
            act.activation(W0H[:, :, :].rearrange("p k n -> p (k n)"), STG[:, 0:1536], ACT.Copy, scale=WS).then_inc(w0h, 1)
            for k in range(KK):
                act.wait_ge(ffn_t, k + 1)
                act.activation(FH[:, k, :], PS[6 + k][:, 0:D], ACT.Copy).then_inc(ffn_h, 1)

            def high(c, k0):
                for k in range(KK):
                    wait(act, xt_ps, k0 + KK * c + k + 1)
                    act.activation(XTH[:, k, ds(CH * c, CH)], PS[k][:, :], ACT.Copy).then_inc(xth, 1)

            def front(c):
                high(c, 0)
                for n, (m, t) in enumerate(((0, 0), (1, 1), (2, 4), (3, 5))):
                    wait(act, proj, 6 * c + t + 1)
                    wait(act, phi_k if m < 2 else phi_q, 2 * c)
                    bank = PS[2 + t % 4]
                    act.activation(EX[:, m, :], bank[:, :], ACT.Exp, scale=1 / WS).then_inc(exps, 1)
                    act.activation(RE[:, m, :], bank[:, :], ACT.Relu, scale=1 / WS).then_inc(relus, 1)

            def back(c):
                for r in range(2):
                    wait(act, z_ps, 2 * c + r + 1)
                    act.activation(TH[:, r, :], PS[6][:, :], ACT.Tanh, scale=0.5).then_inc(gate_th, 1)

            front(0)
            for c in range(NC - 1):
                front(c + 1)
                back(c)
            back(NC - 1)

            act.wait_ge(w_q1_in, 16)
            act.wait_ge(s_ps, 2 * NC)
            act.wait_ge(numden, 2 * NC)
            act.activation(WQH[:, :, :].rearrange("p k n -> p (k n)"), STG[:, 0:1536], ACT.Copy, scale=WS).then_inc(wq1h, 1)
            act.activation(GWH[:, :, :], GW[:, :, :], ACT.Copy, scale=WS).then_inc(wq1h, 1)
            act.wait_ge(phi_q, 2 * NC)
            act.wait_ge(scan_kv, 2 * NC)
            act.wait_ge(numden, 2 * NC)
            for c in range(NC):
                high(c, KK * NC)
                for m in range(4):
                    side = m // 2
                    wait(act, qk_ps, 4 * c + m + 1)
                    wait(act, qk_p2, 4 * c)
                    wait(act, parts_out, 64 * c)
                    scale = 1 / WS if side else HD ** -0.5 / WS
                    act.activation(QV[:, m, :], PS[2 + m][:, :], ACT.Identity, scale=scale,
                                   bias=BQK[:, m:m + 1]).then_inc(qk_v, 1)
                    wait(act, qk_v, 4 * c + m + 1)
                    act.activation(QP[:, m, 0, :], QV[:, m, :], ACT.Copy).then_inc(qk_p0, 1)
                for m in range(4):
                    wait(act, qk_r1, 4 * c + m + 1)
                    act.activation(QP[:, m, 1, :], QR[:, m, :], ACT.Copy).then_inc(qk_p1, 1)
                for r in range(2):
                    wait(act, v_ps, 2 * c + r + 1)
                    act.activation(VV[:, ds(TC * c + 2 * r, 2), :].rearrange("p t d -> p (t d)"), PS[6 + r][:, :],
                                   ACT.Copy, scale=1 / WS).then_inc(v_copied, 1)
            act.wait_ge(route, 1)
            act.activation(TOP[:, 3, :], TOP[:, 2, :], ACT.Exp).then_inc(expd, 1)
            for c in range(NC):
                act.wait_ge(wet_ps, c + 1)
                act.activation(WET[:, CH * c:CH * c + CH], PS[4 + c % 2][0:E, :], ACT.Copy).then_inc(wet_copied, 1)
            for r in range(NT // 2):
                act.wait_ge(b2_ps, r + 1)
                act.activation(ACC[:, 2 * r:2 * r + 2, :].rearrange("p t d -> p (t d)"), PS[4 + r % 2][:, :],
                               ACT.Copy).then_inc(acc_init, 1)

            def max_rows(par, k, dma):
                act.wait_ge(mt_ps, k)
                if dma is not None:
                    act.wait_ge(*dma)
                act.activation(MT[:, par, :], MTP, ACT.Copy).then_inc(mt_copied, 1)

            for s in range(NC):
                max_rows(s % 2, s + 1, (mrow[s - 2], 16) if s >= 2 else None)

            def slot(i, u, s):
                h = 2 * i + u
                n = NC * h + s
                prev = prev_of(i, u, s)
                for t in range(STEPS):
                    for k in share(N_B[s], t, STEPS - 2):
                        idx = PER_HEAD * h + OFF_B[s] + k
                        j = k
                        off = P * max(0, j - TC * B_ORDER[s])
                        act.wait_ge(b_scored, idx + 1)
                        if k >= RING:
                            act.wait_ge(pv_done, idx + 1 - RING)
                        act.activation(PR[:, (OFF_B[s] + k) % RING, off:CH], PS[2 + (OFF_B[s] + k) % 2][:, off:CH],
                                       ACT.Exp).then_inc(b_exped, 1)
                    for unit, f, _, _, _, _, t_tanh, _, _ in UNITS[s]:
                        if t == t_tanh:
                            m = NC * h + unit
                            act.wait_ge(up_ps, 2 * m + 1)
                            if not (isinstance(m, int) and m < 2):
                                act.wait_ge(glu_read, m - 1)
                            act.activation(TH[:, unit % 2, :], PS[5][:, :], ACT.Tanh, scale=0.851 / WS,
                                           bias=B1T[:, ds(i, 1), f:f + 1].rearrange("p a b -> p (a b)"))\
                                .then_inc(th_done, 1)
                    if t == T_MAXC and prev and finds_maxima(*prev[:2]):
                        ph, q = 2 * prev[0] + prev[1], prev[2]
                        sent = (mrow[q - 2], 16 * (ph + 2)) if q >= 2 else (mrow[q + 2], 16 * (ph + 1))
                        max_rows(q % 2, NC * (ph + 1) + q + 1, sent)
                act.wait_ge(pv_done, PER_HEAD * h + OFF_B[s] + N_B[s])
                act.activation(U[:, s % 2, :], PS[4][:, :], ACT.Copy).then_inc(u_ready, 1)

            slots_of_loop(slot, act)
            for q in range(NT // 4):
                for r in range(2):
                    if r == 0:
                        act.wait_ge(ye_added, NC * H)
                    wait(act, fin_a, 2 * q)
                    act.activation(TH[:, r, :], ACC[:, ds(4 * q + 2 * r, 2), :].rearrange("p t d -> p (t d)"), ACT.Tanh,
                                   scale=0.5).then_inc(fin_th, 1)
                    wait(act, ot_ps, 2 * q + r + 1)
                    wait(act, fin_ps, 2 * q)
                    act.activation(TQ[:, r, :], PS[r][:, :], ACT.Copy).then_inc(ot_copied, 1)

        @block.vector
        def _(dve):
            def norm_stats(c, k0):
                for t in range(TC):
                    dve.bn_stats(BST[:, t, :], XO[:, ds(TC * c + t, 1), :].rearrange("p a d -> p (a d)"))\
                        .then_inc(stats, 1)
                for t in range(TC):
                    dve.wait_ge(stats, 2 * TC * (k0 + c) + TC)
                    dve.bn_aggr(MV[:, ds(TC * c + t, 1), :].rearrange("p a d -> p (a d)"), BST[:, t, :]).then_inc(stats, 1)
                dve.wait_ge(stats, 2 * TC * (k0 + c) + 2 * TC)
                dve.tensor_scalar(VEPS[:, ds(TC * c, TC)], MV[:, ds(TC * c, TC), 1:2].rearrange("p a d -> p (a d)"),
                                  LN_EPS, None, ALU.add).then_inc(var_eps, 1)

            def norm_apply(c, k0):
                dve.wait_ge(rstd_done, k0 + c + 1)
                if not (isinstance(c, int) and k0 + c == 0):
                    dve.wait_ge(xt_ps, KK * (k0 + c))
                for t in range(TC):
                    dve.tensor_scalar(XN[:, t, :],
                                      XO[:, ds(TC * c + t, 1), :].rearrange("p a d -> p (a d)"),
                                      MV[:, ds(TC * c + t, 1), 0:1].rearrange("p a d -> p (a d)"),
                                      RSTD[:, ds(TC * c + t, 1)], ALU.subtract, ALU.mult).then_inc(xn, 1)

            def low(c, k0):
                for k in range(KK):
                    wait(dve, xth, k0 + KK * c + k + 1)
                    dve.tensor_tensor(XTL[:, k, ds(CH * c, CH)], PS[k][:, :], XTH[:, k, ds(CH * c, CH)],
                                      ALU.subtract).then_inc(xtl, 1)

            for c in range(NC):
                dve.wait_ge(x_in[c], 16)
                norm_stats(c, 0)
                if c == 0:
                    norm_apply(0, 0)
                    dve.wait_ge(w0h, 1)
                    dve.scalar_tensor_tensor(W0L[:, :, :].rearrange("p k n -> p (k n)"), STG[:, 0:1536], WS,
                                             W0H[:, :, :].rearrange("p k n -> p (k n)"),
                                             ALU.mult, ALU.subtract).then_inc(w0l, 1)
                    dve.wait_ge(w_ffn_in, 16)
                    dve.tensor_reduce(TOP[:, 0, 0:KK], WF[:, :, :], AX.X, ALU.add, apply_absolute_value=True)\
                        .then_inc(ffn_thr, 1)
                    dve.wait_ge(ffn_thr, 1)
                    dve.tensor_scalar(TOP[:, 1, 0:KK], TOP[:, 0, 0:KK], 1.0 / D, 0.7, ALU.mult, ALU.mult)\
                        .then_inc(ffn_thr, 1)
                    dve.wait_ge(ffn_thr, 2)
                    dve.tensor_scalar(TOP[:, 2, 0:KK], TOP[:, 1, 0:KK], -1.0, None, ALU.mult).then_inc(ffn_thr, 1)
                    dve.wait_ge(ffn_thr, 3)
                    for k in range(KK):
                        dve.tensor_scalar(NF[:, k, :], WF[:, k, :], TOP[:, 2, k:k + 1], None, ALU.is_lt).then_inc(ffn_q, 1)
                    dve.wait_ge(ffn_q, 2)
                    for k in range(KK):
                        dve.scalar_tensor_tensor(QF[:, k, :], WF[:, k, :], TOP[:, 1, k:k + 1], NF[:, k, :],
                                                 ALU.is_gt, ALU.subtract).then_inc(ffn_q, 1)
                    dve.wait_ge(ffn_q, 4)
                    dve.tensor_tensor(QF[:, :, :], QF[:, :, :], WF[:, :, :], ALU.subtract).then_inc(ffn_q, 1)
                    dve.wait_ge(ffn_q, 5)
                    dve.tensor_tensor(QF[:, :, :], WF[:, :, :], QF[:, :, :], ALU.add).then_inc(ffn_q, 1)
                    for k in range(KK):
                        dve.wait_ge(ffn_h, k + 1)
                        dve.tensor_tensor(FL[:, k, :], PS[6 + k][:, 0:D], FH[:, k, :], ALU.subtract).then_inc(ffn_split, 1)

            dve.wait_ge(memset_done, 10)

            def front(c, more):
                low(c, 0)
                if more:
                    norm_apply(c + 1, 0)
                for m in range(2):
                    wait(dve, relus, 4 * c + m + 1)
                    wait(dve, nd2, 2 * c)
                    dve.scalar_tensor_tensor(PH[:, m, :], EX[:, m, :], 1.0, RE[:, m, :], ALU.min, ALU.add)\
                        .then_inc(phi_k, 1)
                    wait(dve, phi_k, 2 * c + m + 1)
                    wait(dve, carry, 4 * c)
                    dve.tensor_tensor_scan(KC[:, m, :], ONES[:, 0:1].broadcast_to([P, CH]), PH[:, m, :], CAR[:, m, :], ALU.mult, ALU.add)\
                        .then_inc(scan_k, 1)
                for m in range(2):
                    wait(dve, proj, 6 * c + 3 + m)
                    dve.scalar_tensor_tensor(KV[:, m, :], PS[4 + m][:, :], 1 / WS, PH[:, m, :], ALU.mult, ALU.mult)\
                        .then_inc(v_read, 1)
                    wait(dve, v_read, 2 * c + m + 1)
                    wait(dve, numden, 2 * c)
                    dve.tensor_tensor_scan(KVC[:, m, :], ONES[:, 0:1].broadcast_to([P, CH]), KV[:, m, :], CAR[:, 2 + m, :], ALU.mult, ALU.add)\
                        .then_inc(scan_kv, 1)
                for m in range(2):
                    wait(dve, relus, 4 * c + m + 3)
                    dve.scalar_tensor_tensor(PH[:, 2 + m, :], EX[:, 2 + m, :], 1.0, RE[:, 2 + m, :], ALU.min, ALU.add)\
                        .then_inc(phi_q, 1)
                for m in range(2):
                    wait(dve, scan_k, 2 * c + m + 1)
                    dve.tensor_copy(CAR[:, m, :], KC[:, m, CH - 1:CH]).then_inc(carry, 1)
                    wait(dve, scan_kv, 2 * c + m + 1)
                    dve.tensor_copy(CAR[:, 2 + m, :], KVC[:, m, CH - 1:CH]).then_inc(carry, 1)

            def back(c):
                for m in range(2):
                    wait(dve, nd2, 2 * c + m + 1)
                    dve.reciprocal(DEN[:, m, :], DEN[:, m, :]).then_inc(rcp, 1)
                    wait(dve, rcp, 2 * c + m + 1)
                    wait(dve, numden, 2 * c + m + 1)
                    wait(dve, s_ps, 2 * c)
                    dve.tensor_tensor(OT0[:, m, :], NUM[:, m, :], DEN[:, m, :], ALU.mult).then_inc(outT, 1)
                for r in range(2):
                    wait(dve, gate_th, 2 * c + r + 1)
                    wait(dve, x1_add, 2 * c)
                    dve.scalar_tensor_tensor(GT[:, r, :], TH[:, r, :], 1.0, PS[6][:, :], ALU.add, ALU.mult)\
                        .then_inc(gate_a, 1)
                    wait(dve, gate_a, 2 * c + r + 1)
                    wait(dve, s_ps, 2 * c + r + 1)
                    dve.scalar_tensor_tensor(GT[:, r, :], PS[7][:, :], 0.5 * HD ** -0.5, GT[:, r, :], ALU.mult, ALU.mult)\
                        .then_inc(gate_mid, 1)
                wait(dve, x1_add, 2 * c + 2)
                norm_stats(c, NC)

            front(0, True)
            for c in range(NC - 2):
                front(c + 1, True)
                back(c)
            front(NC - 1, False)
            back(NC - 2)
            back(NC - 1)
            norm_apply(0, NC)

            dve.wait_ge(wq1h, 2)
            dve.scalar_tensor_tensor(WQL[:, :, :].rearrange("p k n -> p (k n)"), STG[:, 0:1536], WS,
                                     WQH[:, :, :].rearrange("p k n -> p (k n)"), ALU.mult, ALU.subtract).then_inc(wq1l, 1)
            dve.wait_ge(small_in, 16 * 11)
            dve.scalar_tensor_tensor(GWL[:, :, :], GW[:, :, :], WS, GWH[:, :, :], ALU.mult, ALU.subtract).then_inc(wq1l, 1)
            dve.tensor_scalar(BQK[:, 0:2], BQK[:, 0:2], HD ** -0.5, None, ALU.mult).then_inc(gsplit, 1)
            dve.tensor_copy(SLP[:, 0, :], SLB[:, :]).then_inc(slope_part, 1)
            dve.wait_ge(slope_part, 1)
            dve.tensor_tensor(SLR[:, :], SLB[:, :], SLP[:, 0, :], ALU.subtract).then_inc(slope_part, 1)
            dve.wait_ge(slope_part, 2)
            dve.tensor_copy(SLP[:, 1, :], SLR[:, :]).then_inc(slope_part, 1)
            dve.wait_ge(slope_part, 3)
            dve.tensor_tensor(SLR[:, :], SLR[:, :], SLP[:, 1, :], ALU.subtract).then_inc(slope_part, 1)
            dve.wait_ge(slope_part, 4)
            dve.tensor_copy(SLP[:, 2, :], SLR[:, :]).then_inc(slope_part, 1)
            dve.wait_ge(slope_part, 5)
            for side in range(2):
                dve.tensor_scalar(SCL[:, side, :], SLP[:, 0, :], PICK[:, side, 0:1], PICK[:, side, 3:4],
                                  ALU.mult, ALU.add).then_inc(scl, 1)
            for j in (1, 2):
                for side in range(2):
                    dve.wait_ge(scl, 2 * j)
                    dve.scalar_tensor_tensor(SCL[:, side, :], SLP[:, j, :], PICK[:, side, j:j + 1], SCL[:, side, :],
                                             ALU.mult, ALU.add).then_inc(scl, 1)
            dve.tensor_scalar(B1S[:, :, 0, :], B1[:, :, 0, :], WS, None, ALU.mult).then_inc(scl, 1)
            dve.tensor_scalar(B1T[:, :, :], B1[:, :, 0, :], 0.851, None, ALU.mult).then_inc(scl, 1)
            dve.tensor_scalar(B1S[:, :, 1, :], B1[:, :, 1, :], 1.0, WS, ALU.add, ALU.mult).then_inc(b1_prep, 1)

            def project(c, more):
                low(c, KK * NC)
                if more:
                    norm_apply(c + 1, NC)
                for m in range(4):
                    wait(dve, qk_p0, 4 * c + m + 1)
                    dve.tensor_tensor(QR[:, m, :], QV[:, m, :], QP[:, m, 0, :], ALU.subtract).then_inc(qk_r1, 1)
                for m in range(4):
                    wait(dve, qk_p1, 4 * c + m + 1)
                    dve.tensor_tensor(QP[:, m, 2, :], QR[:, m, :], QP[:, m, 1, :], ALU.subtract).then_inc(qk_p2, 1)
                dve.wait_ge(lg_ps, c + 1)
                dve.tensor_scalar(LG[:, ds(TC * c, TC), :].rearrange("p t e -> p (t e)"), PS[0][:, 0:TC * E], 1 / WS, None,
                                  ALU.mult).then_inc(lg_copied, 1)

            for c in range(NC - 1):
                project(c, True)
            project(NC - 1, False)

            def step(ins):
                ins.then_inc(rstep, 1)
                dve.wait_ge(rstep, step.n)
                step.n += 1
            step.n = 1
            dve.wait_ge(lg_copied, NC)
            RANK, TMP, FIRST, SECOND = RT[:, 0], RT[:, 1], RT[:, 2], RT[:, 3]
            step(dve.memset(RANK, 0.0))
            for e in range(E):
                rival = LG[:, :, e:e + 1].broadcast_to([P, NT, E])
                if e:
                    step(dve.tensor_tensor(TMP[:, :, 0:e], rival[:, :, 0:e], LG[:, :, 0:e], ALU.is_gt))
                if e < E - 1:
                    step(dve.tensor_tensor(TMP[:, :, e + 1:E], rival[:, :, e + 1:E], LG[:, :, e + 1:E], ALU.is_ge))
                if e:
                    step(dve.tensor_tensor(RANK[:, :, 0:e], RANK[:, :, 0:e], TMP[:, :, 0:e], ALU.add))
                if e < E - 1:
                    step(dve.tensor_tensor(RANK[:, :, e + 1:E], RANK[:, :, e + 1:E], TMP[:, :, e + 1:E], ALU.add))
            step(dve.tensor_scalar(FIRST, RANK, 0.0, None, ALU.is_equal))
            step(dve.tensor_scalar(SECOND, RANK, 1.0, None, ALU.is_equal))
            step(dve.tensor_tensor(TMP, FIRST, LG[:, :, :], ALU.mult))
            step(dve.tensor_reduce(TOP[:, 0, :], TMP, AX.X, ALU.add))
            step(dve.tensor_tensor(TMP, SECOND, LG[:, :, :], ALU.mult))
            step(dve.tensor_reduce(TOP[:, 1, :], TMP, AX.X, ALU.add))
            dve.tensor_tensor(TOP[:, 2, :], TOP[:, 1, :], TOP[:, 0, :], ALU.subtract).then_inc(route, 1)
            dve.wait_ge(expd, 1)
            step(dve.tensor_scalar(TOP[:, 0, :], TOP[:, 3, :], 1.0, None, ALU.add))
            step(dve.reciprocal(TOP[:, 1, :], TOP[:, 0, :]))
            step(dve.tensor_tensor(TOP[:, 2, :], TOP[:, 3, :], TOP[:, 1, :], ALU.mult))
            step(dve.tensor_tensor(FIRST, FIRST, TOP[:, 1, :].unsqueeze(2).broadcast_to([P, NT, E]), ALU.mult))
            step(dve.tensor_tensor(SECOND, SECOND, TOP[:, 2, :].unsqueeze(2).broadcast_to([P, NT, E]), ALU.mult))
            step(dve.tensor_tensor(WE[:, :, :], FIRST, SECOND, ALU.add))
            dve.tensor_scalar(WES[:, :, :], WE[:, :, :], 0.5 / WS ** 2, None, ALU.mult).then_inc(we_done, 1)

            def reduce_a(h40, s, k):
                a = A_ORDER[s]
                xq, gg = k // (a + 1), k % (a + 1)
                width = CH if gg < a else P * (xq + 1)
                dve.wait_ge(a_scored, h40 + OFF_A[s] + k + 1)
                dve.tensor_reduce(PM[:, s % 2, xq, gg:gg + 1], PS[(OFF_A[s] + k) % 2][:, 0:width], AX.X, ALU.max)\
                    .then_inc(a_reduced, 1)

            def row_maxima(h40, s, k):
                a = A_ORDER[s]
                dve.wait_ge(a_reduced, h40 + OFF_A[s] + N_A[s])
                if not (isinstance(k, int) and k <= 2):
                    dve.wait_ge(mt_ps, k - 2)
                dve.tensor_reduce(NM[:, s % 2, :], PM[:, s % 2, :, 0:a + 1], AX.X, ALU.max, negate=True)\
                    .then_inc(row_max, 1)

            for s in range(NC):
                for k in range(N_A[s]):
                    reduce_a(0, s, k)
                row_maxima(0, s, s + 1)

            def heads_out(i, u, s, t):
                n = NC * (2 * i + u) + s
                o = PS[7][:, 0:TC * (HD + 1)].rearrange("p (q c) -> p q c", q=TC)
                if t == T_RCP:
                    dve.wait_ge(o_ps, n + 1)
                    dve.reciprocal(RC[:, s % 2, :], o[:, :, HD:HD + 1].rearrange("p q c -> p (q c)")).then_inc(o_rc, 1)
                else:
                    b = B_ORDER[s]
                    dve.wait_ge(o_rc, n + 1)
                    dve.tensor_tensor(XO[:, TC * b:TC * b + TC, ds(HD * (2 * i + u), HD)], o[:, :, 0:HD],
                                      RC[:, s % 2, :].unsqueeze(2).broadcast_to([P, TC, HD]), ALU.mult)\
                        .then_inc(o_normed, 1)

            def slot(i, u, s):
                h = 2 * i + u
                prev = prev_of(i, u, s)
                for t in range(STEPS):
                    if finds_maxima(i, u):
                        for k in share(N_A[s], t, STEPS):
                            reduce_a(PER_HEAD * (h + 1), s, k)
                    for unit, f, buf, _, _, _, _, t_gate, t_out in UNITS[s]:
                        m = NC * h + unit
                        if t == t_gate:
                            dve.wait_ge(th1, m + 1)
                            dve.scalar_tensor_tensor(GT[:, unit % 2, :], PS[5][:, :],
                                                     B1S[:, ds(i, 1), 0, f:f + 1].rearrange("p a b -> p (a b)"),
                                                     TH[:, unit % 2, :], ALU.add, ALU.mult).then_inc(glu_read, 1)
                        if t == t_out:
                            dve.wait_ge(up_ps, 2 * m + 2)
                            dve.wait_ge(glu_read, m + 1)
                            dve.scalar_tensor_tensor(YT[:, buf, f, :], PS[6][:, :],
                                                     B1S[:, ds(i, 1), 1, f:f + 1].rearrange("p a b -> p (a b)"),
                                                     GT[:, unit % 2, :], ALU.add, ALU.mult).then_inc(y_ready, 1)
                    for fill, buf, pair, _, t_add in FILLS[s]:
                        if t == t_add:
                            dve.wait_ge(ye_ps, NC * h + fill + 1)
                            for q in range(2):
                                tile = TC * (2 * u + buf) + 2 * pair + q
                                add = dve.scalar_tensor_tensor(
                                    ACC[:, tile, :], PS[7][:, D * q:D * q + D], WES[:, tile, ds(i, 1)],
                                    ACC[:, tile, :], ALU.mult, ALU.add)
                            add.then_inc(ye_added, 1)
                    if t in (T_RCP, T_NORM) and prev:
                        heads_out(*prev, t)
                if finds_maxima(i, u):
                    row_maxima(PER_HEAD * (h + 1), s, NC * (h + 1) + s + 1)

            dve.wait_ge(x1_spill, 16 * NC)
            dve.wait_ge(acc_init, NT // 2)
            slots_of_loop(slot, dve)
            for t in (T_RCP, T_NORM):
                heads_out(H // 2 - 1, 1, NC - 1, t)
            dve.wait_ge(ye_added, NC * H)
            for q in range(NT // 4):
                for r in range(2):
                    wait(dve, fin_th, 2 * q + r + 1)
                    wait(dve, fin_x, 2 * q)
                    dve.scalar_tensor_tensor(GT[:, r, :], TH[:, r, :], 1.0,
                                             ACC[:, ds(4 * q + 2 * r, 2), :].rearrange("p t d -> p (t d)"),
                                             ALU.add, ALU.mult).then_inc(fin_a, 1)
                    wait(dve, fin_a, 2 * q + r + 1)
                    wait(dve, fin_ps, 2 * q + r + 1)
                    dve.scalar_tensor_tensor(GT[:, r, :], PS[2 + r][:, :], 0.5, GT[:, r, :], ALU.mult, ALU.mult)\
                        .then_inc(fin_b, 1)

        @block.tensor
        def _(pe):
            mm = pe.matmul

            def transposes(c, k0):
                pe.wait_ge(xn, TC * (k0 + c) + TC)
                for k in range(KK):
                    for t in range(TC):
                        last = pe.transpose(PS[k][:, P * t:P * t + P],
                                            XN[:, t, P * k:P * k + P],
                                            IDN[:, :])
                    last.then_inc(xt_ps, 1)

            def pairs(out, weight, data, weight_first, last=True, first=True):
                for k in range(KK):
                    for j, (wp, dp) in enumerate(((0, 0), (1, 0), (0, 1))):
                        w, d = weight[wp](k), data[dp](k)
                        done = mm(out, w if weight_first else d, d if weight_first else w,
                                  start=first and k == 0 and j == 0, stop=last and k == KK - 1 and j == 2)
                return done

            def x_cols(c):
                return [lambda k: XTH[:, k, ds(CH * c, CH)], lambda k: XTL[:, k, ds(CH * c, CH)]]

            def x_tile(c, t):
                return [lambda k: XTH[:, k, ds(CH * c + P * t, P)], lambda k: XTL[:, k, ds(CH * c + P * t, P)]]

            pe.wait_ge(const_in, 32)
            pe.wait_ge(ffn_q, 6)
            for k in range(KK):
                for o in range(KK):
                    last = pe.transpose(PS[6 + k][:, P * o:P * o + P], QF[:, o, P * k:P * k + P], IDN[:, :])
                last.then_inc(ffn_t, 1)

            def front(c):
                transposes(c, 0)
                wait(pe, xth, KK * c + KK)
                wait(pe, xtl, KK * c + KK)
                for t, m in enumerate((2, 3, 4, 5, 0, 1)):
                    if t < 2:
                        wait(pe, relus, 4 * c)
                    elif t < 4:
                        wait(pe, v_read, 2 * c)
                    else:
                        wait(pe, relus, 4 * c + t - 3)
                    cols = slice(P * m, P * m + P)
                    pairs(PS[2 + t % 4][:, :], [lambda k: W0H[:, k, cols], lambda k: W0L[:, k, cols]],
                          x_cols(c), True).then_inc(proj, 1)

            def back(c):
                for r in range(2):
                    wait(pe, gate_a, 2 * c + r)
                    for q in range(2):
                        mm(PS[6][:, D * q:D * q + D], ONE1[0:1, 0, :], BROW[0:1, 0, :], start=True, stop=False)
                        last = pairs(PS[6][:, D * q:D * q + D], [lambda k: FH[:, k, :], lambda k: FL[:, k, :]],
                                     x_tile(c, 2 * r + q), False, first=False)
                    last.then_inc(z_ps, 1)
                    wait(pe, gate_mid, 2 * c + r)
                    wait(pe, outT, 2 * c + 2)
                    for q in range(2):
                        for k in range(KK):
                            last = mm(PS[7][:, D * q:D * q + D], OT0[:, k, P * (2 * r + q):P * (2 * r + q) + P],
                                      WO0[:, k, :], start=k == 0, stop=k == KK - 1)
                    last.then_inc(s_ps, 1)

            pe.wait_ge(w0l, 1)
            front(0)
            pe.wait_ge(small_in, 16 * 11)
            pe.wait_ge(ffn_split, 2)
            pe.wait_ge(w_out_in, 16)
            pe.wait_ge(memset_done, 10)
            for c in range(NC - 1):
                front(c + 1)
                back(c)
            back(NC - 1)

            pe.wait_ge(wq1l, 2)
            pe.wait_ge(gate_mid, 2 * NC)
            pe.wait_ge(relus, 4 * NC)
            for c in range(NC):
                wait(pe, lg_copied, c)
                transposes(c, NC)
                pe.wait_ge(xth, KK * (NC + c) + KK)
                pe.wait_ge(xtl, KK * (NC + c) + KK)
                for m in range(4):
                    wait(pe, qk_v, 4 * c)
                    cols = slice(P * m, P * m + P)
                    pairs(PS[2 + m][:, :], [lambda k: WQH[:, k, cols], lambda k: WQL[:, k, cols]],
                          x_cols(c), True).then_inc(qk_ps, 1)
                for t in range(TC):
                    last = mm(PS[0][:, E * t:E * t + E], ONE1[0:1, 1, :], GBR[0:1, :], start=True, stop=False)
                    last = pairs(PS[0][:, E * t:E * t + E], [lambda k: GWH[:, k, :], lambda k: GWL[:, k, :]],
                                 x_tile(c, t), False, first=False)
                last.then_inc(lg_ps, 1)
                cols = slice(2 * D, 3 * D)
                for r in range(2):
                    wait(pe, v_copied, 2 * c)
                    for q in range(2):
                        mm(PS[6 + r][:, D * q:D * q + D], ONE1[0:1, 1, :], BROW[0:1, 1, :], start=True, stop=False)
                        last = pairs(PS[6 + r][:, D * q:D * q + D], [lambda k: WQH[:, k, cols], lambda k: WQL[:, k, cols]],
                                     x_tile(c, 2 * r + q), False, first=False)
                    last.then_inc(v_ps, 1)

            pe.wait_ge(we_done, 1)
            for c in range(NC):
                if c >= 2:
                    pe.wait_ge(wet_copied, c - 1)
                for t in range(TC):
                    last = pe.transpose(PS[4 + c % 2][0:E, P * t:P * t + P], WE[:, TC * c + t, :], IDN[:, :])
                last.then_inc(wet_ps, 1)
            pe.wait_ge(wet_copied, NC)
            for r in range(NT // 2):
                if r >= 2:
                    pe.wait_ge(acc_init, r - 1)
                for q in range(2):
                    tile = 2 * r + q
                    last = mm(PS[4 + r % 2][:, D * q:D * q + D], WET[:, P * tile:P * tile + P], B2[:, :],
                              start=True, stop=True)
                last.then_inc(b2_ps, 1)

            def score_a(h40, par, s, k):
                a = A_ORDER[s]
                xq, gg = k // (a + 1), k % (a + 1)
                width = CH if gg < a else P * (xq + 1)
                idx = h40 + OFF_A[s] + k
                if not (isinstance(idx, int) and idx < 2):
                    pe.wait_ge(a_reduced, idx - 1)
                bank = PS[(OFF_A[s] + k) % 2]
                last = mm(bank[:, 0:width], OPS[0:ROWS_A, par, 0, P * (TC * a + xq):P * (TC * a + xq) + P],
                          OPS[0:ROWS_A, par, 1, CH * gg:CH * gg + width], start=True, stop=gg < a)
                if gg == a:
                    last = mm(bank[:, P * xq:P * xq + P], MASK[:, 0, :], MASK[:, 2, :], start=False, stop=True)
                last.then_inc(a_scored, 1)

            def turn_maxima(par, k):
                pe.wait_ge(max_part, 5 * k)
                pe.transpose(MTP, NP[:, par, :, :].rearrange("p j q -> p (j q)"), MASK[:, 2, :]).then_inc(mt_ps, 1)

            pe.wait_ge(cast_in, 32)
            pe.wait_ge(opa_in[0], 16 * 12)
            pe.wait_ge(opa_rows, 2)
            for s in range(NC):
                for k in range(N_A[s]):
                    score_a(0, 0, s, k)
                if s:
                    if s >= 2:
                        pe.wait_ge(mt_copied, s - 1)
                    turn_maxima((s - 1) % 2, s)
            pe.wait_ge(mt_copied, NC - 1)
            turn_maxima((NC - 1) % 2, NC)

            def score_b(h, u, s, k):
                b = B_ORDER[s]
                off = P * max(0, k - TC * b)
                idx = PER_HEAD * h + OFF_B[s] + k
                if not (isinstance(idx, int) and idx < 2):
                    pe.wait_ge(b_exped, idx - 1)
                if k == 0:
                    pe.wait_ge(mrow[A_ORDER.index(b)], 16 * h + 16)
                bank = PS[2 + (OFF_B[s] + k) % 2]
                last = mm(bank[:, off:CH], OPS[0:ROWS_B, 2 + u, 1, P * k:P * k + P],
                          OPS[0:ROWS_B, 2 + u, 0, CH * b + off:CH * b + CH], start=True, stop=k < TC * b)
                if k >= TC * b:
                    last = mm(bank[:, off:off + P], MASK[:, 1, :], MASK[:, 2, :], start=False, stop=True)
                last.then_inc(b_scored, 1)

            def value(h, u, s, k):
                b = B_ORDER[s]
                off = P * max(0, k - TC * b)
                idx = PER_HEAD * h + OFF_B[s] + k
                if k == 0:
                    if not (isinstance(idx, int) and idx == 0):
                        pe.wait_ge(u_ready, NC * h + s)
                    if b == 0:
                        mm(PS[4][:, :], ZERO[:, :], ONEB[:, :], start=True, stop=True, skip_group_check=True)
                pe.wait_ge(b_exped, idx + 1)
                quad = 32 * (k % TC)
                mm(PS[4][quad:quad + 32, off:CH], VS[:, u, k, :], PR[:, (OFF_B[s] + k) % RING, off:CH],
                   start=b > 0 and k < TC, stop=k >= TC * b, skip_group_check=True, tile_position=(0, quad))\
                    .then_inc(pv_done, 1)

            def heads_out(s):
                for q in range(TC):
                    last = mm(PS[7][:, (HD + 1) * q:(HD + 1) * q + HD + 1], U[:, s % 2, P * q:P * q + P], SEL[:, :],
                              start=True, stop=True)
                last.then_inc(o_ps, 1)

            def slot(i, u, s):
                h = 2 * i + u
                prev = prev_of(i, u, s)
                if s == 0:
                    if finds_maxima(i, u):
                        pe.wait_ge(opa_in[1 - u], 16 * 12 * (i + 1 + u))
                        pe.wait_ge(opa_rows, 2 * h + 4)
                    pe.wait_ge(opb_in[u], 16 * (i + 1))
                    pe.wait_ge(vs_ready, h + 1)
                    pe.wait_ge(w1l_done, i + 1)
                for t in range(STEPS):
                    aa = share(N_A[s], t, STEPS) if finds_maxima(i, u) else range(0)
                    bb = share(N_B[s], t, STEPS - 2)
                    for n in range(max(len(aa), len(bb))):
                        if n < len(aa):
                            score_a(PER_HEAD * (h + 1), 1 - u, s, aa[n])
                        if n < len(bb):
                            score_b(h, u, s, bb[n])
                            if bb[n] >= LAG:
                                value(h, u, s, bb[n] - LAG)
                    if t == STEPS - 2:
                        for k in range(N_B[s] - LAG, N_B[s] - 1):
                            value(h, u, s, k)
                    if t == STEPS - 1:
                        value(h, u, s, N_B[s] - 1)
                    if t == T_HEADS and prev:
                        n = NC * h + s
                        pe.wait_ge(u_ready, n)
                        if FILLS[prev[2]]:
                            pe.wait_ge(ye_added, NC * (2 * prev[0] + prev[1]) + FILLS[prev[2]][-1][0] + 1)
                        heads_out(prev[2])
                    if t == T_MAXT and prev and finds_maxima(*prev[:2]):
                        pe.wait_ge(o_normed, NC * h + s)
                        turn_maxima(prev[2] % 2, NC * (2 * prev[0] + prev[1] + 1) + prev[2] + 1)
                    for unit, f, _, t_g, t_l, rate, _, _, _ in UNITS[s]:
                        m = NC * h + unit
                        for part, start in ((0, t_g), (1, t_l)):
                            for j in range(max(0, rate * (t - start)), max(0, min(6, rate * (t - start + 1)))):
                                if j == 0 and not (isinstance(m, int) and m == 0):
                                    pe.wait_ge(y_ready if part else glu_read, m)
                                k, (wp, dp) = j // 3, ((0, 0), (1, 0), (0, 1))[j % 3]
                                col = ((part * 2 + f) * KK + k) * P
                                last = mm(PS[5 + part][:, :], (W1L if wp else W1H)[:, ds(1024 * i + col, P)],
                                          (XTL if dp else XTH)[:, k, CH * (2 * u + unit // 2):CH * (2 * u + unit // 2) + CH],
                                          start=j == 0, stop=j == 5)
                                if j == 5:
                                    last.then_inc(up_ps, 1)
                    for fill, buf, pair, t_f, _ in FILLS[s]:
                        if t == t_f:
                            pe.wait_ge(y_ready, NC * h + 2 * buf + 2)
                            if prev and finds_maxima(*prev[:2]):
                                pe.wait_ge(mt_copied, NC * (2 * prev[0] + prev[1] + 1) + prev[2] + 1)
                            pe.wait_ge(o_normed, NC * h + s)
                            if fill == 3:
                                pe.wait_ge(ye_added, NC * h + 3)
                            for q in range(2):
                                for f in range(KK):
                                    tok = P * (2 * pair + q)
                                    last = mm(PS[7][:, D * q:D * q + D], YT[:, buf, f, tok:tok + P],
                                              W2[:, ds(i, 1), f, :].rearrange("p a d -> p (a d)"),
                                              start=f == 0, stop=f == KK - 1)
                            last.then_inc(ye_ps, 1)

            pe.wait_ge(acc_init, NT // 2)
            pe.wait_ge(w2_in, 16)
            pe.wait_ge(mt_copied, NC)
            slots_of_loop(slot, pe)
            pe.wait_ge(u_ready, NC * H)
            pe.wait_ge(ye_added, NC * H)
            heads_out(NC - 1)
            pe.wait_ge(o_normed, NC * H)
            for n in range(NT // 2):
                r, q = n % 2, n // 2
                pe.wait_ge(ot_copied, max(0, n - 1))
                for k in range(KK):
                    for t in range(2):
                        last = pe.transpose(PS[r][:, P * (2 * k + t):P * (2 * k + t) + P],
                                            XO[:, 2 * n + t, P * k:P * k + P], IDN[:, :])
                last.then_inc(ot_ps, 1)
                pe.wait_ge(fin_b, max(0, n - 1))
                pe.wait_ge(ot_copied, n + 1)
                for t in range(2):
                    o = PS[2 + r][:, D * t:D * t + D]
                    mm(o, ONE1[0:1, 0, :], BROW[0:1, 2, :], start=True, stop=False)
                    for k in range(KK):
                        last = mm(o, TQ[:, r, P * (2 * k + t):P * (2 * k + t) + P], WO1[:, k, :],
                                  start=False, stop=k == KK - 1)
                last.then_inc(fin_ps, 1)


def _rows(w):
    import numpy as np
    return np.ascontiguousarray(w.reshape(w.shape[0] // P, P, *w.shape[1:]).swapaxes(0, 1))


def _shape_constants():
    import numpy as np
    q, k = np.arange(P)[:, None], np.arange(P)[None, :]
    far = -float(2 ** 30)
    masks = np.stack([np.where(q > k, far, 0.0),
                      np.where(q < k, far, 0.0),
                      np.eye(P)], 1)
    pos = np.arange(S)
    high, low, one = pos // P * P, pos % P, np.ones(S)
    side_q = [one, -high, one, -low] * 3
    side_k = [high, one, low, one] * 3
    pos_rows = np.stack([side_q, side_k], 1).reshape(POS, 2, S)
    pick = np.zeros((POS, 2, 4), np.float32)
    for r in range(POS):
        pick[r, 0, r // 4 if r % 2 == 0 else 3] = 1
        pick[r, 1, r // 4 if r % 2 == 1 else 3] = 1
    sel = np.zeros((P, HD + 1), np.float32)
    for p in range(P):
        if p % 32 <= HD:
            sel[p, p % 32] = 1
    return pos_rows.astype(np.float32), pick, masks.astype(np.float32), np.eye(P, dtype=np.float32), sel


def kernel(L0_attn_x, L0_attn_W_qkv, L0_attn_W_out, L0_ffn_weight, L0_ffn_bias, L1_attn_qkv_w, L1_attn_qkv_b,
           L1_attn_out_w, L1_attn_out_b, L1_attn_alibi_slopes, L1_ffn_gate_w, L1_ffn_gate_b, L1_ffn_w1, L1_ffn_b1,
           L1_ffn_w2, L1_ffn_b2):
    import numpy as np
    import concourse.bacc as bacc
    from concourse.bass_utils import run_bass_kernel_spmd

    a = [np.asarray(v) for v in (L0_attn_x, L0_attn_W_qkv, L0_attn_W_out, L0_ffn_weight, L0_ffn_bias, L1_attn_qkv_w,
                                 L1_attn_qkv_b, L1_attn_out_w, L1_attn_out_b, L1_attn_alibi_slopes, L1_ffn_gate_w,
                                 L1_ffn_gate_b, L1_ffn_w1, L1_ffn_b1, L1_ffn_w2, L1_ffn_b2)]
    x, wqkv0, wout0, wf, bf, wqkv1, bqkv1, wout1, bout1, slopes, gw, gb, w1, b1, w2, b2 = a
    pos_rows, pick, masks, ident, sel = _shape_constants()
    w1v = w1.reshape(E, 2, P, 2, KK, P).transpose(5, 0, 3, 1, 4, 2).reshape(P, E * 1024)
    b1v = b1.reshape(E, 2, P, 2).transpose(2, 0, 3, 1)
    w2v = w2.reshape(E, D, KK, P).transpose(3, 0, 2, 1)
    arrays = dict(
        x=x, w_qkv0=_rows(wqkv0.T), w_out0=_rows(wout0.T), w_ffn=_rows(wf), b_ffn=bf[None],
        w_qkv1=_rows(wqkv1.T), b_qk1=bqkv1[:2 * D].reshape(4, P).T, b_v1=bqkv1[None, 2 * D:], w_out1=_rows(wout1.T),
        b_out1=bout1[None], slopes=slopes[None], pos_rows=pos_rows, pick=pick, masks=masks, ident=ident, sel=sel,
        gate_w=_rows(gw.T), gate_b=gb[None], w1=w1v, b1=b1v, w2=w2v, b2=b2)
    nc = bacc.Bacc("TRN2", target_bir_lowering=False, num_devices=1)
    ins, feed = {}, {}
    for name, v in arrays.items():
        v = np.ascontiguousarray(v)
        feed["in_" + name] = v
        ins[name] = nc.dram_tensor("in_" + name, v.shape, mybir.dt.from_np(v.dtype), kind="ExternalInput").ap()
    out = nc.dram_tensor("out_rows", (1, S, D), F32, kind="ExternalOutput").ap()
    build(nc, out=out, **ins)
    return run_bass_kernel_spmd(nc, [feed], core_ids=[0]).results[0]["out_rows"]
```

```python
from contextlib import ExitStack

import concourse.bass as bass
from concourse import mybir

F32, F16, BF16 = mybir.dt.float32, mybir.dt.float16, mybir.dt.bfloat16
ALU = mybir.AluOpType
ACT = mybir.ActivationFunctionType
AX = mybir.AxisListType

P = 128
S, D = 2048, 256
H, HD = 16, 16
KK = D // P
NT = S // P
CH = 512
NC = S // CH
TC = CH // P
E, I = 8, 256
WS = 16.0
LN_EPS = 1e-5
L0_EPS = 1e-9

POS = 12
SPLITS = ((0, 0, 0, 1, 1, 2), (0, 1, 2, 0, 1, 0))
LOADS = (((0, 1, 3), (1, 1, 2), (2, 1, 1)), ((0, 3, 1), (0, 2, 1), (0, 1, 1)))
ROWS_A = POS + 6 * HD
ROWS_B = ROWS_A + 3

ORDER = (0, 3, 1, 2)
TILES = [TC * (a + 1) for a in ORDER]
OFF = [sum(TILES[:s]) for s in range(NC)]
PER_HEAD = sum(TILES)
PER_SLOT = PER_HEAD // NC
RING = 5
LAG = 3
STEPS = 16

UNITS = (((0, 0, 0, 1, 6, 2, 5, 7, 9), (1, 1, 0, 9, 12, 2, 12, 14, 15)),
         ((2, 0, 1, 1, 7, 1, 6, 9, 13),),
         ((3, 1, 1, 1, 7, 1, 8, 9, 13),),
         ())
FILLS = ((),
         ((0, 0, 0, 14, 15),),
         ((1, 0, 1, 13, 14),),
         ((2, 1, 0, 2, 3), (3, 1, 1, 14, 15)))
MAXT, MAXC = (7, 7, 6, 7), (8, 8, 7, 8)
HEADS, RCP, NORM = (10, 9, 10, 11), (11, 10, 11, 12), (12, 11, 12, 13)


def share(n, t, steps):
    return range(min(n, n * t // steps), min(n, n * (t + 1) // steps))


def tiles_at(s, t, steps=STEPS):
    return [PER_SLOT * s + k for k in share(PER_SLOT, t, steps)]


def last_in_bank7(s, t, n):
    for back in range(2):
        slot, m, until = (s - back) % NC, n - back if back else n, STEPS if back else t
        known = isinstance(m, int)
        uses = [(f[3], "fill", k + 1) for k, f in enumerate(FILLS[slot])] if not known or m >= 0 else []
        if not known or 0 < m <= NC * (H - 1):
            uses.append((MAXT[slot], "maxima", 0))
        if not known or m > 0:
            uses.append((HEADS[slot], "outputs", 0))
        uses = [use for use in uses if use[0] < until]
        if uses:
            return max(uses)[1], m, max(uses)[2]
    return None, 0, 0


def steps_b(s):
    return STEPS - 2 if s == NC - 1 else STEPS


def values_after(tile):
    n = tile - LAG
    if n < 0 or n in OFF[1:]:
        return []
    return [n - 1, n] if n - 1 in OFF[1:] else [n]


def place(n):
    c = max(c for c in range(NC) if OFF[c] <= n)
    return c, n - OFF[c]


def ds(start, size):
    return bass.ds(start, size)


def build(nc, x, w_qkv0, w_out0, w_ffn, b_ffn, w_qkv1, b_qk1, b_v1, w_out1, b_out1, slopes, pos_rows, pick,
          masks, ident, sel, gate_w, gate_b, w1, b1, w2, b2, out):
    ctx = ExitStack()
    with ctx:
        def sb(name, shape, dt=F32):
            return ctx.enter_context(nc.sbuf_tensor(name, shape, dt))

        def sem(name):
            return ctx.enter_context(nc.semaphore(name))

        XO = sb("XO", [P, NT, D])
        ACC = sb("ACC", [P, NT, D])
        XTH = sb("XTH", [P, KK, S], F16)
        XTL = sb("XTL", [P, KK, S], F16)
        W1H = sb("W1H", [P, E * 1024], F16)
        W1L = sb("W1L", [P, E * 1024], F16)
        W2 = sb("W2", [P, E, KK, D])
        VV = sb("VV", [P, NT, D])
        OPS = sb("OPS", [P, 4, 2, S], BF16)
        PR = sb("PR", [P, RING, CH])
        YT = sb("YT", [P, 2, KK, CH])
        U = sb("U", [P, 2, CH])
        VS = sb("VS", [P, 2, NT, 32])
        STG = sb("STG", [P, 2048])
        WO1 = sb("WO1", [P, KK, D])
        POSR = sb("POSR", [POS, 2, S], BF16)
        PICK = sb("PICK", [POS, 2, 4])
        SLB = sb("SLB", [POS, H])
        SLR = sb("SLR", [POS, H])
        SLP = sb("SLP", [POS, 3, H], BF16)
        SCL = sb("SCL", [POS, 2, H])
        MASK = sb("MASK", [P, 3, P], BF16)
        IDN = sb("IDN", [P, P])
        SEL = sb("SEL", [P, HD + 1])
        MV = sb("MV", [P, NT, 2])
        BST = sb("BST", [P, TC, 6])
        RSTD = sb("RSTD", [P, NT])
        VEPS = sb("VEPS", [P, NT])
        HALF = sb("HALF", [P, NT])
        ONE1 = sb("ONE1", [1, 2, P])
        ONES = sb("ONES", [P, 1])
        ZERO = sb("ZERO", [P, P], BF16)
        NIL = sb("NIL", [P, 1])
        ONEB = sb("ONEB", [P, CH], BF16)
        BROW = sb("BROW", [1, 3, D])
        GBR = sb("GBR", [1, E])
        BQK = sb("BQK", [P, 4])
        CAR = sb("CAR", [P, 4, 1])
        TH = sb("TH", [P, 2, CH])
        GT = sb("GT", [P, 2, CH])
        PM = sb("PM", [P, 2, TC, NC])
        NM = sb("NM", [P, 2, TC])
        NR = sb("NR", [P, 2, 2, TC])
        NP = sb("NP", [P, 2, 3, TC], BF16)
        MT = sb("MT", [12, 2, P], BF16)
        RC = sb("RC", [P, 2, TC])
        GW = sb("GW", [P, KK, E])
        GWH = sb("GWH", [P, KK, E], F16)
        GWL = sb("GWL", [P, KK, E], F16)
        LG = sb("LG", [P, NT, E])
        TOP = sb("TOP", [P, 4, NT])
        WE = sb("WE", [P, NT, E])
        WES = sb("WES", [P, NT, E])
        B1 = sb("B1", [P, E, 2, 2])
        B1S = sb("B1S", [P, E, 2, 2])
        B1T = sb("B1T", [P, E, 2])

        ops32 = OPS[:, :, :, :].rearrange("p a b s -> p (a b s)").bitcast(F32)
        EX = ops32[:, 0:2048].rearrange("p (m n) -> p m n", m=4)
        RE = ops32[:, 2048:4096].rearrange("p (m n) -> p m n", m=4)
        PH = ops32[:, 4096:6144].rearrange("p (m n) -> p m n", m=4)
        KV = ops32[:, 6144:7168].rearrange("p (m n) -> p m n", m=2)
        KC = ops32[:, 7168:8192].rearrange("p (m n) -> p m n", m=2)
        pr32 = PR[:, :, :].rearrange("p r n -> p (r n)")
        NUM = pr32[:, 0:1024].rearrange("p (m n) -> p m n", m=2)
        DEN = pr32[:, 1024:2048].rearrange("p (m n) -> p m n", m=2)
        yt32 = YT[:, :, :, :].rearrange("p a b n -> p (a b n)")
        w2flat = W2[:, :, :, :].rearrange("p e f d -> p (e f d)")
        WQH = w2flat[:, 0:768].bitcast(F16).rearrange("p (k n) -> p k n", k=KK)
        RT = yt32[:, 0:512].rearrange("p (a t e) -> p a t e", a=4, t=NT)
        WQL = w2flat[:, 768:1536].bitcast(F16).rearrange("p (k n) -> p k n", k=KK)
        WET = pr32[0:E, 0:S]
        B2 = pr32[0:E, S:S + D]
        TQ = pr32[:, 0:2 * CH].rearrange("p (m n) -> p m n", m=2)
        KVC = YT[:, 0]
        XN = ACC[:, 0:TC, :]
        OT0 = YT[:, 1]
        vv32 = VV[:, :, :].rearrange("p a b -> p (a b)")
        W0H = vv32[:, 0:768].bitcast(F16).rearrange("p (k n) -> p k n", k=KK)
        W0L = vv32[:, 768:1536].bitcast(F16).rearrange("p (k n) -> p k n", k=KK)
        FH = vv32[:, 1536:1792].bitcast(F16).rearrange("p (k n) -> p k n", k=KK)
        FL = vv32[:, 1792:2048].bitcast(F16).rearrange("p (k n) -> p k n", k=KK)
        WO0 = vv32[:, 2048:2560].rearrange("p (k n) -> p k n", k=KK)
        WF = vv32[:, 2560:3072].rearrange("p (k n) -> p k n", k=KK)
        QF = vv32[:, 3072:3584].rearrange("p (k n) -> p k n", k=KK)
        NF = vv32[:, 3584:4096].rearrange("p (k n) -> p k n", k=KK)
        RAW = [W1H[:, (E - 2) * 1024:].bitcast(F32), W1L[:, (E - 2) * 1024:].bitcast(F32)]
        RAW_LAST = [STG[:, 0:1024], STG[:, 1024:2048]]
        QV = ops32[:, 0:2048].rearrange("p (m n) -> p m n", m=4)
        QR = ops32[:, 2048:4096].rearrange("p (m n) -> p m n", m=4)
        QP = ops32[:, 4096:7168].bitcast(BF16).rearrange("p (m j n) -> p m j n", m=4, j=3)

        parts = nc.dram_tensor("qk_parts", (2, 3, D, S), BF16, kind="Internal").ap()
        x1_dram = nc.dram_tensor("x1_rows", (P, NT, D), F32, kind="Internal").ap()

        PS = [ctx.enter_context(nc.psum_tensor(f"bank{i}", [P, CH], F32)) for i in range(8)]
        MTP = PS[7][0:3 * TC, 256:256 + P // 2].bitcast(BF16)

        w_in0, cast_in, w_ffn_in, w_out_in, w_q1_in = (
            sem("w_in0"), sem("cast_in"), sem("w_ffn_in"), sem("w_out_in"), sem("w_q1_in"))
        small_in, const_in, w2_in, memset_done, w0h = (
            sem("small_in"), sem("const_in"), sem("w2_in"), sem("memset_done"), sem("w0h"))
        w0l, ffn_thr, ffn_q, ffn_t, ffn_h = (
            sem("w0l"), sem("ffn_thr"), sem("ffn_q"), sem("ffn_t"), sem("ffn_h"))
        ffn_split, w1_scaled, w1h_done, w1l_done, wq1h, wq1l = (
            sem("ffn_split"), sem("w1_scaled"), sem("w1h_done"), sem("w1l_done"), sem("wq1h"), sem("wq1l"))
        stats, var_eps, rstd_done, xn, xt_ps = (
            sem("stats"), sem("var_eps"), sem("rstd_done"), sem("xn"), sem("xt_ps"))
        xth, xtl, proj, exps, relus = (
            sem("xth"), sem("xtl"), sem("proj"), sem("exps"), sem("relus"))
        phi_k, phi_q, scan_k, v_read, scan_kv = (
            sem("phi_k"), sem("phi_q"), sem("scan_k"), sem("v_read"), sem("scan_kv"))
        nd, nd2, numden, rcp, outT = (
            sem("nd"), sem("nd2"), sem("numden"), sem("rcp"), sem("outT"))
        z_ps, s_ps, z_read, gate_a, gate_mid = (
            sem("z_ps"), sem("s_ps"), sem("z_read"), sem("gate_a"), sem("gate_mid"))
        x1_add, x1_spill, qk_ps, qk_v, qk_p0 = (
            sem("x1_add"), sem("x1_spill"), sem("qk_ps"), sem("qk_v"), sem("qk_p0"))
        qk_r1, qk_p1, qk_p2, parts_out, v_ps = (
            sem("qk_r1"), sem("qk_p1"), sem("qk_p2"), sem("parts_out"), sem("v_ps"))
        v_copied, lg_ps, lg_copied, gsplit, route = (
            sem("v_copied"), sem("lg_ps"), sem("lg_copied"), sem("gsplit"), sem("route"))
        expd, rstep, ones_rows, we_done, wet_ps = (
            sem("expd"), sem("rstep"), sem("ones_rows"), sem("we_done"), sem("wet_ps"))
        wet_copied, b2_ps, acc_init, b1_prep, slope_part = (
            sem("wet_copied"), sem("b2_ps"), sem("acc_init"), sem("b1_prep"), sem("slope_part"))
        scl, opa_rows, vs_ready, a_scored, a_reduced = (
            sem("scl"), sem("opa_rows"), sem("vs_ready"), sem("a_scored"), sem("a_reduced"))
        row_max, max_part, mt_ps, mt_copied, b_scored = (
            sem("row_max"), sem("max_part"), sem("mt_ps"), sem("mt_copied"), sem("b_scored"))
        b_exped, pv_done, u_ready, o_ps, o_rc = (
            sem("b_exped"), sem("pv_done"), sem("u_ready"), sem("o_ps"), sem("o_rc"))
        o_normed, up_ps, glu_done, gate_read = (
            sem("o_normed"), sem("up_ps"), sem("glu_done"), sem("gate_read"))
        y_ready, ye_ps, ye_added, carry, ot_ps = (
            sem("y_ready"), sem("ye_ps"), sem("ye_added"), sem("carry"), sem("ot_ps"))
        ot_copied, fin_ps, fin_th, fin_a, fin_b = (
            sem("ot_copied"), sem("fin_ps"), sem("fin_th"), sem("fin_a"), sem("fin_b"))
        fin_x, x1_in, out_st = (
            sem("fin_x"), sem("x1_in"), sem("out_st"))
        opa_in = [sem("opa_in0"), sem("opa_in1")]
        raw_in = [sem("raw_in0"), sem("raw_in1")]
        last_in = [sem("last_in0"), sem("last_in1")]
        opb_in = [sem("opb_in0"), sem("opb_in1")]
        mrow = [sem(f"mrow{s}") for s in range(NC)]
        x_in = [sem(f"x_in{c}") for c in range(NC)]

        block = ctx.enter_context(nc.Block())

        def wait(eng, semaphore, count):
            if not (isinstance(count, int) and count <= 0):
                eng.wait_ge(semaphore, count)

        def raw_of(e):
            return (RAW_LAST if e >= E - 2 else RAW)[e % 2]

        def slots_of_loop(run, eng):
            def fresh(value, least):
                return eng.snap(eng.to_reg(value), min_val=least, max_val=H // 2 - 2 + least)

            run(0, 0, 0)
            with eng.Fori(0, H // 2 - 1) as i:
                for u in range(2):
                    for s in range(NC):
                        if (u, s) != (0, 0):
                            run(fresh(i, 0), u, s)
                run(fresh(i + 1, 1), 0, 0)
            for u in range(2):
                for s in range(NC):
                    if (u, s) != (0, 0):
                        run(H // 2 - 1, u, s)

        def prev_of(i, u, s):
            if s:
                return i, u, s - 1
            if u:
                return i, 0, NC - 1
            if isinstance(i, int) and i == 0:
                return None
            return i - 1, 1, NC - 1

        def finds_maxima(i, u):
            return not (isinstance(i, int) and 2 * i + u == H - 1)

        @block.sync
        def _(sp):
            def fetch_experts(q):
                for half in range(2):
                    e = 2 * q + half
                    sp.dma_start(raw_of(e), w1[:, 1024 * e:1024 * e + 1024]).then_inc(
                        (last_in if e >= E - 2 else raw_in)[half], 16)

            for c in range(NC):
                sp.dma_start(XO[:, TC * c:TC * c + TC, :],
                             x[0].rearrange("(t p) d -> p t d", p=P)[:, TC * c:TC * c + TC, :]).then_inc(x_in[c], 16)
            fetch_experts(0)
            sp.wait_ge(w0l, 1)
            sp.dma_start(STG[:, 0:1536], w_qkv1.rearrange("p k n -> p (k n)")).then_inc(w_q1_in, 16)
            for c in range(NC):
                if c + 2 < E // 2:
                    sp.wait_ge(w1l_done, 2 * c + 2)
                    fetch_experts(c + 1)
                if c == 1:
                    sp.wait_ge(wq1l, 1)
                    fetch_experts(E // 2 - 1)
                sp.wait_ge(x1_add, 2 * c + 2)
                sp.dma_start(x1_dram[:, TC * c:TC * c + TC, :], XO[:, TC * c:TC * c + TC, :]).then_inc(x1_spill, 16)
            with sp.Fori(0, NC) as c:
                for m in range(4):
                    side, half = m // 2, m % 2
                    sp.wait_ge(qk_p2, 4 * c + m + 1)
                    sp.dma_start(parts[side, :, half * P:half * P + P, ds(c * CH, CH)].rearrange("j f t -> f j t"),
                                 QP[:, m, :, :]).then_inc(parts_out, 16)

            def load_a(h, par):
                for side in range(2):
                    row = POS
                    for first, parts_of, times_of in LOADS[side]:
                        rows = HD * parts_of * times_of
                        src = parts[side, first:first + parts_of, ds(HD * h, HD), :]
                        if times_of > 1:
                            src = src.broadcast_to([times_of, HD, S])
                        sp.dma_start(OPS[row:row + rows, par, side, :], src).then_inc(opa_in[par], 16)
                        row += rows

            def copy_b(h, par, times):
                sp.wait_ge(opa_in[par], 16 * 6 * times)
                sp.wait_ge(ones_rows, 2)
                sp.wait_ge(opa_rows, 2 * h + 2)
                sp.dma_start(OPS[0:ROWS_A, 2 + par, :, :], OPS[0:ROWS_A, par, :, :]).then_inc(opb_in[par], 16)

            def rows_out(par, s, k):
                sp.wait_ge(mt_copied, k)
                a = ORDER[s]
                sp.dma_start(OPS[ROWS_A:ROWS_B, 2 + par, 0, CH * a:CH * a + CH].rearrange("j (q t) -> j q t", q=TC),
                             MT[:, s % 2, :]).then_inc(mrow[s], 16)

            sp.wait_ge(v_ps, 2 * NC)
            sp.dma_start(W2[:, :, :, :], w2).then_inc(w2_in, 16)
            sp.wait_ge(parts_out, 16 * 16)
            load_a(0, 0)
            copy_b(0, 0, 1)
            load_a(1, 1)
            for s in range(NC):
                rows_out(0, s, s + 1)

            def slot(i, u, s):
                h = 2 * i + u
                prev = prev_of(i, u, s)
                if prev and finds_maxima(*prev[:2]):
                    rows_out((prev[1] + 1) % 2, prev[2], NC + NC * (2 * prev[0] + prev[1]) + prev[2] + 1)
                if s == 1:
                    if not (isinstance(i, int) and h + 2 >= H):
                        load_a(h + 2, u)
                    if not (isinstance(i, int) and h + 1 >= H):
                        copy_b(h + 1, 1 - u, i + 1 + u)

            slots_of_loop(slot, sp)
            sp.wait_ge(a_scored, PER_HEAD * H)
            sp.wait_ge(x1_spill, 16 * NC)
            sp.dma_start(ops32[:, 0:4096], x1_dram.rearrange("p t d -> p (t d)")).then_inc(x1_in, 16)
            with sp.Fori(0, NT // 2) as r:
                sp.wait_ge(fin_x, r + 1)
                sp.dma_start(out[0].rearrange("(t p) d -> p t d", p=P)[:, ds(2 * r, 2), :],
                             ops32[:, ds(CH * r, CH)].rearrange("p (t d) -> p t d", d=D)).then_inc(out_st, 16)
            sp.wait_ge(out_st, 16 * (NT // 2))

        @block.gpsimd
        def _(pool):
            pool.dma_start(MASK[:, :, :], masks).then_inc(cast_in, 16)
            pool.dma_start(POSR[:, :, :], pos_rows, max_dma_last_dim=4096).then_inc(cast_in, 16)
            pool.memset(ONES[:, :], 1.0).then_inc(memset_done, 1)
            pool.memset(HALF[:, :], -0.5).then_inc(memset_done, 1)
            pool.memset(ONE1[:, 0, :], 1.0).then_inc(memset_done, 1)
            pool.memset(ONE1[:, 1, :], WS).then_inc(memset_done, 1)
            pool.memset(ZERO[:, :], 0.0).then_inc(memset_done, 1)
            pool.memset(ONEB[:, :], 1.0).then_inc(memset_done, 1)
            pool.memset(NIL[:, :], 0.0).then_inc(memset_done, 1)
            pool.memset(CAR[:, :, :], 0.0).then_inc(memset_done, 1)
            pool.memset(VS[:, :, :, HD + 1:32], 0.0).then_inc(memset_done, 1)
            pool.memset(VS[:, :, :, HD:HD + 1], 1.0).then_inc(memset_done, 1)

            def rstd(k, tiles):
                pool.wait_ge(var_eps, k)
                pool.tensor_tensor(RSTD[:, tiles], VEPS[:, tiles], HALF[:, 0:TC], ALU.pow).then_inc(rstd_done, 1)

            pool.wait_ge(memset_done, 10)
            for c in range(NC):
                rstd(c + 1, slice(TC * c, TC * c + TC))

            def front(c):
                for m in range(2):
                    wait(pool, phi_q, 2 * c + m + 1)
                    wait(pool, scan_k, 2 * c + m + 1)
                    wait(pool, outT, 2 * c)
                    pool.tensor_tensor(DEN[:, m, :], PH[:, 2 + m, :], KC[:, m, :], ALU.mult).then_inc(nd, 1)
                    wait(pool, nd, 2 * c + m + 1)
                    pool.tensor_scalar(DEN[:, m, :], DEN[:, m, :], L0_EPS, None, ALU.add).then_inc(nd2, 1)
                    wait(pool, scan_kv, 2 * c + m + 1)
                    pool.tensor_tensor(NUM[:, m, :], PH[:, 2 + m, :], KVC[:, m, :], ALU.mult).then_inc(numden, 1)

            def back(c):
                for r in range(2):
                    wait(pool, gate_mid, 2 * c + r + 1)
                    xs = XO[:, ds(TC * c + 2 * r, 2), :].rearrange("p t d -> p (t d)")
                    pool.tensor_tensor(xs, xs, GT[:, r, :], ALU.add).then_inc(x1_add, 1)
                if c:
                    rstd(NC + c, ds(TC * c - TC, TC))

            def scale(q):
                for half in range(2):
                    if 2 * q >= E - 2:
                        pool.wait_ge(last_in[half], 16)
                    else:
                        pool.wait_ge(raw_in[half], 16 * q + 16)
                    pool.tensor_scalar(raw_of(2 * q + half), raw_of(2 * q + half), WS, 0.0, ALU.mult, ALU.add)\
                        .then_inc(w1_scaled, 1)

            def low_parts(q):
                for e in (2 * q, 2 * q + 1):
                    pool.wait_ge(w1h_done, e + 1)
                    pool.tensor_tensor(W1L[:, 1024 * e:1024 * e + 1024], raw_of(e), W1H[:, 1024 * e:1024 * e + 1024],
                                       ALU.subtract).then_inc(w1l_done, 1)

            front(0)
            scale(0)
            for c in range(NC - 1):
                front(c + 1)
                low_parts(c)
                back(c)
                if c + 1 < E // 2 - 1:
                    scale(c + 1)
            back(NC - 1)
            rstd(2 * NC, ds(TC * (NC - 1), TC))
            scale(E // 2 - 1)
            pool.wait_ge(w1l_done, E - 2)
            low_parts(E // 2 - 1)

            def rows(h, par):
                for side in range(2):
                    pool.tensor_tensor(OPS[0:POS, par, side, :], POSR[:, side, :],
                                       SCL[:, side, ds(h, 1)].broadcast_to([POS, S]), ALU.mult).then_inc(opa_rows, 1)

            def values(h, par):
                pool.tensor_copy(VS[:, par, :, 0:HD], VV[:, :, ds(HD * h, HD)]).then_inc(vs_ready, 1)

            nought = NIL[:, 0:1].broadcast_to([P, TC])

            def maxima(par, k):
                pool.wait_ge(row_max, k)
                pool.tensor_tensor(NP[:, par, 0, :], NM[:, par, :], nought, ALU.add).then_inc(max_part, 1)
                pool.wait_ge(max_part, 5 * k - 4)
                pool.tensor_tensor(NR[:, par, 0, :], NM[:, par, :], NP[:, par, 0, :], ALU.subtract).then_inc(max_part, 1)
                pool.wait_ge(max_part, 5 * k - 3)
                pool.tensor_tensor(NP[:, par, 1, :], NR[:, par, 0, :], nought, ALU.add).then_inc(max_part, 1)
                pool.wait_ge(max_part, 5 * k - 2)
                pool.tensor_tensor(NR[:, par, 1, :], NR[:, par, 0, :], NP[:, par, 1, :], ALU.subtract).then_inc(max_part, 1)
                pool.wait_ge(max_part, 5 * k - 1)
                pool.tensor_tensor(NP[:, par, 2, :], NR[:, par, 1, :], nought, ALU.add).then_inc(max_part, 1)

            pool.wait_ge(scl, 8)
            pool.wait_ge(cast_in, 32)
            pool.wait_ge(parts_out, 16 * 16)
            pool.wait_ge(w1l_done, E)
            for par in range(2):
                pool.memset(OPS[96:P, 2 + par, 1, :], 1.0).then_inc(ones_rows, 1)
            pool.wait_ge(ones_rows, 2)
            pool.wait_ge(opa_rows, 2)
            rows(1, 1)
            pool.wait_ge(v_copied, 2 * NC)
            values(0, 0)
            for s in range(NC):
                maxima(s % 2, s + 1)

            def slot(i, u, s):
                h = 2 * i + u
                if s == 1:
                    pool.wait_ge(up_ps, 2 * (NC * h + UNITS[s][0][0]) + 1)
                    if not (isinstance(i, int) and h + 2 >= H):
                        rows(h + 2, u)
                    if not (isinstance(i, int) and h + 1 >= H):
                        values(h + 1, 1 - u)
                if finds_maxima(i, u):
                    maxima(s % 2, NC * (h + 1) + s + 1)

            slots_of_loop(slot, pool)

            pool.wait_ge(x1_in, 16)
            for q in range(NT // 4):
                for r in range(2):
                    wait(pool, fin_b, 2 * q + r + 1)
                    xs = ops32[:, ds(2 * CH * q + CH * r, CH)]
                    pool.tensor_tensor(xs, xs, GT[:, r, :], ALU.add).then_inc(fin_x, 1)

        @block.scalar
        def _(act):
            act.dma_start(STG[:, 0:1536], w_qkv0.rearrange("p k n -> p (k n)")).then_inc(w_in0, 16)
            act.dma_start(IDN[:, :], ident).then_inc(const_in, 16)
            act.dma_start(SEL[:, :], sel).then_inc(const_in, 16)
            act.dma_start(WF[:, :, :], w_ffn).then_inc(w_ffn_in, 16)
            act.dma_start(WO0[:, :, :], w_out0).then_inc(w_out_in, 16)
            act.dma_start(BROW[0:1, 0, :], b_ffn).then_inc(small_in, 16)
            act.dma_start(BROW[0:1, 1, :], b_v1).then_inc(small_in, 16)
            act.dma_start(BROW[0:1, 2, :], b_out1).then_inc(small_in, 16)
            act.dma_start(GBR[0:1, :], gate_b).then_inc(small_in, 16)
            act.dma_start(GW[:, :, :], gate_w).then_inc(small_in, 16)
            act.dma_start(BQK[:, :], b_qk1).then_inc(small_in, 16)
            act.dma_start(WO1[:, :, :], w_out1).then_inc(small_in, 16)
            act.dma_start(B2[:, :], b2).then_inc(small_in, 16)
            act.dma_start(B1[:, :, :, :], b1).then_inc(small_in, 16)
            act.dma_start(SLB[:, :], slopes.broadcast_to([POS, H])).then_inc(small_in, 16)
            act.dma_start(PICK[:, :, :], pick).then_inc(small_in, 16)
            act.wait_ge(w_in0, 16)
            act.activation(W0H[:, :, :].rearrange("p k n -> p (k n)"), STG[:, 0:1536], ACT.Copy, scale=WS).then_inc(w0h, 1)

            def high(c, k0):
                for k in range(KK):
                    wait(act, xt_ps, k0 + KK * c + k + 1)
                    act.activation(XTH[:, k, ds(CH * c, CH)], PS[k][:, :], ACT.Copy).then_inc(xth, 1)

            def front(c):
                high(c, 0)
                for n, (m, t) in enumerate(((0, 0), (1, 1), (2, 4), (3, 5))):
                    wait(act, proj, 6 * c + t + 1)
                    wait(act, phi_k if m < 2 else phi_q, 2 * c)
                    bank = PS[2 + t % 4]
                    act.activation(EX[:, m, :], bank[:, :], ACT.Exp, scale=1 / WS).then_inc(exps, 1)
                    act.activation(RE[:, m, :], bank[:, :], ACT.Relu, scale=1 / WS).then_inc(relus, 1)

            def back(c):
                for r in range(2):
                    wait(act, z_ps, 2 * c + r + 1)
                    if c:
                        wait(act, x1_add, 2 * c - 1 + r)
                    act.activation(TH[:, r, :], PS[6 + r][:, :], ACT.Tanh, scale=0.5)
                    act.activation(GT[:, r, :], PS[6 + r][:, :], ACT.Copy).then_inc(z_read, 1)

            def high_parts(q):
                for e in (2 * q, 2 * q + 1):
                    act.wait_ge(w1_scaled, e + 1)
                    act.activation(W1H[:, 1024 * e:1024 * e + 1024], raw_of(e), ACT.Copy).then_inc(w1h_done, 1)

            front(0)
            act.wait_ge(w_q1_in, 16)
            act.activation(WQH[:, :, :].rearrange("p k n -> p (k n)"), STG[:, 0:1536], ACT.Copy, scale=WS).then_inc(wq1h, 1)
            act.wait_ge(small_in, 16 * 11)
            act.activation(GWH[:, :, :], GW[:, :, :], ACT.Copy, scale=WS).then_inc(wq1h, 1)
            for k in range(KK):
                act.wait_ge(ffn_t, k + 1)
                act.activation(FH[:, k, :], PS[6 + k][:, 0:D], ACT.Copy).then_inc(ffn_h, 1)
            for c in range(NC - 1):
                front(c + 1)
                high_parts(c)
                back(c)
            back(NC - 1)

            high(0, KK * NC)
            act.wait_ge(phi_q, 2 * NC)
            act.wait_ge(scan_kv, 2 * NC)
            act.wait_ge(numden, 2 * NC)
            act.wait_ge(gsplit, 1)
            for c in range(NC):
                for m in range(4):
                    side = m // 2
                    wait(act, qk_ps, 4 * c + m + 1)
                    wait(act, qk_r1, 4 * c)
                    scale = 1 / WS if side else HD ** -0.5 / WS
                    act.activation(QV[:, m, :], PS[2 + m][:, :], ACT.Identity, scale=scale,
                                   bias=BQK[:, m:m + 1]).then_inc(qk_v, 1)
                    wait(act, qk_v, 4 * c + m + 1)
                    wait(act, parts_out, 64 * c)
                    act.activation(QP[:, m, 0, :], QV[:, m, :], ACT.Copy).then_inc(qk_p0, 1)
                if c + 1 < NC:
                    high(c + 1, KK * NC)
                for m in range(4):
                    wait(act, qk_r1, 4 * c + m + 1)
                    act.activation(QP[:, m, 1, :], QR[:, m, :], ACT.Copy).then_inc(qk_p1, 1)
                for r in range(2):
                    wait(act, v_ps, 2 * c + r + 1)
                    act.activation(VV[:, ds(TC * c + 2 * r, 2), :].rearrange("p t d -> p (t d)"), PS[6 + r][:, :],
                                   ACT.Copy, scale=1 / WS).then_inc(v_copied, 1)
                if c == 1:
                    act.wait_ge(w1l_done, E - 2)
                    high_parts(E // 2 - 1)
            act.wait_ge(scl, 8)
            act.wait_ge(cast_in, 32)
            act.wait_ge(parts_out, 16 * 16)
            for side in range(2):
                act.activation(OPS[0:POS, 0, side, :], POSR[:, side, :], ACT.Copy, scale=SCL[:, side, 0:1])\
                    .then_inc(opa_rows, 1)
            act.wait_ge(route, 1)
            act.activation(TOP[:, 3, :], TOP[:, 2, :], ACT.Exp).then_inc(expd, 1)
            for c in range(NC):
                act.wait_ge(wet_ps, c + 1)
                act.activation(WET[:, CH * c:CH * c + CH], PS[4 + c % 2][0:E, :], ACT.Copy).then_inc(wet_copied, 1)
            for r in range(NT // 2):
                act.wait_ge(b2_ps, r + 1)
                act.activation(ACC[:, 2 * r:2 * r + 2, :].rearrange("p t d -> p (t d)"), PS[4 + r % 2][:, :],
                               ACT.Copy).then_inc(acc_init, 1)

            def max_rows(par, k, dma):
                act.wait_ge(mt_ps, k)
                if dma is not None:
                    act.wait_ge(*dma)
                act.activation(MT[:, par, :], MTP, ACT.Copy).then_inc(mt_copied, 1)

            for s in range(NC):
                max_rows(s % 2, s + 1, (mrow[s - 2], 16) if s >= 2 else None)

            def chunk_out(h, c):
                act.wait_ge(pv_done, PER_HEAD * h + OFF[c] + TILES[c])
                act.activation(U[:, c % 2, :], PS[4][:, :], ACT.Copy).then_inc(u_ready, 1)

            def slot(i, u, s):
                h = 2 * i + u
                prev = prev_of(i, u, s)
                for t in range(STEPS):
                    for tile in tiles_at(s, t, steps_b(s)):
                        c, k = place(tile)
                        idx = PER_HEAD * h + tile
                        off = P * max(0, k - TC * ORDER[c])
                        act.wait_ge(b_scored, idx + 1)
                        if tile >= RING:
                            act.wait_ge(pv_done, idx + 1 - RING)
                        act.activation(PR[:, tile % RING, off:CH], PS[2 + tile % 2][:, off:CH],
                                       ACT.Exp).then_inc(b_exped, 1)
                        if tile - LAG + 1 in OFF[1:]:
                            chunk_out(h, OFF.index(tile - LAG + 1) - 1)
                    for unit, f, _, _, _, _, t_tanh, _, _ in UNITS[s]:
                        if t == t_tanh:
                            m = NC * h + unit
                            act.wait_ge(up_ps, 2 * m + 1)
                            if not (isinstance(m, int) and m < 2):
                                act.wait_ge(y_ready, m - 1)
                            act.activation(TH[:, unit % 2, :], PS[5][:, :], ACT.Tanh, scale=0.851 / WS,
                                           bias=B1T[:, ds(i, 1), f:f + 1].rearrange("p a b -> p (a b)"))
                            act.activation(GT[:, unit % 2, :], PS[5][:, :], ACT.Identity,
                                           bias=B1S[:, ds(i, 1), 0, f:f + 1].rearrange("p a b -> p (a b)"))\
                                .then_inc(gate_read, 1)
                    if t == MAXC[s] and prev and finds_maxima(*prev[:2]):
                        ph, q = 2 * prev[0] + prev[1], prev[2]
                        sent = (mrow[q - 2], 16 * (ph + 2)) if q >= 2 else (mrow[q + 2], 16 * (ph + 1))
                        max_rows(q % 2, NC * (ph + 1) + q + 1, sent)
                if s == NC - 1:
                    chunk_out(h, s)

            slots_of_loop(slot, act)
            for q in range(NT // 4):
                for r in range(2):
                    if r == 0:
                        act.wait_ge(ye_added, NC * H)
                    wait(act, fin_a, 2 * q)
                    act.activation(TH[:, r, :], ACC[:, ds(4 * q + 2 * r, 2), :].rearrange("p t d -> p (t d)"), ACT.Tanh,
                                   scale=0.5).then_inc(fin_th, 1)
                    wait(act, ot_ps, 2 * q + r + 1)
                    wait(act, fin_ps, 2 * q)
                    act.activation(TQ[:, r, :], PS[r][:, :], ACT.Copy).then_inc(ot_copied, 1)

        @block.vector
        def _(dve):
            def norm_stats(c, k0):
                for t in range(TC):
                    dve.bn_stats(BST[:, t, :], XO[:, ds(TC * c + t, 1), :].rearrange("p a d -> p (a d)"))\
                        .then_inc(stats, 1)
                for t in range(TC):
                    dve.wait_ge(stats, 2 * TC * (k0 + c) + TC)
                    dve.bn_aggr(MV[:, ds(TC * c + t, 1), :].rearrange("p a d -> p (a d)"), BST[:, t, :]).then_inc(stats, 1)
                dve.wait_ge(stats, 2 * TC * (k0 + c) + 2 * TC)
                dve.tensor_scalar(VEPS[:, ds(TC * c, TC)], MV[:, ds(TC * c, TC), 1:2].rearrange("p a d -> p (a d)"),
                                  LN_EPS, None, ALU.add).then_inc(var_eps, 1)

            def norm_apply(c, k0):
                dve.wait_ge(rstd_done, k0 + c + 1)
                if not (isinstance(c, int) and k0 + c == 0):
                    dve.wait_ge(xt_ps, KK * (k0 + c))
                for t in range(TC):
                    dve.tensor_scalar(XN[:, t, :],
                                      XO[:, ds(TC * c + t, 1), :].rearrange("p a d -> p (a d)"),
                                      MV[:, ds(TC * c + t, 1), 0:1].rearrange("p a d -> p (a d)"),
                                      RSTD[:, ds(TC * c + t, 1)], ALU.subtract, ALU.mult).then_inc(xn, 1)

            def low(c, k0):
                for k in range(KK):
                    wait(dve, xth, k0 + KK * c + k + 1)
                    dve.tensor_tensor(XTL[:, k, ds(CH * c, CH)], PS[k][:, :], XTH[:, k, ds(CH * c, CH)],
                                      ALU.subtract).then_inc(xtl, 1)

            for c in range(NC):
                dve.wait_ge(x_in[c], 16)
                norm_stats(c, 0)
                if c == 0:
                    norm_apply(0, 0)
                    dve.wait_ge(w0h, 1)
                    dve.scalar_tensor_tensor(W0L[:, :, :].rearrange("p k n -> p (k n)"), STG[:, 0:1536], WS,
                                             W0H[:, :, :].rearrange("p k n -> p (k n)"),
                                             ALU.mult, ALU.subtract).then_inc(w0l, 1)
                    low(0, 0)
                    dve.wait_ge(w_ffn_in, 16)
                    dve.tensor_reduce(TOP[:, 0, 0:KK], WF[:, :, :], AX.X, ALU.add, apply_absolute_value=True)\
                        .then_inc(ffn_thr, 1)
                    dve.wait_ge(ffn_thr, 1)
                    dve.tensor_scalar(TOP[:, 1, 0:KK], TOP[:, 0, 0:KK], 1.0 / D, 0.7, ALU.mult, ALU.mult)\
                        .then_inc(ffn_thr, 1)
                    dve.wait_ge(ffn_thr, 2)
                    dve.tensor_scalar(TOP[:, 2, 0:KK], TOP[:, 1, 0:KK], -1.0, None, ALU.mult).then_inc(ffn_thr, 1)
                    dve.wait_ge(ffn_thr, 3)
                    for k in range(KK):
                        dve.tensor_scalar(NF[:, k, :], WF[:, k, :], TOP[:, 2, k:k + 1], None, ALU.is_lt).then_inc(ffn_q, 1)
                    dve.wait_ge(ffn_q, 2)
                    for k in range(KK):
                        dve.scalar_tensor_tensor(QF[:, k, :], WF[:, k, :], TOP[:, 1, k:k + 1], NF[:, k, :],
                                                 ALU.is_gt, ALU.subtract).then_inc(ffn_q, 1)
                    dve.wait_ge(ffn_q, 4)
                    dve.tensor_tensor(QF[:, :, :], QF[:, :, :], WF[:, :, :], ALU.subtract).then_inc(ffn_q, 1)
                    dve.wait_ge(ffn_q, 5)
                    dve.tensor_tensor(QF[:, :, :], WF[:, :, :], QF[:, :, :], ALU.add).then_inc(ffn_q, 1)

            dve.wait_ge(memset_done, 10)

            def front(c, more):
                if c:
                    low(c, 0)
                if more:
                    norm_apply(c + 1, 0)
                if c >= 2:
                    gated(c - 2)
                for m in range(2):
                    wait(dve, relus, 4 * c + m + 1)
                    wait(dve, nd2, 2 * c)
                    dve.scalar_tensor_tensor(PH[:, m, :], EX[:, m, :], 1.0, RE[:, m, :], ALU.min, ALU.add)\
                        .then_inc(phi_k, 1)
                    wait(dve, phi_k, 2 * c + m + 1)
                    wait(dve, carry, 4 * c)
                    dve.tensor_tensor_scan(KC[:, m, :], ONES[:, 0:1].broadcast_to([P, CH]), PH[:, m, :], CAR[:, m, :], ALU.mult, ALU.add)\
                        .then_inc(scan_k, 1)
                for m in range(2):
                    wait(dve, proj, 6 * c + 3 + m)
                    dve.scalar_tensor_tensor(KV[:, m, :], PS[4 + m][:, :], 1 / WS, PH[:, m, :], ALU.mult, ALU.mult)\
                        .then_inc(v_read, 1)
                    wait(dve, v_read, 2 * c + m + 1)
                    wait(dve, numden, 2 * c)
                    dve.tensor_tensor_scan(KVC[:, m, :], ONES[:, 0:1].broadcast_to([P, CH]), KV[:, m, :], CAR[:, 2 + m, :], ALU.mult, ALU.add)\
                        .then_inc(scan_kv, 1)
                for m in range(2):
                    wait(dve, relus, 4 * c + m + 3)
                    dve.scalar_tensor_tensor(PH[:, 2 + m, :], EX[:, 2 + m, :], 1.0, RE[:, 2 + m, :], ALU.min, ALU.add)\
                        .then_inc(phi_q, 1)
                for m in range(2):
                    wait(dve, scan_k, 2 * c + m + 1)
                    dve.tensor_copy(CAR[:, m, :], KC[:, m, CH - 1:CH]).then_inc(carry, 1)
                    wait(dve, scan_kv, 2 * c + m + 1)
                    dve.tensor_copy(CAR[:, 2 + m, :], KVC[:, m, CH - 1:CH]).then_inc(carry, 1)

            def back(c):
                for m in range(2):
                    wait(dve, nd2, 2 * c + m + 1)
                    dve.reciprocal(DEN[:, m, :], DEN[:, m, :]).then_inc(rcp, 1)
                    wait(dve, rcp, 2 * c + m + 1)
                    wait(dve, numden, 2 * c + m + 1)
                    wait(dve, s_ps, 2 * c)
                    dve.tensor_tensor(OT0[:, m, :], NUM[:, m, :], DEN[:, m, :], ALU.mult).then_inc(outT, 1)

            def gate(c):
                for r in range(2):
                    wait(dve, z_read, 2 * c + r + 1)
                    dve.scalar_tensor_tensor(GT[:, r, :], TH[:, r, :], 1.0, GT[:, r, :], ALU.add, ALU.mult)\
                        .then_inc(gate_a, 1)

            def gated(c):
                for r in range(2):
                    wait(dve, gate_a, 2 * c + r + 1)
                    wait(dve, s_ps, 2 * c + r + 1)
                    dve.scalar_tensor_tensor(GT[:, r, :], PS[6 + r][:, :], 0.5 * HD ** -0.5, GT[:, r, :], ALU.mult, ALU.mult)\
                        .then_inc(gate_mid, 1)

            def next_stats(c):
                wait(dve, x1_add, 2 * c + 2)
                norm_stats(c, NC)

            front(0, True)
            dve.wait_ge(wq1h, 2)
            dve.scalar_tensor_tensor(WQL[:, :, :].rearrange("p k n -> p (k n)"), STG[:, 0:1536], WS,
                                     WQH[:, :, :].rearrange("p k n -> p (k n)"), ALU.mult, ALU.subtract).then_inc(wq1l, 1)
            dve.wait_ge(small_in, 16 * 11)
            dve.scalar_tensor_tensor(GWL[:, :, :], GW[:, :, :], WS, GWH[:, :, :], ALU.mult, ALU.subtract).then_inc(wq1l, 1)
            dve.tensor_scalar(BQK[:, 0:2], BQK[:, 0:2], HD ** -0.5, None, ALU.mult).then_inc(gsplit, 1)
            for k in range(KK):
                dve.wait_ge(ffn_h, k + 1)
                dve.tensor_tensor(FL[:, k, :], PS[6 + k][:, 0:D], FH[:, k, :], ALU.subtract).then_inc(ffn_split, 1)
            for c in range(NC):
                if c + 1 < NC:
                    front(c + 1, c + 2 < NC)
                if c == NC - 1:
                    gated(c - 1)
                    norm_apply(0, NC)
                back(c)
                gate(c)
                if c:
                    next_stats(c - 1)
            low(0, KK * NC)
            gated(NC - 1)
            next_stats(NC - 1)

            def prepare():
                dve.tensor_copy(SLP[:, 0, :], SLB[:, :]).then_inc(slope_part, 1)
                dve.wait_ge(slope_part, 1)
                dve.tensor_tensor(SLR[:, :], SLB[:, :], SLP[:, 0, :], ALU.subtract).then_inc(slope_part, 1)
                dve.wait_ge(slope_part, 2)
                dve.tensor_copy(SLP[:, 1, :], SLR[:, :]).then_inc(slope_part, 1)
                dve.wait_ge(slope_part, 3)
                dve.tensor_tensor(SLR[:, :], SLR[:, :], SLP[:, 1, :], ALU.subtract).then_inc(slope_part, 1)
                dve.wait_ge(slope_part, 4)
                dve.tensor_copy(SLP[:, 2, :], SLR[:, :]).then_inc(slope_part, 1)
                dve.wait_ge(slope_part, 5)
                for side in range(2):
                    dve.tensor_scalar(SCL[:, side, :], SLP[:, 0, :], PICK[:, side, 0:1], PICK[:, side, 3:4],
                                      ALU.mult, ALU.add).then_inc(scl, 1)
                for j in (1, 2):
                    for side in range(2):
                        dve.wait_ge(scl, 2 * j)
                        dve.scalar_tensor_tensor(SCL[:, side, :], SLP[:, j, :], PICK[:, side, j:j + 1], SCL[:, side, :],
                                                 ALU.mult, ALU.add).then_inc(scl, 1)
                dve.tensor_scalar(B1S[:, :, 0, :], B1[:, :, 0, :], WS, None, ALU.mult).then_inc(scl, 1)
                dve.tensor_scalar(B1T[:, :, :], B1[:, :, 0, :], 0.851, None, ALU.mult).then_inc(scl, 1)
                dve.tensor_scalar(B1S[:, :, 1, :], B1[:, :, 1, :], 1.0, WS, ALU.add, ALU.mult).then_inc(b1_prep, 1)

            norm_apply(1, NC)
            for c in range(NC):
                dve.wait_ge(lg_ps, c + 1)
                dve.tensor_scalar(LG[:, ds(TC * c, TC), :].rearrange("p t e -> p (t e)"), PS[7][:, 0:TC * E], 1 / WS, None,
                                  ALU.mult).then_inc(lg_copied, 1)
                for m in range(4):
                    wait(dve, qk_p0, 4 * c + m + 1)
                    wait(dve, qk_p2, 4 * c)
                    dve.tensor_tensor(QR[:, m, :], QV[:, m, :], QP[:, m, 0, :], ALU.subtract).then_inc(qk_r1, 1)
                if c + 1 < NC:
                    low(c + 1, KK * NC)
                if c + 2 < NC:
                    norm_apply(c + 2, NC)
                if c == 0:
                    prepare()
                for m in range(4):
                    wait(dve, qk_p1, 4 * c + m + 1)
                    dve.tensor_tensor(QP[:, m, 2, :], QR[:, m, :], QP[:, m, 1, :], ALU.subtract).then_inc(qk_p2, 1)

            def step(ins):
                ins.then_inc(rstep, 1)
                dve.wait_ge(rstep, step.n)
                step.n += 1
            step.n = 1
            dve.wait_ge(lg_copied, NC)
            RANK, TMP, FIRST, SECOND = RT[:, 0], RT[:, 1], RT[:, 2], RT[:, 3]
            step(dve.memset(RANK, 0.0))
            for e in range(E):
                rival = LG[:, :, e:e + 1].broadcast_to([P, NT, E])
                if e:
                    step(dve.tensor_tensor(TMP[:, :, 0:e], rival[:, :, 0:e], LG[:, :, 0:e], ALU.is_gt))
                if e < E - 1:
                    step(dve.tensor_tensor(TMP[:, :, e + 1:E], rival[:, :, e + 1:E], LG[:, :, e + 1:E], ALU.is_ge))
                if e:
                    step(dve.tensor_tensor(RANK[:, :, 0:e], RANK[:, :, 0:e], TMP[:, :, 0:e], ALU.add))
                if e < E - 1:
                    step(dve.tensor_tensor(RANK[:, :, e + 1:E], RANK[:, :, e + 1:E], TMP[:, :, e + 1:E], ALU.add))
            step(dve.tensor_scalar(FIRST, RANK, 0.0, None, ALU.is_equal))
            step(dve.tensor_scalar(SECOND, RANK, 1.0, None, ALU.is_equal))
            step(dve.tensor_tensor(TMP, FIRST, LG[:, :, :], ALU.mult))
            step(dve.tensor_reduce(TOP[:, 0, :], TMP, AX.X, ALU.add))
            step(dve.tensor_tensor(TMP, SECOND, LG[:, :, :], ALU.mult))
            step(dve.tensor_reduce(TOP[:, 1, :], TMP, AX.X, ALU.add))
            dve.tensor_tensor(TOP[:, 2, :], TOP[:, 1, :], TOP[:, 0, :], ALU.subtract).then_inc(route, 1)
            dve.wait_ge(expd, 1)
            step(dve.tensor_scalar(TOP[:, 0, :], TOP[:, 3, :], 1.0, None, ALU.add))
            step(dve.reciprocal(TOP[:, 1, :], TOP[:, 0, :]))
            step(dve.tensor_tensor(TOP[:, 2, :], TOP[:, 3, :], TOP[:, 1, :], ALU.mult))
            step(dve.tensor_tensor(FIRST, FIRST, TOP[:, 1, :].unsqueeze(2).broadcast_to([P, NT, E]), ALU.mult))
            step(dve.tensor_tensor(SECOND, SECOND, TOP[:, 2, :].unsqueeze(2).broadcast_to([P, NT, E]), ALU.mult))
            step(dve.tensor_tensor(WE[:, :, :], FIRST, SECOND, ALU.add))
            dve.tensor_scalar(WES[:, :, :], WE[:, :, :], 0.5 / WS ** 2, None, ALU.mult).then_inc(we_done, 1)

            def reduce_a(h40, tile, banks=2):
                c, k = place(tile)
                a = ORDER[c]
                xq, gg = k // (a + 1), k % (a + 1)
                width = CH if gg < a else P * (xq + 1)
                dve.wait_ge(a_scored, h40 + tile + 1)
                dve.tensor_reduce(PM[:, c % 2, xq, gg:gg + 1], PS[tile % banks][:, 0:width], AX.X, ALU.max)\
                    .then_inc(a_reduced, 1)

            def row_maxima(h40, s, k):
                a = ORDER[s]
                dve.wait_ge(a_reduced, h40 + OFF[s] + TILES[s])
                if not (isinstance(k, int) and k <= 2):
                    dve.wait_ge(mt_ps, k - 2)
                dve.tensor_reduce(NM[:, s % 2, :], PM[:, s % 2, :, 0:a + 1], AX.X, ALU.max, negate=True)\
                    .then_inc(row_max, 1)

            for s in range(NC):
                for k in range(TILES[s]):
                    reduce_a(0, OFF[s] + k, 4)
                row_maxima(0, s, s + 1)

            outputs = PS[7][:, 0:TC * (HD + 1)].rearrange("p (q c) -> p q c", q=TC)

            def inverse(i, u, s):
                dve.wait_ge(o_ps, NC * (2 * i + u) + s + 1)
                dve.reciprocal(RC[:, s % 2, :], outputs[:, :, HD:HD + 1].rearrange("p q c -> p (q c)")).then_inc(o_rc, 1)

            def divide(i, u, s):
                b = ORDER[s]
                dve.wait_ge(o_rc, NC * (2 * i + u) + s + 1)
                dve.tensor_tensor(XO[:, TC * b:TC * b + TC, ds(HD * (2 * i + u), HD)], outputs[:, :, 0:HD],
                                  RC[:, s % 2, :].unsqueeze(2).broadcast_to([P, TC, HD]), ALU.mult)\
                    .then_inc(o_normed, 1)

            def slot(i, u, s):
                h = 2 * i + u
                prev = prev_of(i, u, s)
                for t in range(STEPS):
                    if finds_maxima(i, u):
                        for tile in tiles_at(s, t):
                            reduce_a(PER_HEAD * (h + 1), tile)
                    for unit, f, buf, _, _, _, _, t_gate, t_out in UNITS[s]:
                        m = NC * h + unit
                        if t == t_gate:
                            dve.wait_ge(gate_read, m + 1)
                            dve.scalar_tensor_tensor(GT[:, unit % 2, :], TH[:, unit % 2, :], 1.0, GT[:, unit % 2, :],
                                                     ALU.add, ALU.mult).then_inc(glu_done, 1)
                        if t == t_out:
                            dve.wait_ge(up_ps, 2 * m + 2)
                            dve.wait_ge(glu_done, m + 1)
                            dve.scalar_tensor_tensor(YT[:, buf, f, :], PS[6][:, :],
                                                     B1S[:, ds(i, 1), 1, f:f + 1].rearrange("p a b -> p (a b)"),
                                                     GT[:, unit % 2, :], ALU.add, ALU.mult).then_inc(y_ready, 1)
                    for fill, buf, pair, _, t_add in FILLS[s]:
                        if t == t_add:
                            dve.wait_ge(ye_ps, NC * h + fill + 1)
                            for q in range(2):
                                tile = TC * (2 * u + buf) + 2 * pair + q
                                add = dve.scalar_tensor_tensor(
                                    ACC[:, tile, :], PS[7][:, D * q:D * q + D], WES[:, tile, ds(i, 1)],
                                    ACC[:, tile, :], ALU.mult, ALU.add)
                            add.then_inc(ye_added, 1)
                    if t == RCP[s] and prev:
                        inverse(*prev)
                    if t == NORM[s] and prev:
                        divide(*prev)
                if finds_maxima(i, u):
                    row_maxima(PER_HEAD * (h + 1), s, NC * (h + 1) + s + 1)

            dve.wait_ge(x1_spill, 16 * NC)
            dve.wait_ge(acc_init, NT // 2)
            slots_of_loop(slot, dve)
            inverse(H // 2 - 1, 1, NC - 1)
            divide(H // 2 - 1, 1, NC - 1)
            dve.wait_ge(ye_added, NC * H)
            for q in range(NT // 4):
                for r in range(2):
                    wait(dve, fin_th, 2 * q + r + 1)
                    wait(dve, fin_x, 2 * q)
                    dve.scalar_tensor_tensor(GT[:, r, :], TH[:, r, :], 1.0,
                                             ACC[:, ds(4 * q + 2 * r, 2), :].rearrange("p t d -> p (t d)"),
                                             ALU.add, ALU.mult).then_inc(fin_a, 1)
                    wait(dve, fin_a, 2 * q + r + 1)
                    wait(dve, fin_ps, 2 * q + r + 1)
                    dve.scalar_tensor_tensor(GT[:, r, :], PS[2 + r][:, :], 0.5, GT[:, r, :], ALU.mult, ALU.mult)\
                        .then_inc(fin_b, 1)

        @block.tensor
        def _(pe):
            mm = pe.matmul

            def transposes(c, k0):
                pe.wait_ge(xn, TC * (k0 + c) + TC)
                for k in range(KK):
                    for t in range(TC):
                        last = pe.transpose(PS[k][:, P * t:P * t + P],
                                            XN[:, t, P * k:P * k + P],
                                            IDN[:, :])
                    last.then_inc(xt_ps, 1)

            def pairs(out, weight, data, weight_first, last=True, first=True):
                for k in range(KK):
                    for j, (wp, dp) in enumerate(((0, 0), (1, 0), (0, 1))):
                        w, d = weight[wp](k), data[dp](k)
                        done = mm(out, w if weight_first else d, d if weight_first else w,
                                  start=first and k == 0 and j == 0, stop=last and k == KK - 1 and j == 2)
                return done

            def x_cols(c):
                return [lambda k: XTH[:, k, ds(CH * c, CH)], lambda k: XTL[:, k, ds(CH * c, CH)]]

            def x_tile(c, t):
                return [lambda k: XTH[:, k, ds(CH * c + P * t, P)], lambda k: XTL[:, k, ds(CH * c + P * t, P)]]

            def front(c):
                wait(pe, xth, KK * c + KK)
                wait(pe, xtl, KK * c + KK)
                for t, m in enumerate((2, 3, 4, 5, 0, 1)):
                    if t < 2:
                        wait(pe, relus, 4 * c)
                    elif t < 4:
                        wait(pe, v_read, 2 * c)
                    else:
                        wait(pe, relus, 4 * c + t - 3)
                    cols = slice(P * m, P * m + P)
                    pairs(PS[2 + t % 4][:, :], [lambda k: W0H[:, k, cols], lambda k: W0L[:, k, cols]],
                          x_cols(c), True).then_inc(proj, 1)

            def back(c):
                for r in range(2):
                    if c:
                        wait(pe, gate_mid, 2 * c - 1 + r)
                    for q in range(2):
                        mm(PS[6 + r][:, D * q:D * q + D], ONE1[0:1, 0, :], BROW[0:1, 0, :], start=True, stop=False)
                        last = pairs(PS[6 + r][:, D * q:D * q + D], [lambda k: FH[:, k, :], lambda k: FL[:, k, :]],
                                     x_tile(c, 2 * r + q), False, first=False)
                    last.then_inc(z_ps, 1)
                if c + 2 < NC:
                    transposes(c + 2, 0)
                if c == NC - 1:
                    transposes(0, NC)
                for r in range(2):
                    wait(pe, z_read, 2 * c + r + 1)
                    wait(pe, outT, 2 * c + 2)
                    for q in range(2):
                        for k in range(KK):
                            last = mm(PS[6 + r][:, D * q:D * q + D], OT0[:, k, P * (2 * r + q):P * (2 * r + q) + P],
                                      WO0[:, k, :], start=k == 0, stop=k == KK - 1)
                    last.then_inc(s_ps, 1)

            pe.wait_ge(const_in, 32)
            transposes(0, 0)
            pe.wait_ge(w0l, 1)
            front(0)
            transposes(1, 0)
            pe.wait_ge(ffn_q, 6)
            for k in range(KK):
                for o in range(KK):
                    last = pe.transpose(PS[6 + k][:, P * o:P * o + P], QF[:, o, P * k:P * k + P], IDN[:, :])
                last.then_inc(ffn_t, 1)
            pe.wait_ge(small_in, 16 * 11)
            pe.wait_ge(ffn_split, 2)
            pe.wait_ge(w_out_in, 16)
            pe.wait_ge(memset_done, 10)
            for c in range(NC - 1):
                front(c + 1)
                back(c)
            back(NC - 1)

            pe.wait_ge(wq1l, 2)
            pe.wait_ge(gate_mid, 2 * NC)
            pe.wait_ge(relus, 4 * NC)
            for c in range(NC):
                pe.wait_ge(xth, KK * (NC + c) + KK)
                pe.wait_ge(xtl, KK * (NC + c) + KK)
                wait(pe, v_copied, 2 * c)
                for t in range(TC):
                    last = mm(PS[7][:, E * t:E * t + E], ONE1[0:1, 1, :], GBR[0:1, :], start=True, stop=False)
                    last = pairs(PS[7][:, E * t:E * t + E], [lambda k: GWH[:, k, :], lambda k: GWL[:, k, :]],
                                 x_tile(c, t), False, first=False)
                last.then_inc(lg_ps, 1)
                for m in range(4):
                    wait(pe, qk_v, 4 * c)
                    cols = slice(P * m, P * m + P)
                    pairs(PS[2 + m][:, :], [lambda k: WQH[:, k, cols], lambda k: WQL[:, k, cols]],
                          x_cols(c), True).then_inc(qk_ps, 1)
                if c + 1 < NC:
                    transposes(c + 1, NC)
                cols = slice(2 * D, 3 * D)
                for r in range(2):
                    if r:
                        wait(pe, lg_copied, c + 1)
                    for q in range(2):
                        mm(PS[6 + r][:, D * q:D * q + D], ONE1[0:1, 1, :], BROW[0:1, 1, :], start=True, stop=False)
                        last = pairs(PS[6 + r][:, D * q:D * q + D], [lambda k: WQH[:, k, cols], lambda k: WQL[:, k, cols]],
                                     x_tile(c, 2 * r + q), False, first=False)
                    last.then_inc(v_ps, 1)

            def turn_routing(c):
                pe.wait_ge(we_done, 1)
                if c >= 2:
                    pe.wait_ge(wet_copied, c - 1)
                for t in range(TC):
                    last = pe.transpose(PS[4 + c % 2][0:E, P * t:P * t + P], WE[:, TC * c + t, :], IDN[:, :])
                last.then_inc(wet_ps, 1)

            def output_biases(r):
                if r == 0:
                    pe.wait_ge(wet_copied, NC)
                if r >= 2:
                    pe.wait_ge(acc_init, r - 1)
                for q in range(2):
                    tile = 2 * r + q
                    last = mm(PS[4 + r % 2][:, D * q:D * q + D], WET[:, P * tile:P * tile + P], B2[:, :],
                              start=True, stop=True)
                last.then_inc(b2_ps, 1)

            def score_a(h40, par, tile, banks=2):
                c, k = place(tile)
                a = ORDER[c]
                xq, gg = k // (a + 1), k % (a + 1)
                width = CH if gg < a else P * (xq + 1)
                idx = h40 + tile
                if not (isinstance(idx, int) and idx < banks):
                    pe.wait_ge(a_reduced, idx + 1 - banks)
                bank = PS[tile % banks]
                last = mm(bank[:, 0:width], OPS[0:ROWS_A, par, 0, P * (TC * a + xq):P * (TC * a + xq) + P],
                          OPS[0:ROWS_A, par, 1, CH * gg:CH * gg + width], start=True, stop=gg < a)
                if gg == a:
                    last = mm(bank[:, P * xq:P * xq + P], MASK[:, 0, :], MASK[:, 2, :], start=False, stop=True)
                last.then_inc(a_scored, 1)

            def turn_maxima(par, k):
                pe.wait_ge(max_part, 5 * k)
                pe.transpose(MTP, NP[:, par, :, :].rearrange("p j q -> p (j q)"), MASK[:, 2, :]).then_inc(mt_ps, 1)

            pe.wait_ge(cast_in, 32)
            pe.wait_ge(opa_in[0], 16 * 6)
            pe.wait_ge(opa_rows, 2)
            side_work = [(turn_routing, c) for c in range(NC)] + [(output_biases, r) for r in range(NT // 2)]
            for s in range(NC):
                for k in range(TILES[s]):
                    tile = OFF[s] + k
                    score_a(0, 0, tile, 4)
                    if tile % 2 and tile // 2 < len(side_work):
                        stage, which = side_work[tile // 2]
                        stage(which)
                if s:
                    if s >= 2:
                        pe.wait_ge(mt_copied, s - 1)
                    turn_maxima((s - 1) % 2, s)
            pe.wait_ge(mt_copied, NC - 1)
            turn_maxima((NC - 1) % 2, NC)

            def score_b(h, u, tile):
                c, k = place(tile)
                b = ORDER[c]
                off = P * max(0, k - TC * b)
                idx = PER_HEAD * h + tile
                if not (isinstance(idx, int) and idx < 2):
                    pe.wait_ge(b_exped, idx - 1)
                if k == 0:
                    pe.wait_ge(mrow[c], 16 * h + 16)
                bank = PS[2 + tile % 2]
                last = mm(bank[:, off:CH], OPS[0:ROWS_B, 2 + u, 1, P * k:P * k + P],
                          OPS[0:ROWS_B, 2 + u, 0, CH * b + off:CH * b + CH], start=True, stop=k < TC * b)
                if k >= TC * b:
                    last = mm(bank[:, off:off + P], MASK[:, 1, :], MASK[:, 2, :], start=False, stop=True)
                last.then_inc(b_scored, 1)

            def value(h, u, tile):
                c, k = place(tile)
                b = ORDER[c]
                off = P * max(0, k - TC * b)
                idx = PER_HEAD * h + tile
                if k == 0:
                    if not (isinstance(idx, int) and idx == 0):
                        pe.wait_ge(u_ready, NC * h + c)
                    if b == 0:
                        mm(PS[4][:, :], ZERO[:, :], ONEB[:, :], start=True, stop=True, skip_group_check=True)
                pe.wait_ge(b_exped, idx + 1)
                quad = 32 * (k % TC)
                mm(PS[4][quad:quad + 32, off:CH], VS[:, u, k, :], PR[:, tile % RING, off:CH],
                   start=b > 0 and k < TC, stop=k >= TC * b, skip_group_check=True, tile_position=(0, quad))\
                    .then_inc(pv_done, 1)

            def heads_out(s):
                for q in range(TC):
                    last = mm(PS[7][:, (HD + 1) * q:(HD + 1) * q + HD + 1], U[:, s % 2, P * q:P * q + P], SEL[:, :],
                              start=True, stop=True)
                last.then_inc(o_ps, 1)

            def bank7_read(i, u, s, t):
                n = NC * (2 * i + u) + s
                kind, m, number = last_in_bank7(s, t, n)
                if kind == "fill":
                    q = s if m is n else (s - 1) % NC
                    pe.wait_ge(ye_added, m - q + sum(len(FILLS[r]) for r in range(q)) + number)
                elif kind == "outputs":
                    pe.wait_ge(o_normed, m)
                elif kind == "maxima":
                    pe.wait_ge(mt_copied, m + NC)

            def slot(i, u, s):
                h = 2 * i + u
                prev = prev_of(i, u, s)
                if s == 0:
                    if finds_maxima(i, u):
                        pe.wait_ge(opa_in[1 - u], 16 * 6 * (i + 1 + u))
                        pe.wait_ge(opa_rows, 2 * h + 4)
                    pe.wait_ge(opb_in[u], 16 * (i + 1))
                    pe.wait_ge(vs_ready, h + 1)
                    pe.wait_ge(w1l_done, i + 1)
                for t in range(STEPS):
                    if finds_maxima(i, u):
                        for tile in tiles_at(s, t):
                            score_a(PER_HEAD * (h + 1), 1 - u, tile)
                    for tile in tiles_at(s, t, steps_b(s)):
                        score_b(h, u, tile)
                        for n in values_after(tile):
                            value(h, u, n)
                    if s == NC - 1 and t == STEPS - 2:
                        for k in range(PER_HEAD - LAG, PER_HEAD - 1):
                            value(h, u, k)
                    if s == NC - 1 and t == STEPS - 1:
                        value(h, u, PER_HEAD - 1)
                    if t == MAXT[s] and prev and finds_maxima(*prev[:2]):
                        bank7_read(i, u, s, t)
                        turn_maxima(prev[2] % 2, NC * h + s + NC)
                    if t == HEADS[s] and prev:
                        pe.wait_ge(u_ready, NC * h + s)
                        bank7_read(i, u, s, t)
                        heads_out(prev[2])
                    for unit, f, _, t_g, t_l, rate, _, _, _ in UNITS[s]:
                        m = NC * h + unit
                        for part, start in ((0, t_g), (1, t_l)):
                            for j in range(max(0, rate * (t - start)), max(0, min(6, rate * (t - start + 1)))):
                                if j == 0 and not (isinstance(m, int) and m == 0):
                                    pe.wait_ge(y_ready if part else gate_read, m)
                                k, (wp, dp) = j // 3, ((0, 0), (1, 0), (0, 1))[j % 3]
                                col = ((part * 2 + f) * KK + k) * P
                                last = mm(PS[5 + part][:, :], (W1L if wp else W1H)[:, ds(1024 * i + col, P)],
                                          (XTL if dp else XTH)[:, k, CH * (2 * u + unit // 2):CH * (2 * u + unit // 2) + CH],
                                          start=j == 0, stop=j == 5)
                                if j == 5:
                                    last.then_inc(up_ps, 1)
                    for fill, buf, pair, t_f, _ in FILLS[s]:
                        if t == t_f:
                            pe.wait_ge(y_ready, NC * h + 2 * buf + 2)
                            bank7_read(i, u, s, t)
                            for q in range(2):
                                for f in range(KK):
                                    tok = P * (2 * pair + q)
                                    last = mm(PS[7][:, D * q:D * q + D], YT[:, buf, f, tok:tok + P],
                                              W2[:, ds(i, 1), f, :].rearrange("p a d -> p (a d)"),
                                              start=f == 0, stop=f == KK - 1)
                            last.then_inc(ye_ps, 1)

            pe.wait_ge(acc_init, NT // 2)
            pe.wait_ge(w2_in, 16)
            pe.wait_ge(mt_copied, NC)
            slots_of_loop(slot, pe)
            pe.wait_ge(u_ready, NC * H)
            pe.wait_ge(ye_added, NC * H)
            heads_out(NC - 1)
            pe.wait_ge(o_normed, NC * H)
            for n in range(NT // 2):
                r, q = n % 2, n // 2
                pe.wait_ge(ot_copied, max(0, n - 1))
                for k in range(KK):
                    for t in range(2):
                        last = pe.transpose(PS[r][:, P * (2 * k + t):P * (2 * k + t) + P],
                                            XO[:, 2 * n + t, P * k:P * k + P], IDN[:, :])
                last.then_inc(ot_ps, 1)
                pe.wait_ge(fin_b, max(0, n - 1))
                pe.wait_ge(ot_copied, n + 1)
                for t in range(2):
                    o = PS[2 + r][:, D * t:D * t + D]
                    mm(o, ONE1[0:1, 0, :], BROW[0:1, 2, :], start=True, stop=False)
                    for k in range(KK):
                        last = mm(o, TQ[:, r, P * (2 * k + t):P * (2 * k + t) + P], WO1[:, k, :],
                                  start=False, stop=k == KK - 1)
                last.then_inc(fin_ps, 1)


def _rows(w):
    import numpy as np
    return np.ascontiguousarray(w.reshape(w.shape[0] // P, P, *w.shape[1:]).swapaxes(0, 1))


def _shape_constants():
    import numpy as np
    q, k = np.arange(P)[:, None], np.arange(P)[None, :]
    far = -float(2 ** 30)
    masks = np.stack([np.where(q > k, far, 0.0),
                      np.where(q < k, far, 0.0),
                      np.eye(P)], 1)
    pos = np.arange(S)
    high, low, one = pos // P * P, pos % P, np.ones(S)
    side_q = [one, -high, one, -low] * 3
    side_k = [high, one, low, one] * 3
    pos_rows = np.stack([side_q, side_k], 1).reshape(POS, 2, S)
    pick = np.zeros((POS, 2, 4), np.float32)
    for r in range(POS):
        pick[r, 0, r // 4 if r % 2 == 0 else 3] = 1
        pick[r, 1, r // 4 if r % 2 == 1 else 3] = 1
    sel = np.zeros((P, HD + 1), np.float32)
    for p in range(P):
        if p % 32 <= HD:
            sel[p, p % 32] = 1
    return pos_rows.astype(np.float32), pick, masks.astype(np.float32), np.eye(P, dtype=np.float32), sel


def kernel(L0_attn_x, L0_attn_W_qkv, L0_attn_W_out, L0_ffn_weight, L0_ffn_bias, L1_attn_qkv_w, L1_attn_qkv_b,
           L1_attn_out_w, L1_attn_out_b, L1_attn_alibi_slopes, L1_ffn_gate_w, L1_ffn_gate_b, L1_ffn_w1, L1_ffn_b1,
           L1_ffn_w2, L1_ffn_b2):
    import numpy as np
    import concourse.bacc as bacc
    from concourse.bass_utils import run_bass_kernel_spmd

    a = [np.asarray(v) for v in (L0_attn_x, L0_attn_W_qkv, L0_attn_W_out, L0_ffn_weight, L0_ffn_bias, L1_attn_qkv_w,
                                 L1_attn_qkv_b, L1_attn_out_w, L1_attn_out_b, L1_attn_alibi_slopes, L1_ffn_gate_w,
                                 L1_ffn_gate_b, L1_ffn_w1, L1_ffn_b1, L1_ffn_w2, L1_ffn_b2)]
    x, wqkv0, wout0, wf, bf, wqkv1, bqkv1, wout1, bout1, slopes, gw, gb, w1, b1, w2, b2 = a
    pos_rows, pick, masks, ident, sel = _shape_constants()
    w1v = w1.reshape(E, 2, P, 2, KK, P).transpose(5, 0, 3, 1, 4, 2).reshape(P, E * 1024)
    b1v = b1.reshape(E, 2, P, 2).transpose(2, 0, 3, 1)
    w2v = w2.reshape(E, D, KK, P).transpose(3, 0, 2, 1)
    arrays = dict(
        x=x, w_qkv0=_rows(wqkv0.T), w_out0=_rows(wout0.T), w_ffn=_rows(wf), b_ffn=bf[None],
        w_qkv1=_rows(wqkv1.T), b_qk1=bqkv1[:2 * D].reshape(4, P).T, b_v1=bqkv1[None, 2 * D:], w_out1=_rows(wout1.T),
        b_out1=bout1[None], slopes=slopes[None], pos_rows=pos_rows, pick=pick, masks=masks, ident=ident, sel=sel,
        gate_w=_rows(gw.T), gate_b=gb[None], w1=w1v, b1=b1v, w2=w2v, b2=b2)
    nc = bacc.Bacc("TRN2", target_bir_lowering=False, num_devices=1)
    ins, feed = {}, {}
    for name, v in arrays.items():
        v = np.ascontiguousarray(v)
        feed["in_" + name] = v
        ins[name] = nc.dram_tensor("in_" + name, v.shape, mybir.dt.from_np(v.dtype), kind="ExternalInput").ap()
    out = nc.dram_tensor("out_rows", (1, S, D), F32, kind="ExternalOutput").ap()
    build(nc, out=out, **ins)
    return run_bass_kernel_spmd(nc, [feed], core_ids=[0]).results[0]["out_rows"]
```

```python
from contextlib import ExitStack

import concourse.bass as bass
from concourse import mybir

F32, F16, BF16 = mybir.dt.float32, mybir.dt.float16, mybir.dt.bfloat16
ALU = mybir.AluOpType
ACT = mybir.ActivationFunctionType
AX = mybir.AxisListType

P = 128
S, D = 2048, 256
H, HD = 16, 16
KK = D // P
NT = S // P
CH = 512
NC = S // CH
TC = CH // P
E, I = 8, 256
WS = 16.0
LN_EPS = 1e-5
L0_EPS = 1e-9

POS = 12
LOADS = (((0, 1, 3), (1, 1, 2), (2, 1, 1)), ((0, 3, 1), (0, 2, 1), (0, 1, 1)))
ROWS_A = POS + 6 * HD
ROWS_B = ROWS_A + 3

ORDER = (0, 3, 1, 2)
TILES = [TC * (a + 1) for a in ORDER]
OFF = [sum(TILES[:s]) for s in range(NC)]
PER_HEAD = sum(TILES)
PER_SLOT = PER_HEAD // NC
RING = 5
LAG = 3
STEPS = 16

UNITS = (((0, 0, 0, 1, 6, 2, 5, 7, 9), (1, 1, 0, 9, 13, 2, 12, 14, 15)),
         ((2, 0, 1, 1, 7, 1, 6, 9, 13),),
         ((3, 1, 1, 0, 7, 1, 8, 9, 13),),
         ())
FILLS = ((),
         ((0, 0, 0, 14, 15),),
         ((1, 0, 1, 13, 14),),
         ((2, 1, 0, 2, 3), (3, 1, 1, 14, 15)))
MAXT, MAXC = (7, 5, 6, 7), (8, 6, 7, 8)
HEADS, RCP, NORM = (10, 9, 10, 11), (11, 10, 11, 12), (12, 11, 12, 13)
FIRST_FILLS = (24, 26, 31, 34)
PAIRS = [2 * c + r for c in ORDER for r in range(2)]
ENDS = ((), (), ((0, 1, 2, 3, 4, 6), (1, 7, 8, 9, 10, 12)), ((2, 1, 2, 3, 4, 6), (3, 7, 8, 9, 10, 12)))


def share(n, t, steps):
    return range(min(n, n * t // steps), min(n, n * (t + 1) // steps))


def tiles_at(s, t, steps=STEPS):
    return [PER_SLOT * s + k for k in share(PER_SLOT, t, steps)]


def last_in_bank7(s, t, n):
    for back in range(2):
        slot, m, until = (s - back) % NC, n - back if back else n, STEPS if back else t
        known = isinstance(m, int)
        uses = []
        if not known or 0 <= m < NC * (H - 1):
            uses += [(f[3], "fill", k + 1) for k, f in enumerate(FILLS[slot])]
        if not known or 0 <= m <= NC * (H - 1):
            uses.append((MAXT[slot], "maxima", 0))
        if not known or m > 0:
            uses.append((HEADS[slot], "outputs", 0))
        uses = [use for use in uses if use[0] < until]
        if uses:
            return max(uses)[1], m, max(uses)[2]
    return None, 0, 0


def steps_b(s):
    return STEPS - 2 if s == NC - 1 else STEPS


def lag_of(h):
    return LAG + 1 if isinstance(h, int) and h == H - 1 else LAG


def values_after(tile, lag):
    n = tile - lag
    if n < 0 or n in OFF[1:]:
        return []
    return [n - 1, n] if n - 1 in OFF[1:] else [n]


def place(n):
    c = max(c for c in range(NC) if OFF[c] <= n)
    return c, n - OFF[c]


def ds(start, size):
    return bass.ds(start, size)


def build(nc, x, w_qkv0, w_out0, w_ffn, b_ffn, w_qkv1, b_qk1, b_v1, w_out1, b_out1, slopes, pos_rows, pick,
          masks, ident, sel, gate_w, gate_b, w1, b1, w2, b2, out):
    ctx = ExitStack()
    with ctx:
        def sb(name, shape, dt=F32):
            return ctx.enter_context(nc.sbuf_tensor(name, shape, dt))

        def sem(name):
            return ctx.enter_context(nc.semaphore(name))

        XO = sb("XO", [P, NT, D])
        ACC = sb("ACC", [P, NT, D])
        XTH = sb("XTH", [P, KK, S], F16)
        XTL = sb("XTL", [P, KK, S], F16)
        W1H = sb("W1H", [P, E * 1024], F16)
        W1L = sb("W1L", [P, E * 1024], F16)
        W2 = sb("W2", [P, E, KK, D])
        VV = sb("VV", [P, NT, D])
        OPS = sb("OPS", [P, 4, 2, S], BF16)
        PR = sb("PR", [P, RING, CH])
        YT = sb("YT", [P, 2, KK, CH])
        U = sb("U", [P, 2, CH])
        VS = sb("VS", [P, 2, NT, 32])
        STG = sb("STG", [P, 2048])
        WO1 = sb("WO1", [P, KK, D])
        POSR = sb("POSR", [POS, 2, S], BF16)
        PICK = sb("PICK", [POS, 2, 4])
        SLB = sb("SLB", [POS, H])
        SLR = sb("SLR", [POS, H])
        SLP = sb("SLP", [POS, 3, H], BF16)
        SCL = sb("SCL", [POS, 2, H])
        MASK = sb("MASK", [P, 3, P], BF16)
        IDN = sb("IDN", [P, P])
        SEL = sb("SEL", [P, HD + 1])
        MV = sb("MV", [P, NT, 2])
        BST = sb("BST", [P, TC, 6])
        RSTD = sb("RSTD", [P, NT])
        VEPS = sb("VEPS", [P, NT])
        HALF = sb("HALF", [P, NT])
        ONE1 = sb("ONE1", [1, 2, P])
        ONES = sb("ONES", [P, 1])
        ZERO = sb("ZERO", [P, P], BF16)
        NIL = sb("NIL", [P, 1])
        ONEB = sb("ONEB", [P, CH], BF16)
        BROW = sb("BROW", [1, 3 * D + E])
        BQK = sb("BQK", [P, 4])
        CAR = sb("CAR", [P, 4, 1])
        TH = sb("TH", [P, 2, CH])
        GT = sb("GT", [P, 2, CH])
        PM = sb("PM", [P, 2, TC, NC])
        NM = sb("NM", [P, 2, TC])
        NR = sb("NR", [P, 2, 2, TC])
        NP = sb("NP", [P, 2, 3, TC], BF16)
        MT = sb("MT", [12, 2, P], BF16)
        RC = sb("RC", [P, 2, TC])
        GW = sb("GW", [P, KK, E])
        LG = sb("LG", [P, NT, E])
        TOP = sb("TOP", [P, 4, NT])
        WE = sb("WE", [P, NT, E])
        WES = sb("WES", [P, NT, E])
        B1 = sb("B1", [P, E, 2, 2])
        B1S = sb("B1S", [P, E, 2, 2])
        B1T = sb("B1T", [P, E, 2])

        ops32 = OPS[:, :, :, :].rearrange("p a b s -> p (a b s)").bitcast(F32)
        EX = ops32[:, 0:2048].rearrange("p (m n) -> p m n", m=4)
        RE = ops32[:, 2048:4096].rearrange("p (m n) -> p m n", m=4)
        PH = ops32[:, 4096:6144].rearrange("p (m n) -> p m n", m=4)
        KV = ops32[:, 6144:7168].rearrange("p (m n) -> p m n", m=2)
        KC = ops32[:, 7168:8192].rearrange("p (m n) -> p m n", m=2)
        pr32 = PR[:, :, :].rearrange("p r n -> p (r n)")
        NUM = pr32[:, 0:1024].rearrange("p (m n) -> p m n", m=2)
        DEN = pr32[:, 1024:2048].rearrange("p (m n) -> p m n", m=2)
        yt32 = YT[:, :, :, :].rearrange("p a b n -> p (a b n)")
        w2flat = W2[:, :, :, :].rearrange("p e f d -> p (e f d)")
        WQG = 3 * D + E
        WQH = w2flat[:, 0:WQG].bitcast(F16).rearrange("p (k n) -> p k n", k=KK)
        RT = U[:, :, :].rearrange("p a n -> p (a n)")[:, 0:512].rearrange("p (a t e) -> p a t e", a=4, t=NT)
        WQL = w2flat[:, WQG:2 * WQG].bitcast(F16).rearrange("p (k n) -> p k n", k=KK)
        WET = pr32[:, 0:S]
        B2 = pr32[:, S:S + D]
        TQ = YT[:, 0]
        KVC = YT[:, 0]
        XN = ACC[:, 0:TC, :]
        OT0 = YT[:, 1]
        vv32 = VV[:, :, :].rearrange("p a b -> p (a b)")
        W0H = vv32[:, 0:768].bitcast(F16).rearrange("p (k n) -> p k n", k=KK)
        W0L = vv32[:, 768:1536].bitcast(F16).rearrange("p (k n) -> p k n", k=KK)
        FH = vv32[:, 1536:1792].bitcast(F16).rearrange("p (k n) -> p k n", k=KK)
        FL = vv32[:, 1792:2048].bitcast(F16).rearrange("p (k n) -> p k n", k=KK)
        WO0 = vv32[:, 2048:2560].rearrange("p (k n) -> p k n", k=KK)
        WF = vv32[:, 2560:3072].rearrange("p (k n) -> p k n", k=KK)
        QF = vv32[:, 3072:3584].rearrange("p (k n) -> p k n", k=KK)
        NF = vv32[:, 3584:4096].rearrange("p (k n) -> p k n", k=KK)
        RAW = [W1H[:, (E - 2) * 1024:].bitcast(F32), W1L[:, (E - 2) * 1024:].bitcast(F32)]
        STG3 = STG[:, 0:KK * 3 * D].rearrange("p (k n) -> p k n", k=KK)
        RAW_LAST = [STG[:, 0:1024], STG[:, 1024:2048]]
        QV = ops32[:, 0:2048].rearrange("p (m n) -> p m n", m=4)
        QR = ops32[:, 2048:4096].rearrange("p (m n) -> p m n", m=4)
        QP = ops32[:, 4096:7168].bitcast(BF16).rearrange("p (m j n) -> p m j n", m=4, j=3)

        parts = nc.dram_tensor("qk_parts", (2, 3, D, S), BF16, kind="Internal").ap()
        x1_dram = nc.dram_tensor("x1_rows", (P, NT, D), F32, kind="Internal").ap()

        PS = [ctx.enter_context(nc.psum_tensor(f"bank{i}", [P, CH], F32)) for i in range(8)]
        MTP = PS[7][0:3 * TC, 256:256 + P // 2].bitcast(BF16)

        w_in0, cast_in, w_ffn_in, w_out_in, w_q1_in = (
            sem("w_in0"), sem("cast_in"), sem("w_ffn_in"), sem("w_out_in"), sem("w_q1_in"))
        small_in, const_in, w2_in, memset_done, w0h = (
            sem("small_in"), sem("const_in"), sem("w2_in"), sem("memset_done"), sem("w0h"))
        w0l, ffn_thr, ffn_q, ffn_t, ffn_h = (
            sem("w0l"), sem("ffn_thr"), sem("ffn_q"), sem("ffn_t"), sem("ffn_h"))
        ffn_split, w1_scaled, w1h_done, w1l_done, wq1h, wq1l = (
            sem("ffn_split"), sem("w1_scaled"), sem("w1h_done"), sem("w1l_done"), sem("wq1h"), sem("wq1l"))
        stats, var_eps, rstd_done, xn, xt_ps = (
            sem("stats"), sem("var_eps"), sem("rstd_done"), sem("xn"), sem("xt_ps"))
        xth, xtl, proj, negs, relus = (
            sem("xth"), sem("xtl"), sem("proj"), sem("negs"), sem("relus"))
        phi_k, phi_q, scan_k, v_read, scan_kv = (
            sem("phi_k"), sem("phi_q"), sem("scan_k"), sem("v_read"), sem("scan_kv"))
        nd, nd2, numden, rcp, outT = (
            sem("nd"), sem("nd2"), sem("numden"), sem("rcp"), sem("outT"))
        z_ps, s_ps, z_read, gate_a, gate_mid = (
            sem("z_ps"), sem("s_ps"), sem("z_read"), sem("gate_a"), sem("gate_mid"))
        x1_add, x1_spill, qk_ps, qk_v, qk_p0 = (
            sem("x1_add"), sem("x1_spill"), sem("qk_ps"), sem("qk_v"), sem("qk_p0"))
        qk_r1, qk_p1, qk_p2, v_ps = (
            sem("qk_r1"), sem("qk_p1"), sem("qk_p2"), sem("v_ps"))
        v_copied, lg_copied, gsplit, route = (
            sem("v_copied"), sem("lg_copied"), sem("gsplit"), sem("route"))
        expd, rstep, ones_rows, we_done, wet_ps = (
            sem("expd"), sem("rstep"), sem("ones_rows"), sem("we_done"), sem("wet_ps"))
        wet_copied, b2_ps, acc_init, b1_prep, slope_part = (
            sem("wet_copied"), sem("b2_ps"), sem("acc_init"), sem("b1_prep"), sem("slope_part"))
        scl, opa_rows, vs_ready, a_scored, a_reduced = (
            sem("scl"), sem("opa_rows"), sem("vs_ready"), sem("a_scored"), sem("a_reduced"))
        row_max, max_part, mt_ps, mt_copied, b_scored = (
            sem("row_max"), sem("max_part"), sem("mt_ps"), sem("mt_copied"), sem("b_scored"))
        b_exped, pv_done, u_ready, o_ps, o_rc = (
            sem("b_exped"), sem("pv_done"), sem("u_ready"), sem("o_ps"), sem("o_rc"))
        o_normed, up_ps, glu_done, gate_read = (
            sem("o_normed"), sem("up_ps"), sem("glu_done"), sem("gate_read"))
        y_ready, ye_ps, ye_added, carry, ot_ps = (
            sem("y_ready"), sem("ye_ps"), sem("ye_added"), sem("carry"), sem("ot_ps"))
        ot_copied, fin_ps, fin_th, fin_a, fin_b = (
            sem("ot_copied"), sem("fin_ps"), sem("fin_th"), sem("fin_a"), sem("fin_b"))
        fin_x, x1_in, out_st = (
            sem("fin_x"), sem("x1_in"), sem("out_st"))
        opa_in = [sem("opa_in0"), sem("opa_in1")]
        b2_zero, wet_zero = sem("b2_zero"), sem("wet_zero")
        parts_out = [sem(f"parts_out{m}") for m in range(4)]
        raw_in = [sem("raw_in0"), sem("raw_in1")]
        last_in = [sem("last_in0"), sem("last_in1")]
        opb_in = [sem("opb_in0"), sem("opb_in1")]
        mrow = [sem(f"mrow{s}") for s in range(NC)]
        x_in = [sem(f"x_in{c}") for c in range(NC)]

        block = ctx.enter_context(nc.Block())

        def wait(eng, semaphore, count):
            if not (isinstance(count, int) and count <= 0):
                eng.wait_ge(semaphore, count)

        def raw_of(e):
            return (RAW_LAST if e >= E - 2 else RAW)[e % 2]

        def slots_of_loop(run, eng):
            def fresh(value, least):
                return eng.snap(eng.to_reg(value), min_val=least, max_val=H // 2 - 2 + least)

            run(0, 0, 0)
            with eng.Fori(0, H // 2 - 1) as i:
                for u in range(2):
                    for s in range(NC):
                        if (u, s) != (0, 0):
                            run(fresh(i, 0), u, s)
                run(fresh(i + 1, 1), 0, 0)
            for u in range(2):
                for s in range(NC):
                    if (u, s) != (0, 0):
                        run(H // 2 - 1, u, s)

        def prev_of(i, u, s):
            if s:
                return i, u, s - 1
            if u:
                return i, 0, NC - 1
            if isinstance(i, int) and i == 0:
                return None
            return i - 1, 1, NC - 1

        def maxima_before(i, u, s):
            return s == 0 or finds_maxima(i, u)

        def ends_at(i, u, s, which, t):
            return [] if finds_maxima(i, u) else [end[0] for end in ENDS[s] if end[which] == t]

        def end_banks(n):
            return (PS[0], PS[1]) if n > 4 and n % 2 else (PS[5], PS[6])

        def banks_before(n):
            return n if n < 5 else n - 1 if n > 5 else 0

        def b_bank(h, tile):
            return PS[2 + tile % 2] if lag_of(h) == LAG else PS[(2 + tile) % 4]

        def expert_turn(i, u):
            return (i + 1, 0) if u else (i, 1)

        def finds_maxima(i, u):
            return not (isinstance(i, int) and 2 * i + u == H - 1)

        @block.sync
        def _(sp):
            def fetch_experts(q):
                for half in range(2):
                    e = 2 * q + half
                    sp.dma_start(raw_of(e), w1[:, 1024 * e:1024 * e + 1024]).then_inc(
                        (last_in if e >= E - 2 else raw_in)[half], 16)

            for c in range(NC):
                sp.dma_start(XO[:, TC * c:TC * c + TC, :],
                             x[0].rearrange("(t p) d -> p t d", p=P)[:, TC * c:TC * c + TC, :]).then_inc(x_in[c], 16)
            fetch_experts(0)
            sp.wait_ge(w0l, 1)
            sp.dma_start(STG[:, 0:1536], w_qkv1.rearrange("p k n -> p (k n)")).then_inc(w_q1_in, 16)
            for c in range(NC):
                if c + 2 < E // 2:
                    sp.wait_ge(w1l_done, 2 * c + 2)
                    fetch_experts(c + 1)
                if c == 1:
                    sp.wait_ge(wq1l, 1)
                    fetch_experts(E // 2 - 1)
                sp.wait_ge(x1_add, 2 * c + 2)
                sp.dma_start(x1_dram[:, TC * c:TC * c + TC, :], XO[:, TC * c:TC * c + TC, :]).then_inc(x1_spill, 16)
            with sp.Fori(0, NC) as c:
                for m in range(4):
                    side, half = m // 2, m % 2
                    sp.wait_ge(qk_p2, 4 * c + m + 1)
                    sp.dma_start(parts[side, :, half * P:half * P + P, ds(c * CH, CH)].rearrange("j f t -> f j t"),
                                 QP[:, m, :, :]).then_inc(parts_out[m], 16)

            def load_a(h, par):
                for side in range(2):
                    row = POS
                    for first, parts_of, times_of in LOADS[side]:
                        rows = HD * parts_of * times_of
                        src = parts[side, first:first + parts_of, ds(HD * h, HD), :]
                        if times_of > 1:
                            src = src.broadcast_to([times_of, HD, S])
                        sp.dma_start(OPS[row:row + rows, par, side, :], src).then_inc(opa_in[par], 16)
                        row += rows

            def copy_b(h, par, times):
                sp.wait_ge(opa_in[par], 16 * 6 * times)
                sp.wait_ge(ones_rows, 2)
                sp.wait_ge(opa_rows, 2 * h + 2)
                sp.dma_start(OPS[0:ROWS_A, 2 + par, :, :], OPS[0:ROWS_A, par, :, :]).then_inc(opb_in[par], 16)

            def rows_out(par, s, k):
                sp.wait_ge(mt_copied, k)
                a = ORDER[s]
                sp.dma_start(OPS[ROWS_A:ROWS_B, 2 + par, 0, CH * a:CH * a + CH].rearrange("j (q t) -> j q t", q=TC),
                             MT[:, s % 2, :]).then_inc(mrow[s], 16)

            sp.wait_ge(v_ps, NT)
            sp.dma_start(W2[:, :, :, :], w2).then_inc(w2_in, 16)
            for m in range(4):
                sp.wait_ge(parts_out[m], 16 * NC)
            load_a(0, 0)
            copy_b(0, 0, 1)
            load_a(1, 1)
            for s in range(NC - 1):
                rows_out(0, s, s + 1)

            def slot(i, u, s):
                h = 2 * i + u
                if maxima_before(i, u, s):
                    rows_out(1 - u if s else u, (s - 1) % NC, NC * h + s + NC)
                if s == 1:
                    if not (isinstance(i, int) and h + 2 >= H):
                        load_a(h + 2, u)
                    if not (isinstance(i, int) and h + 1 >= H):
                        copy_b(h + 1, 1 - u, i + 1 + u)

            slots_of_loop(slot, sp)
            sp.wait_ge(a_scored, PER_HEAD * H)
            sp.wait_ge(x1_spill, 16 * NC)
            sp.dma_start(ops32[:, 0:4096], x1_dram.rearrange("p t d -> p (t d)")).then_inc(x1_in, 16)
            for n, pair in enumerate(PAIRS):
                sp.wait_ge(fin_x, n + 1)
                sp.dma_start(out[0].rearrange("(t p) d -> p t d", p=P)[:, 2 * pair:2 * pair + 2, :],
                             ops32[:, CH * pair:CH * pair + CH].rearrange("p (t d) -> p t d", d=D)).then_inc(out_st, 16)
            sp.wait_ge(out_st, 16 * (NT // 2))

        @block.gpsimd
        def _(pool):
            pool.dma_start(MASK[:, :, :], masks).then_inc(cast_in, 16)
            pool.dma_start(POSR[:, :, :], pos_rows, max_dma_last_dim=4096).then_inc(cast_in, 16)
            pool.memset(B2[:, :], 0.0).then_inc(b2_zero, 1)
            pool.memset(ONES[:, :], 1.0).then_inc(memset_done, 1)
            pool.memset(HALF[:, :], -0.5).then_inc(memset_done, 1)
            pool.memset(ONE1[:, 0, :], 1.0).then_inc(memset_done, 1)
            pool.memset(ONE1[:, 1, :], WS).then_inc(memset_done, 1)
            pool.memset(ZERO[:, :], 0.0).then_inc(memset_done, 1)
            pool.memset(ONEB[:, :], 1.0).then_inc(memset_done, 1)
            pool.memset(NIL[:, :], 0.0).then_inc(memset_done, 1)
            pool.memset(CAR[:, :, :], 0.0).then_inc(memset_done, 1)
            pool.memset(VS[:, :, :, HD + 1:32], 0.0).then_inc(memset_done, 1)
            pool.memset(VS[:, :, :, HD:HD + 1], 1.0).then_inc(memset_done, 1)

            def rstd(k, tiles):
                pool.wait_ge(var_eps, k)
                pool.tensor_tensor(RSTD[:, tiles], VEPS[:, tiles], HALF[:, 0:TC], ALU.pow).then_inc(rstd_done, 1)

            pool.wait_ge(memset_done, 10)
            for c in range(NC):
                rstd(c + 1, slice(TC * c, TC * c + TC))

            def front(c):
                for m in range(2):
                    pool.wait_ge(relus, 4 * c + m + 3)
                    wait(pool, numden, 2 * c)
                    pool.tensor_tensor(PH[:, 2 + m, :], EX[:, 2 + m, :], RE[:, 2 + m, :], ALU.add).then_inc(phi_q, 1)
                for m in range(2):
                    wait(pool, phi_q, 2 * c + m + 1)
                    wait(pool, scan_k, 2 * c + m + 1)
                    wait(pool, outT, 2 * c)
                    pool.tensor_tensor(DEN[:, m, :], PH[:, 2 + m, :], KC[:, m, :], ALU.mult).then_inc(nd, 1)
                    wait(pool, nd, 2 * c + m + 1)
                    pool.tensor_scalar(DEN[:, m, :], DEN[:, m, :], L0_EPS, None, ALU.add).then_inc(nd2, 1)
                    wait(pool, scan_kv, 2 * c + m + 1)
                    pool.tensor_tensor(NUM[:, m, :], PH[:, 2 + m, :], KVC[:, m, :], ALU.mult).then_inc(numden, 1)

            def back(c):
                for r in range(2):
                    wait(pool, gate_mid, 2 * c + r + 1)
                    xs = XO[:, ds(TC * c + 2 * r, 2), :].rearrange("p t d -> p (t d)")
                    pool.tensor_tensor(xs, xs, GT[:, r, :], ALU.add).then_inc(x1_add, 1)
                if c:
                    rstd(NC + c, ds(TC * c - TC, TC))

            def scale(q):
                for half in range(2):
                    if 2 * q >= E - 2:
                        pool.wait_ge(last_in[half], 16)
                    else:
                        pool.wait_ge(raw_in[half], 16 * q + 16)
                    pool.tensor_scalar(raw_of(2 * q + half), raw_of(2 * q + half), WS, 0.0, ALU.mult, ALU.add)\
                        .then_inc(w1_scaled, 1)

            def low_parts(q):
                for e in (2 * q, 2 * q + 1):
                    pool.wait_ge(w1h_done, e + 1)
                    pool.tensor_tensor(W1L[:, 1024 * e:1024 * e + 1024], raw_of(e), W1H[:, 1024 * e:1024 * e + 1024],
                                       ALU.subtract).then_inc(w1l_done, 1)

            front(0)
            scale(0)
            for c in range(NC - 1):
                front(c + 1)
                low_parts(c)
                back(c)
                if c + 1 < E // 2 - 1:
                    scale(c + 1)
            back(NC - 1)
            rstd(2 * NC, ds(TC * (NC - 1), TC))
            pool.wait_ge(outT, 2 * NC)
            pool.memset(WET[:, :], 0.0).then_inc(wet_zero, 1)
            scale(E // 2 - 1)
            pool.wait_ge(w1l_done, E - 2)
            low_parts(E // 2 - 1)

            def rows(h, par):
                for side in range(2):
                    pool.tensor_tensor(OPS[0:POS, par, side, :], POSR[:, side, :],
                                       SCL[:, side, ds(h, 1)].broadcast_to([POS, S]), ALU.mult).then_inc(opa_rows, 1)

            def values(h, par):
                pool.tensor_copy(VS[:, par, :, 0:HD], VV[:, :, ds(HD * h, HD)]).then_inc(vs_ready, 1)

            nought = NIL[:, 0:1].broadcast_to([P, TC])

            def maxima(par, k):
                pool.wait_ge(row_max, k)
                pool.tensor_tensor(NP[:, par, 0, :], NM[:, par, :], nought, ALU.add).then_inc(max_part, 1)
                pool.wait_ge(max_part, 5 * k - 4)
                pool.tensor_tensor(NR[:, par, 0, :], NM[:, par, :], NP[:, par, 0, :], ALU.subtract).then_inc(max_part, 1)
                pool.wait_ge(max_part, 5 * k - 3)
                pool.tensor_tensor(NP[:, par, 1, :], NR[:, par, 0, :], nought, ALU.add).then_inc(max_part, 1)
                pool.wait_ge(max_part, 5 * k - 2)
                pool.tensor_tensor(NR[:, par, 1, :], NR[:, par, 0, :], NP[:, par, 1, :], ALU.subtract).then_inc(max_part, 1)
                pool.wait_ge(max_part, 5 * k - 1)
                pool.tensor_tensor(NP[:, par, 2, :], NR[:, par, 1, :], nought, ALU.add).then_inc(max_part, 1)

            pool.wait_ge(scl, 8)
            pool.wait_ge(cast_in, 32)
            for m in range(4):
                pool.wait_ge(parts_out[m], 16 * NC)
            pool.wait_ge(w1l_done, E)
            for par in range(2):
                pool.memset(OPS[96:P, 2 + par, 1, :], 1.0).then_inc(ones_rows, 1)
            pool.wait_ge(ones_rows, 2)
            pool.wait_ge(opa_rows, 2)
            rows(1, 1)
            pool.wait_ge(v_copied, NT)
            values(0, 0)
            for s in range(NC):
                maxima(s % 2, s + 1)

            def slot(i, u, s):
                h = 2 * i + u
                if s == 1 and finds_maxima(i, u):
                    pool.wait_ge(up_ps, 2 * (NC * (h + 1) + UNITS[s][0][0]) + 1)
                    if not (isinstance(i, int) and h + 2 >= H):
                        rows(h + 2, u)
                    if not (isinstance(i, int) and h + 1 >= H):
                        values(h + 1, 1 - u)
                if finds_maxima(i, u):
                    maxima(s % 2, NC * (h + 1) + s + 1)

            slots_of_loop(slot, pool)

            pool.wait_ge(x1_in, 16)
            for n, pair in enumerate(PAIRS):
                pool.wait_ge(fin_b, n + 1)
                xs = ops32[:, CH * pair:CH * pair + CH]
                pool.tensor_tensor(xs, xs, GT[:, n % 2, :], ALU.add).then_inc(fin_x, 1)

        @block.scalar
        def _(act):
            act.dma_start(STG[:, 0:1536], w_qkv0.rearrange("p k n -> p (k n)")).then_inc(w_in0, 16)
            act.dma_start(IDN[:, :], ident).then_inc(const_in, 16)
            act.dma_start(SEL[:, :], sel).then_inc(const_in, 16)
            act.dma_start(WF[:, :, :], w_ffn).then_inc(w_ffn_in, 16)
            act.dma_start(WO0[:, :, :], w_out0).then_inc(w_out_in, 16)
            act.dma_start(BROW[0:1, 0:D], b_ffn).then_inc(small_in, 16)
            act.dma_start(BROW[0:1, 2 * D:3 * D], b_v1).then_inc(small_in, 16)
            act.dma_start(BROW[0:1, D:2 * D], b_out1).then_inc(small_in, 16)
            act.dma_start(BROW[0:1, 3 * D:], gate_b).then_inc(small_in, 16)
            act.dma_start(GW[:, :, :], gate_w).then_inc(small_in, 16)
            act.dma_start(BQK[:, :], b_qk1).then_inc(small_in, 16)
            act.dma_start(WO1[:, :, :], w_out1).then_inc(small_in, 16)
            act.dma_start(B1[:, :, :, :], b1).then_inc(small_in, 16)
            act.dma_start(SLB[:, :], slopes.broadcast_to([POS, H])).then_inc(small_in, 16)
            act.dma_start(PICK[:, :, :], pick).then_inc(small_in, 16)
            act.wait_ge(b2_zero, 1)
            act.dma_start(B2[0:E, :], b2).then_inc(small_in, 16)
            act.wait_ge(w_in0, 16)
            act.activation(W0H[:, :, :].rearrange("p k n -> p (k n)"), STG[:, 0:1536], ACT.Copy, scale=WS).then_inc(w0h, 1)

            def high(c, k0):
                for k in range(KK):
                    wait(act, xt_ps, k0 + KK * c + k + 1)
                    act.activation(XTH[:, k, ds(CH * c, CH)], PS[k][:, :], ACT.Copy).then_inc(xth, 1)

            def front(c):
                high(c, 0)
                for n, (m, t) in enumerate(((0, 0), (1, 1), (2, 4), (3, 5))):
                    wait(act, proj, 6 * c + t + 1)
                    wait(act, phi_k if m < 2 else phi_q, 2 * c)
                    bank = PS[2 + t % 4]
                    if m < 2:
                        act.activation(EX[:, m, :], bank[:, :], ACT.Exp, scale=1 / WS)
                    else:
                        act.activation(EX[:, m, :], bank[:, :], ACT.Relu, scale=-1 / WS).then_inc(negs, 1)
                        act.wait_ge(negs, 2 * c + m - 1)
                        act.activation(EX[:, m, :], EX[:, m, :], ACT.Exp, scale=-1.0)
                    act.activation(RE[:, m, :], bank[:, :], ACT.Relu, scale=1 / WS).then_inc(relus, 1)

            def back(c):
                for r in range(2):
                    wait(act, z_ps, 2 * c + r + 1)
                    if c:
                        wait(act, x1_add, 2 * c - 1 + r)
                    act.activation(TH[:, r, :], PS[6 + r][:, :], ACT.Tanh, scale=0.5)
                    act.activation(GT[:, r, :], PS[6 + r][:, :], ACT.Copy).then_inc(z_read, 1)

            def high_parts(q):
                for e in (2 * q, 2 * q + 1):
                    act.wait_ge(w1_scaled, e + 1)
                    act.activation(W1H[:, 1024 * e:1024 * e + 1024], raw_of(e), ACT.Copy).then_inc(w1h_done, 1)

            front(0)
            for k in range(KK):
                act.wait_ge(ffn_t, k + 1)
                act.activation(FH[:, k, :], PS[6 + k][:, 0:D], ACT.Copy).then_inc(ffn_h, 1)
            for c in range(NC - 1):
                front(c + 1)
                if c == 0:
                    act.wait_ge(w_q1_in, 16)
                    act.activation(WQH[:, :, 0:3 * D], STG3, ACT.Copy, scale=WS).then_inc(wq1h, 1)
                    act.wait_ge(small_in, 16 * 11)
                    act.activation(WQH[:, :, 3 * D:], GW[:, :, :], ACT.Copy, scale=WS).then_inc(wq1h, 1)
                high_parts(c)
                back(c)
            back(NC - 1)

            high(0, KK * NC)
            act.wait_ge(phi_q, 2 * NC)
            act.wait_ge(scan_kv, 2 * NC)
            act.wait_ge(numden, 2 * NC)
            def values(c, tiles):
                for t in tiles:
                    tile = TC * c + t
                    bank = PS[6 + tile % 2]
                    act.wait_ge(v_ps, tile + 1)
                    act.activation(VV[:, tile, :], bank[:, 0:D], ACT.Copy, scale=1 / WS).then_inc(v_copied, 1)
                    act.activation(LG[:, tile, :], bank[:, D:D + E], ACT.Copy, scale=1 / WS).then_inc(lg_copied, 1)

            act.wait_ge(gsplit, 1)
            for c in range(NC):
                for m in range(4):
                    side = m // 2
                    wait(act, qk_ps, 4 * c + m + 1)
                    wait(act, qk_r1, 4 * c)
                    scale = 1 / WS if side else HD ** -0.5 / WS
                    act.activation(QV[:, m, :], PS[2 + m][:, :], ACT.Identity, scale=scale,
                                   bias=BQK[:, m:m + 1]).then_inc(qk_v, 1)
                    wait(act, qk_v, 4 * c + m + 1)
                    wait(act, parts_out[m], 16 * c)
                    act.activation(QP[:, m, 0, :], QV[:, m, :], ACT.Copy).then_inc(qk_p0, 1)
                if c + 1 < NC:
                    high(c + 1, KK * NC)
                values(c, (0, 1))
                for m in range(4):
                    wait(act, qk_r1, 4 * c + m + 1)
                    act.activation(QP[:, m, 1, :], QR[:, m, :], ACT.Copy).then_inc(qk_p1, 1)
                values(c, (2, 3))
                if c == 1:
                    act.wait_ge(w1l_done, E - 2)
                    high_parts(E // 2 - 1)
            def gate_out(e, m, unit, f):
                act.wait_ge(up_ps, 2 * m + 1)
                if not (isinstance(m, int) and m < 2):
                    act.wait_ge(y_ready, m - 1)
                act.activation(TH[:, unit % 2, :], PS[5][:, :], ACT.Tanh, scale=0.851 / WS,
                               bias=B1T[:, ds(e, 1), f:f + 1].rearrange("p a b -> p (a b)"))
                act.activation(GT[:, unit % 2, :], PS[5][:, :], ACT.Identity,
                               bias=B1S[:, ds(e, 1), 0, f:f + 1].rearrange("p a b -> p (a b)")).then_inc(gate_read, 1)

            act.wait_ge(x1_add, 2 * NC)
            act.wait_ge(b1_prep, 1)
            for unit in range(NC):
                gate_out(0, unit, unit, unit % 2)
            act.wait_ge(scl, 8)
            act.wait_ge(cast_in, 32)
            for m in range(4):
                act.wait_ge(parts_out[m], 16 * NC)
            for side in range(2):
                act.activation(OPS[0:POS, 0, side, :], POSR[:, side, :], ACT.Copy, scale=SCL[:, side, 0:1])\
                    .then_inc(opa_rows, 1)
            act.wait_ge(route, 1)
            act.activation(TOP[:, 3, :], TOP[:, 2, :], ACT.Exp).then_inc(expd, 1)
            act.wait_ge(wet_zero, 1)
            for c in range(NC):
                act.wait_ge(wet_ps, c + 1)
                act.activation(WET[0:E, CH * c:CH * c + CH], PS[4 + c % 2][0:E, :], ACT.Copy).then_inc(wet_copied, 1)
            for r in range(NT // 2):
                act.wait_ge(b2_ps, r + 1)
                act.activation(ACC[:, 2 * r:2 * r + 2, :].rearrange("p t d -> p (t d)"), PS[4 + r % 2][:, :],
                               ACT.Copy).then_inc(acc_init, 1)

            def max_rows(par, k, dma):
                act.wait_ge(mt_ps, k)
                if dma is not None:
                    act.wait_ge(*dma)
                act.activation(MT[:, par, :], MTP, ACT.Copy).then_inc(mt_copied, 1)

            for s in range(NC - 1):
                max_rows(s % 2, s + 1, (mrow[s - 2], 16) if s >= 2 else None)

            def chunk_out(h, c):
                act.wait_ge(pv_done, PER_HEAD * h + OFF[c] + TILES[c])
                act.activation(U[:, c % 2, :], PS[4][:, :], ACT.Copy).then_inc(u_ready, 1)

            def end_out(n):
                pair = PAIRS[n]
                act.wait_ge(ye_added, NC * H)
                wait(act, fin_a, n - 1)
                act.activation(TH[:, n % 2, :], ACC[:, 2 * pair:2 * pair + 2, :].rearrange("p t d -> p (t d)"),
                               ACT.Tanh, scale=0.5).then_inc(fin_th, 1)
                act.wait_ge(ot_ps, n + 1)
                wait(act, fin_ps, n - 1)
                act.activation(TQ[:, n % 2, :], end_banks(n)[0][:, :], ACT.Copy).then_inc(ot_copied, 1)

            def slot(i, u, s):
                h = 2 * i + u
                for t in range(STEPS):
                    for n in ends_at(i, u, s, 2, t):
                        end_out(n)
                    for tile in tiles_at(s, t, steps_b(s)):
                        c, k = place(tile)
                        idx = PER_HEAD * h + tile
                        off = P * max(0, k - TC * ORDER[c])
                        act.wait_ge(b_scored, idx + 1)
                        if tile >= RING:
                            act.wait_ge(pv_done, idx + 1 - RING)
                        act.activation(PR[:, tile % RING, off:CH], b_bank(h, tile)[:, off:CH],
                                       ACT.Exp).then_inc(b_exped, 1)
                        ended = tile - lag_of(h) + 1
                        if ended in OFF[1:]:
                            chunk_out(h, OFF.index(ended) - 1)
                    for unit, f, _, _, _, _, t_tanh, _, _ in UNITS[s]:
                        if t == t_tanh and finds_maxima(i, u):
                            gate_out(expert_turn(i, u)[0], NC * (h + 1) + unit, unit, f)
                    if t == MAXC[s] and maxima_before(i, u, s):
                        sent = (mrow[(s + 1) % NC], 16 * (h + 1) + (16 if s == NC - 1 else 0))
                        max_rows((s - 1) % 2, NC * h + s + NC, sent)
                if s == NC - 1:
                    chunk_out(h, s)

            slots_of_loop(slot, act)
            for n in range(4, NT // 2):
                end_out(n)

        @block.vector
        def _(dve):
            def norm_stats(c, k0):
                for t in range(TC):
                    dve.bn_stats(BST[:, t, :], XO[:, ds(TC * c + t, 1), :].rearrange("p a d -> p (a d)"))\
                        .then_inc(stats, 1)
                for t in range(TC):
                    dve.wait_ge(stats, 2 * TC * (k0 + c) + TC)
                    dve.bn_aggr(MV[:, ds(TC * c + t, 1), :].rearrange("p a d -> p (a d)"), BST[:, t, :]).then_inc(stats, 1)
                dve.wait_ge(stats, 2 * TC * (k0 + c) + 2 * TC)
                dve.tensor_scalar(VEPS[:, ds(TC * c, TC)], MV[:, ds(TC * c, TC), 1:2].rearrange("p a d -> p (a d)"),
                                  LN_EPS, None, ALU.add).then_inc(var_eps, 1)

            def norm_apply(c, k0):
                dve.wait_ge(rstd_done, k0 + c + 1)
                if not (isinstance(c, int) and k0 + c == 0):
                    dve.wait_ge(xt_ps, KK * (k0 + c))
                for t in range(TC):
                    dve.tensor_scalar(XN[:, t, :],
                                      XO[:, ds(TC * c + t, 1), :].rearrange("p a d -> p (a d)"),
                                      MV[:, ds(TC * c + t, 1), 0:1].rearrange("p a d -> p (a d)"),
                                      RSTD[:, ds(TC * c + t, 1)], ALU.subtract, ALU.mult).then_inc(xn, 1)

            def low(c, k0):
                for k in range(KK):
                    wait(dve, xth, k0 + KK * c + k + 1)
                    dve.tensor_tensor(XTL[:, k, ds(CH * c, CH)], PS[k][:, :], XTH[:, k, ds(CH * c, CH)],
                                      ALU.subtract).then_inc(xtl, 1)

            for c in range(NC):
                dve.wait_ge(x_in[c], 16)
                norm_stats(c, 0)
                if c == 0:
                    norm_apply(0, 0)
                    dve.wait_ge(w0h, 1)
                    dve.scalar_tensor_tensor(W0L[:, :, :].rearrange("p k n -> p (k n)"), STG[:, 0:1536], WS,
                                             W0H[:, :, :].rearrange("p k n -> p (k n)"),
                                             ALU.mult, ALU.subtract).then_inc(w0l, 1)
                    low(0, 0)
                    dve.wait_ge(w_ffn_in, 16)
                    dve.tensor_reduce(TOP[:, 0, 0:KK], WF[:, :, :], AX.X, ALU.add, apply_absolute_value=True)\
                        .then_inc(ffn_thr, 1)
                    dve.wait_ge(ffn_thr, 1)
                    dve.tensor_scalar(TOP[:, 1, 0:KK], TOP[:, 0, 0:KK], 1.0 / D, 0.7, ALU.mult, ALU.mult)\
                        .then_inc(ffn_thr, 1)
                    dve.wait_ge(ffn_thr, 2)
                    dve.tensor_scalar(TOP[:, 2, 0:KK], TOP[:, 1, 0:KK], -1.0, None, ALU.mult).then_inc(ffn_thr, 1)
                    dve.wait_ge(ffn_thr, 3)
                    for k in range(KK):
                        dve.tensor_scalar(NF[:, k, :], WF[:, k, :], TOP[:, 2, k:k + 1], None, ALU.is_lt).then_inc(ffn_q, 1)
                    dve.wait_ge(ffn_q, 2)
                    for k in range(KK):
                        dve.scalar_tensor_tensor(QF[:, k, :], WF[:, k, :], TOP[:, 1, k:k + 1], NF[:, k, :],
                                                 ALU.is_gt, ALU.subtract).then_inc(ffn_q, 1)
                    dve.wait_ge(ffn_q, 4)
                    dve.tensor_tensor(QF[:, :, :], QF[:, :, :], WF[:, :, :], ALU.subtract).then_inc(ffn_q, 1)
                    dve.wait_ge(ffn_q, 5)
                    dve.tensor_tensor(QF[:, :, :], WF[:, :, :], QF[:, :, :], ALU.add).then_inc(ffn_q, 1)

            dve.wait_ge(memset_done, 10)

            def ternary_low():
                for k in range(KK):
                    dve.wait_ge(ffn_h, k + 1)
                    dve.tensor_tensor(FL[:, k, :], PS[6 + k][:, 0:D], FH[:, k, :], ALU.subtract).then_inc(ffn_split, 1)

            def split_next_weights():
                dve.wait_ge(wq1h, 2)
                dve.scalar_tensor_tensor(WQL[:, :, 0:3 * D], STG3, WS, WQH[:, :, 0:3 * D], ALU.mult, ALU.subtract).then_inc(wq1l, 1)
                dve.wait_ge(small_in, 16 * 11)
                dve.scalar_tensor_tensor(WQL[:, :, 3 * D:], GW[:, :, :], WS, WQH[:, :, 3 * D:], ALU.mult, ALU.subtract).then_inc(wq1l, 1)
                dve.tensor_scalar(BQK[:, 0:2], BQK[:, 0:2], HD ** -0.5, None, ALU.mult).then_inc(gsplit, 1)

            def front(c, more):
                if c:
                    low(c, 0)
                if more:
                    norm_apply(c + 1, 0)
                if c >= 2:
                    gated(c - 2)
                if c == 1:
                    ternary_low()
                if c == 2:
                    split_next_weights()
                for m in range(2):
                    wait(dve, relus, 4 * c + m + 1)
                    wait(dve, nd2, 2 * c)
                    dve.scalar_tensor_tensor(PH[:, m, :], EX[:, m, :], 1.0, RE[:, m, :], ALU.min, ALU.add)\
                        .then_inc(phi_k, 1)
                    wait(dve, phi_k, 2 * c + m + 1)
                    wait(dve, carry, 4 * c)
                    dve.tensor_tensor_scan(KC[:, m, :], ONES[:, 0:1].broadcast_to([P, CH]), PH[:, m, :], CAR[:, m, :], ALU.mult, ALU.add)\
                        .then_inc(scan_k, 1)
                for m in range(2):
                    wait(dve, proj, 6 * c + 3 + m)
                    dve.scalar_tensor_tensor(KV[:, m, :], PS[4 + m][:, :], 1 / WS, PH[:, m, :], ALU.mult, ALU.mult)\
                        .then_inc(v_read, 1)
                    wait(dve, v_read, 2 * c + m + 1)
                    wait(dve, numden, 2 * c)
                    dve.tensor_tensor_scan(KVC[:, m, :], ONES[:, 0:1].broadcast_to([P, CH]), KV[:, m, :], CAR[:, 2 + m, :], ALU.mult, ALU.add)\
                        .then_inc(scan_kv, 1)
                for m in range(2):
                    wait(dve, scan_k, 2 * c + m + 1)
                    dve.tensor_copy(CAR[:, m, :], KC[:, m, CH - 1:CH]).then_inc(carry, 1)
                    wait(dve, scan_kv, 2 * c + m + 1)
                    dve.tensor_copy(CAR[:, 2 + m, :], KVC[:, m, CH - 1:CH]).then_inc(carry, 1)

            def back(c):
                for m in range(2):
                    wait(dve, nd2, 2 * c + m + 1)
                    dve.reciprocal(DEN[:, m, :], DEN[:, m, :]).then_inc(rcp, 1)
                    wait(dve, rcp, 2 * c + m + 1)
                    wait(dve, numden, 2 * c + m + 1)
                    wait(dve, s_ps, 2 * c)
                    dve.tensor_tensor(OT0[:, m, :], NUM[:, m, :], DEN[:, m, :], ALU.mult).then_inc(outT, 1)

            def gate(c):
                for r in range(2):
                    wait(dve, z_read, 2 * c + r + 1)
                    dve.scalar_tensor_tensor(GT[:, r, :], TH[:, r, :], 1.0, GT[:, r, :], ALU.add, ALU.mult)\
                        .then_inc(gate_a, 1)

            def gated(c):
                for r in range(2):
                    wait(dve, gate_a, 2 * c + r + 1)
                    wait(dve, s_ps, 2 * c + r + 1)
                    dve.scalar_tensor_tensor(GT[:, r, :], PS[6 + r][:, :], 0.5 * HD ** -0.5, GT[:, r, :], ALU.mult, ALU.mult)\
                        .then_inc(gate_mid, 1)

            def next_stats(c):
                wait(dve, x1_add, 2 * c + 2)
                norm_stats(c, NC)

            front(0, True)
            for c in range(NC):
                if c + 1 < NC:
                    front(c + 1, c + 2 < NC)
                if c == NC - 1:
                    gated(c - 1)
                    norm_apply(0, NC)
                back(c)
                gate(c)
                if c:
                    next_stats(c - 1)
            low(0, KK * NC)
            gated(NC - 1)
            next_stats(NC - 1)

            def prepare():
                dve.tensor_copy(SLP[:, 0, :], SLB[:, :]).then_inc(slope_part, 1)
                dve.wait_ge(slope_part, 1)
                dve.tensor_tensor(SLR[:, :], SLB[:, :], SLP[:, 0, :], ALU.subtract).then_inc(slope_part, 1)
                dve.wait_ge(slope_part, 2)
                dve.tensor_copy(SLP[:, 1, :], SLR[:, :]).then_inc(slope_part, 1)
                dve.wait_ge(slope_part, 3)
                dve.tensor_tensor(SLR[:, :], SLR[:, :], SLP[:, 1, :], ALU.subtract).then_inc(slope_part, 1)
                dve.wait_ge(slope_part, 4)
                dve.tensor_copy(SLP[:, 2, :], SLR[:, :]).then_inc(slope_part, 1)
                dve.wait_ge(slope_part, 5)
                for side in range(2):
                    dve.tensor_scalar(SCL[:, side, :], SLP[:, 0, :], PICK[:, side, 0:1], PICK[:, side, 3:4],
                                      ALU.mult, ALU.add).then_inc(scl, 1)
                for j in (1, 2):
                    for side in range(2):
                        dve.wait_ge(scl, 2 * j)
                        dve.scalar_tensor_tensor(SCL[:, side, :], SLP[:, j, :], PICK[:, side, j:j + 1], SCL[:, side, :],
                                                 ALU.mult, ALU.add).then_inc(scl, 1)
                dve.tensor_scalar(B1S[:, :, 0, :], B1[:, :, 0, :], WS, None, ALU.mult).then_inc(scl, 1)
                dve.tensor_scalar(B1T[:, :, :], B1[:, :, 0, :], 0.851, None, ALU.mult).then_inc(scl, 1)
                dve.tensor_scalar(B1S[:, :, 1, :], B1[:, :, 1, :], 1.0, WS, ALU.add, ALU.mult).then_inc(b1_prep, 1)

            norm_apply(1, NC)
            for c in range(NC):
                for m in range(4):
                    wait(dve, qk_p0, 4 * c + m + 1)
                    wait(dve, qk_p2, 4 * c)
                    dve.tensor_tensor(QR[:, m, :], QV[:, m, :], QP[:, m, 0, :], ALU.subtract).then_inc(qk_r1, 1)
                if c + 1 < NC:
                    low(c + 1, KK * NC)
                if c + 2 < NC:
                    norm_apply(c + 2, NC)
                if c == 0:
                    prepare()
                for m in range(4):
                    wait(dve, qk_p1, 4 * c + m + 1)
                    dve.tensor_tensor(QP[:, m, 2, :], QR[:, m, :], QP[:, m, 1, :], ALU.subtract).then_inc(qk_p2, 1)

            def step(ins):
                ins.then_inc(rstep, 1)
                dve.wait_ge(rstep, step.n)
                step.n += 1
            step.n = 1

            def glu(m, unit):
                dve.wait_ge(gate_read, m + 1)
                dve.scalar_tensor_tensor(GT[:, unit % 2, :], TH[:, unit % 2, :], 1.0, GT[:, unit % 2, :],
                                         ALU.add, ALU.mult).then_inc(glu_done, 1)

            def linear(e, m, unit, f, buf):
                dve.wait_ge(up_ps, 2 * m + 2)
                dve.wait_ge(glu_done, m + 1)
                dve.scalar_tensor_tensor(YT[:, buf, f, :], PS[6][:, :],
                                         B1S[:, ds(e, 1), 1, f:f + 1].rearrange("p a b -> p (a b)"),
                                         GT[:, unit % 2, :], ALU.add, ALU.mult).then_inc(y_ready, 1)

            def add_expert(e, half, number, buf, pair):
                dve.wait_ge(ye_ps, number + 1)
                for q in range(2):
                    tile = TC * (2 * half + buf) + 2 * pair + q
                    add = dve.scalar_tensor_tensor(
                        ACC[:, tile, :], PS[7][:, D * q:D * q + D], WES[:, tile, ds(e, 1)],
                        ACC[:, tile, :], ALU.mult, ALU.add)
                add.then_inc(ye_added, 1)

            dve.wait_ge(lg_copied, NT)
            RANK, TMP, FIRST, SECOND = RT[:, 0], RT[:, 1], RT[:, 2], RT[:, 3]
            step(dve.memset(RANK, 0.0))
            for e in range(E):
                rival = LG[:, :, e:e + 1].broadcast_to([P, NT, E])
                if e:
                    step(dve.tensor_tensor(TMP[:, :, 0:e], rival[:, :, 0:e], LG[:, :, 0:e], ALU.is_gt))
                if e < E - 1:
                    step(dve.tensor_tensor(TMP[:, :, e + 1:E], rival[:, :, e + 1:E], LG[:, :, e + 1:E], ALU.is_ge))
                if e:
                    step(dve.tensor_tensor(RANK[:, :, 0:e], RANK[:, :, 0:e], TMP[:, :, 0:e], ALU.add))
                if e < E - 1:
                    step(dve.tensor_tensor(RANK[:, :, e + 1:E], RANK[:, :, e + 1:E], TMP[:, :, e + 1:E], ALU.add))
                unit = e // 2
                if e % 2:
                    linear(0, unit, unit, unit % 2, unit // 2)
                else:
                    glu(unit, unit)
            step(dve.tensor_scalar(FIRST, RANK, 0.0, None, ALU.is_equal))
            step(dve.tensor_scalar(SECOND, RANK, 1.0, None, ALU.is_equal))
            step(dve.tensor_tensor(TMP, FIRST, LG[:, :, :], ALU.mult))
            step(dve.tensor_reduce(TOP[:, 0, :], TMP, AX.X, ALU.add))
            step(dve.tensor_tensor(TMP, SECOND, LG[:, :, :], ALU.mult))
            step(dve.tensor_reduce(TOP[:, 1, :], TMP, AX.X, ALU.add))
            dve.tensor_tensor(TOP[:, 2, :], TOP[:, 1, :], TOP[:, 0, :], ALU.subtract).then_inc(route, 1)
            dve.wait_ge(expd, 1)
            step(dve.tensor_scalar(TOP[:, 0, :], TOP[:, 3, :], 1.0, None, ALU.add))
            step(dve.reciprocal(TOP[:, 1, :], TOP[:, 0, :]))
            step(dve.tensor_tensor(TOP[:, 2, :], TOP[:, 3, :], TOP[:, 1, :], ALU.mult))
            step(dve.tensor_tensor(FIRST, FIRST, TOP[:, 1, :].unsqueeze(2).broadcast_to([P, NT, E]), ALU.mult))
            step(dve.tensor_tensor(SECOND, SECOND, TOP[:, 2, :].unsqueeze(2).broadcast_to([P, NT, E]), ALU.mult))
            step(dve.tensor_tensor(WE[:, :, :], FIRST, SECOND, ALU.add))
            dve.tensor_scalar(WES[:, :, :], WE[:, :, :], 0.5 / WS ** 2, None, ALU.mult).then_inc(we_done, 1)

            def reduce_a(h40, tile, banks=2):
                c, k = place(tile)
                a = ORDER[c]
                xq, gg = k // (a + 1), k % (a + 1)
                width = CH if gg < a else P * (xq + 1)
                dve.wait_ge(a_scored, h40 + tile + 1)
                dve.tensor_reduce(PM[:, c % 2, xq, gg:gg + 1], PS[tile % banks][:, 0:width], AX.X, ALU.max)\
                    .then_inc(a_reduced, 1)

            def row_maxima(h40, s, k):
                a = ORDER[s]
                dve.wait_ge(a_reduced, h40 + OFF[s] + TILES[s])
                if not (isinstance(k, int) and k <= 2):
                    dve.wait_ge(mt_ps, k - 2)
                dve.tensor_reduce(NM[:, s % 2, :], PM[:, s % 2, :, 0:a + 1], AX.X, ALU.max, negate=True)\
                    .then_inc(row_max, 1)

            for s in range(NC):
                for k in range(TILES[s]):
                    reduce_a(0, OFF[s] + k, 4)
                    if OFF[s] + k in FIRST_FILLS:
                        fill = FIRST_FILLS.index(OFF[s] + k)
                        dve.wait_ge(acc_init, fill + 1)
                        add_expert(0, 0, fill, fill // 2, fill % 2)
                row_maxima(0, s, s + 1)

            outputs = PS[7][:, 0:TC * (HD + 1)].rearrange("p (q c) -> p q c", q=TC)

            def inverse(i, u, s):
                dve.wait_ge(o_ps, NC * (2 * i + u) + s + 1)
                dve.reciprocal(RC[:, s % 2, :], outputs[:, :, HD:HD + 1].rearrange("p q c -> p (q c)")).then_inc(o_rc, 1)

            def divide(i, u, s):
                b = ORDER[s]
                dve.wait_ge(o_rc, NC * (2 * i + u) + s + 1)
                dve.tensor_tensor(XO[:, TC * b:TC * b + TC, ds(HD * (2 * i + u), HD)], outputs[:, :, 0:HD],
                                  RC[:, s % 2, :].unsqueeze(2).broadcast_to([P, TC, HD]), ALU.mult)\
                    .then_inc(o_normed, 1)

            def end_gate(n):
                dve.wait_ge(fin_th, n + 1)
                wait(dve, fin_x, n - 1)
                dve.scalar_tensor_tensor(GT[:, n % 2, :], TH[:, n % 2, :], 1.0,
                                         ACC[:, 2 * PAIRS[n]:2 * PAIRS[n] + 2, :].rearrange("p t d -> p (t d)"),
                                         ALU.add, ALU.mult).then_inc(fin_a, 1)

            def end_product(n):
                dve.wait_ge(fin_a, n + 1)
                dve.wait_ge(fin_ps, n + 1)
                dve.scalar_tensor_tensor(GT[:, n % 2, :], end_banks(n)[1][:, :], 0.5, GT[:, n % 2, :], ALU.mult,
                                         ALU.mult).then_inc(fin_b, 1)

            def slot(i, u, s):
                h = 2 * i + u
                prev = prev_of(i, u, s)
                for t in range(STEPS):
                    if finds_maxima(i, u):
                        for tile in tiles_at(s, t):
                            reduce_a(PER_HEAD * (h + 1), tile)
                    if finds_maxima(i, u):
                        e, half = expert_turn(i, u)
                        for unit, f, buf, _, _, _, _, t_gate, t_out in UNITS[s]:
                            if t == t_gate:
                                glu(NC * (h + 1) + unit, unit)
                            if t == t_out:
                                linear(e, NC * (h + 1) + unit, unit, f, buf)
                        for fill, buf, pair, _, t_add in FILLS[s]:
                            if t == t_add:
                                add_expert(e, half, NC * (h + 1) + fill, buf, pair)
                    for n in ends_at(i, u, s, 3, t):
                        end_gate(n)
                    for n in ends_at(i, u, s, 5, t):
                        end_product(n)
                    if t == RCP[s] and prev:
                        inverse(*prev)
                    if t == NORM[s] and prev:
                        divide(*prev)
                if finds_maxima(i, u):
                    row_maxima(PER_HEAD * (h + 1), s, NC * (h + 1) + s + 1)

            dve.wait_ge(x1_spill, 16 * NC)
            dve.wait_ge(acc_init, NT // 2)
            slots_of_loop(slot, dve)
            inverse(H // 2 - 1, 1, NC - 1)
            divide(H // 2 - 1, 1, NC - 1)
            for n in range(4, NT // 2):
                end_gate(n)
                end_product(n)

        @block.tensor
        def _(pe):
            mm = pe.matmul

            def transposes(c, k0):
                pe.wait_ge(xn, TC * (k0 + c) + TC)
                for k in range(KK):
                    for t in range(TC):
                        last = pe.transpose(PS[k][:, P * t:P * t + P],
                                            XN[:, t, P * k:P * k + P],
                                            IDN[:, :])
                    last.then_inc(xt_ps, 1)

            def pairs(out, weight, data, weight_first, last=True, first=True):
                for k in range(KK):
                    for j, (wp, dp) in enumerate(((0, 0), (1, 0), (0, 1))):
                        w, d = weight[wp](k), data[dp](k)
                        done = mm(out, w if weight_first else d, d if weight_first else w,
                                  start=first and k == 0 and j == 0, stop=last and k == KK - 1 and j == 2)
                return done

            def x_cols(c):
                return [lambda k: XTH[:, k, ds(CH * c, CH)], lambda k: XTL[:, k, ds(CH * c, CH)]]

            def x_tile(c, t):
                return [lambda k: XTH[:, k, ds(CH * c + P * t, P)], lambda k: XTL[:, k, ds(CH * c + P * t, P)]]

            def front(c):
                wait(pe, xth, KK * c + KK)
                wait(pe, xtl, KK * c + KK)
                for t, m in enumerate((2, 3, 4, 5, 0, 1)):
                    if t < 2:
                        wait(pe, relus, 4 * c)
                    elif t < 4:
                        wait(pe, v_read, 2 * c)
                    else:
                        wait(pe, relus, 4 * c + t - 3)
                    cols = slice(P * m, P * m + P)
                    pairs(PS[2 + t % 4][:, :], [lambda k: W0H[:, k, cols], lambda k: W0L[:, k, cols]],
                          x_cols(c), True).then_inc(proj, 1)

            def back(c):
                for r in range(2):
                    if c:
                        wait(pe, gate_mid, 2 * c - 1 + r)
                    for q in range(2):
                        mm(PS[6 + r][:, D * q:D * q + D], ONE1[0:1, 0, :], BROW[0:1, 0:D], start=True, stop=False)
                        last = pairs(PS[6 + r][:, D * q:D * q + D], [lambda k: FH[:, k, :], lambda k: FL[:, k, :]],
                                     x_tile(c, 2 * r + q), False, first=False)
                    last.then_inc(z_ps, 1)
                if c + 2 < NC:
                    transposes(c + 2, 0)
                if c == NC - 1:
                    transposes(0, NC)
                for r in range(2):
                    wait(pe, z_read, 2 * c + r + 1)
                    wait(pe, outT, 2 * c + 2)
                    for q in range(2):
                        for k in range(KK):
                            last = mm(PS[6 + r][:, D * q:D * q + D], OT0[:, k, P * (2 * r + q):P * (2 * r + q) + P],
                                      WO0[:, k, :], start=k == 0, stop=k == KK - 1)
                    last.then_inc(s_ps, 1)

            pe.wait_ge(const_in, 32)
            transposes(0, 0)
            pe.wait_ge(w0l, 1)
            front(0)
            transposes(1, 0)
            pe.wait_ge(ffn_q, 6)
            for k in range(KK):
                for o in range(KK):
                    last = pe.transpose(PS[6 + k][:, P * o:P * o + P], QF[:, o, P * k:P * k + P], IDN[:, :])
                last.then_inc(ffn_t, 1)
            for c in range(NC - 1):
                front(c + 1)
                if c == 0:
                    pe.wait_ge(small_in, 16 * 11)
                    pe.wait_ge(ffn_split, 2)
                    pe.wait_ge(w_out_in, 16)
                    pe.wait_ge(memset_done, 10)
                back(c)
            back(NC - 1)

            pe.wait_ge(wq1l, 2)
            pe.wait_ge(relus, 4 * NC)
            for c in range(NC):
                pe.wait_ge(xth, KK * (NC + c) + KK)
                pe.wait_ge(xtl, KK * (NC + c) + KK)
                for m in range(4):
                    wait(pe, qk_v, 4 * c)
                    cols = slice(P * m, P * m + P)
                    pairs(PS[2 + m][:, :], [lambda k: WQH[:, k, cols], lambda k: WQL[:, k, cols]],
                          x_cols(c), True).then_inc(qk_ps, 1)
                if c + 1 < NC:
                    transposes(c + 1, NC)
                cols = slice(2 * D, 3 * D + E)
                for t in range(TC):
                    tile = TC * c + t
                    bank = PS[6 + tile % 2][:, 0:D + E]
                    if tile == 0:
                        pe.wait_ge(gate_mid, 2 * NC)
                    if tile >= 2:
                        pe.wait_ge(lg_copied, tile - 1)
                    mm(bank, ONE1[0:1, 1, :], BROW[0:1, 2 * D:], start=True, stop=False)
                    pairs(bank, [lambda k: WQH[:, k, cols], lambda k: WQL[:, k, cols]], x_tile(c, t), False,
                          first=False).then_inc(v_ps, 1)

            def up(e, half, m, unit, f, part, j):
                if j == 0 and not (isinstance(m, int) and m == 0):
                    pe.wait_ge(y_ready if part else gate_read, m)
                k, (wp, dp) = j // 3, ((0, 0), (1, 0), (0, 1))[j % 3]
                col = ((part * 2 + f) * KK + k) * P
                tok = CH * (2 * half + unit // 2)
                last = mm(PS[5 + part][:, :], (W1L if wp else W1H)[:, ds(1024 * e + col, P)],
                          (XTL if dp else XTH)[:, k, tok:tok + CH], start=j == 0, stop=j == 5)
                if j == 5:
                    last.then_inc(up_ps, 1)

            def down(e, buf, pair):
                for q in range(2):
                    for f in range(KK):
                        tok = P * (2 * pair + q)
                        last = mm(PS[7][:, D * q:D * q + D], YT[:, buf, f, tok:tok + P],
                                  W2[:, ds(e, 1), f, :].rearrange("p a d -> p (a d)"), start=f == 0, stop=f == KK - 1)
                last.then_inc(ye_ps, 1)

            pe.wait_ge(w1l_done, 1)
            pe.wait_ge(qk_v, 4 * NC)
            pe.wait_ge(lg_copied, NT)
            for unit in range(NC):
                for part in range(2):
                    for j in range(6):
                        up(0, 0, unit, unit, unit % 2, part, j)

            def turn_routing(c):
                pe.wait_ge(we_done, 1)
                if c >= 2:
                    pe.wait_ge(wet_copied, c - 1)
                for t in range(TC):
                    last = pe.transpose(PS[4 + c % 2][0:E, P * t:P * t + P], WE[:, TC * c + t, :], IDN[:, :])
                last.then_inc(wet_ps, 1)

            def output_biases(r):
                if r == 0:
                    pe.wait_ge(wet_copied, NC)
                if r >= 2:
                    pe.wait_ge(acc_init, r - 1)
                for q in range(2):
                    tile = 2 * r + q
                    last = mm(PS[4 + r % 2][:, D * q:D * q + D], WET[:, P * tile:P * tile + P], B2[:, :],
                              start=True, stop=True)
                last.then_inc(b2_ps, 1)

            def score_a(h40, par, tile, banks=2):
                c, k = place(tile)
                a = ORDER[c]
                xq, gg = k // (a + 1), k % (a + 1)
                width = CH if gg < a else P * (xq + 1)
                idx = h40 + tile
                if not (isinstance(idx, int) and idx < banks):
                    pe.wait_ge(a_reduced, idx + 1 - banks)
                bank = PS[tile % banks]
                last = mm(bank[:, 0:width], OPS[0:ROWS_A, par, 0, P * (TC * a + xq):P * (TC * a + xq) + P],
                          OPS[0:ROWS_A, par, 1, CH * gg:CH * gg + width], start=True, stop=gg < a)
                if gg == a:
                    last = mm(bank[:, P * xq:P * xq + P], MASK[:, 0, :], MASK[:, 2, :], start=False, stop=True)
                last.then_inc(a_scored, 1)

            def turn_maxima(par, k):
                pe.wait_ge(max_part, 5 * k)
                pe.transpose(MTP, NP[:, par, :, :].rearrange("p j q -> p (j q)"), MASK[:, 2, :]).then_inc(mt_ps, 1)

            pe.wait_ge(cast_in, 32)
            pe.wait_ge(opa_in[0], 16 * 6)
            pe.wait_ge(opa_rows, 2)
            for s in range(NC):
                for k in range(TILES[s]):
                    tile = OFF[s] + k
                    score_a(0, 0, tile, 4)
                    if tile % 2 and tile // 2 < NC:
                        turn_routing(tile // 2)
                    elif tile % 2 and tile // 2 < NC + NT // 2:
                        output_biases(tile // 2 - NC)
                    if tile in FIRST_FILLS:
                        fill = FIRST_FILLS.index(tile)
                        if fill % 2:
                            pe.wait_ge(ye_added, fill)
                        else:
                            pe.wait_ge(w2_in, 16)
                            pe.wait_ge(mt_copied, fill // 2 + 1)
                        down(0, fill // 2, fill % 2)
                if s:
                    if s >= 2:
                        pe.wait_ge(mt_copied, s - 1)
                        pe.wait_ge(ye_added, 2 * (s - 1))
                    turn_maxima((s - 1) % 2, s)

            def score_b(h, u, tile):
                c, k = place(tile)
                b = ORDER[c]
                off = P * max(0, k - TC * b)
                idx = PER_HEAD * h + tile
                if lag_of(h) == LAG or tile < 2:
                    if not (isinstance(idx, int) and idx < 2):
                        pe.wait_ge(b_exped, idx - 1)
                elif tile < 4:
                    pe.wait_ge(a_reduced, PER_HEAD * H)
                else:
                    pe.wait_ge(b_exped, idx - 3)
                if k == 0:
                    pe.wait_ge(mrow[c], 16 * h + 16)
                bank = b_bank(h, tile)
                last = mm(bank[:, off:CH], OPS[0:ROWS_B, 2 + u, 1, P * k:P * k + P],
                          OPS[0:ROWS_B, 2 + u, 0, CH * b + off:CH * b + CH], start=True, stop=k < TC * b)
                if k >= TC * b:
                    last = mm(bank[:, off:off + P], MASK[:, 1, :], MASK[:, 2, :], start=False, stop=True)
                last.then_inc(b_scored, 1)

            def value(h, u, tile):
                c, k = place(tile)
                b = ORDER[c]
                off = P * max(0, k - TC * b)
                idx = PER_HEAD * h + tile
                if k == 0:
                    if not (isinstance(idx, int) and idx == 0):
                        pe.wait_ge(u_ready, NC * h + c)
                    if b == 0:
                        mm(PS[4][:, :], ZERO[:, :], ONEB[:, :], start=True, stop=True, skip_group_check=True)
                pe.wait_ge(b_exped, idx + 1)
                quad = 32 * (k % TC)
                mm(PS[4][quad:quad + 32, off:CH], VS[:, u, k, :], PR[:, tile % RING, off:CH],
                   start=b > 0 and k < TC, stop=k >= TC * b, skip_group_check=True, tile_position=(0, quad))\
                    .then_inc(pv_done, 1)

            def heads_out(s):
                for q in range(TC):
                    last = mm(PS[7][:, (HD + 1) * q:(HD + 1) * q + HD + 1], U[:, s % 2, P * q:P * q + P], SEL[:, :],
                              start=True, stop=True)
                last.then_inc(o_ps, 1)

            def bank7_read(i, u, s, t):
                n = NC * (2 * i + u) + s
                kind, m, number = last_in_bank7(s, t, n)
                if kind == "fill":
                    q = s if m is n else (s - 1) % NC
                    pe.wait_ge(ye_added, m - q + NC + sum(len(FILLS[r]) for r in range(q)) + number)
                elif kind == "outputs":
                    pe.wait_ge(o_normed, m)
                elif kind == "maxima":
                    pe.wait_ge(mt_copied, m + NC)

            def end_turn(n):
                chunk = n // 2
                pe.wait_ge(o_normed, NC * (H - 1) + chunk + 1)
                wait(pe, ot_copied, banks_before(n))
                if n == 5:
                    pe.wait_ge(b_exped, PER_HEAD * H)
                for k in range(KK):
                    for t in range(2):
                        last = pe.transpose(end_banks(n)[0][:, P * (2 * k + t):P * (2 * k + t) + P],
                                            XO[:, 2 * PAIRS[n] + t, P * k:P * k + P], IDN[:, :])
                last.then_inc(ot_ps, 1)

            def end_project(n):
                wait(pe, fin_b, banks_before(n))
                pe.wait_ge(ot_copied, n + 1)
                for t in range(2):
                    o = end_banks(n)[1][:, D * t:D * t + D]
                    mm(o, ONE1[0:1, 0, :], BROW[0:1, D:2 * D], start=True, stop=False)
                    for k in range(KK):
                        last = mm(o, TQ[:, n % 2, P * (2 * k + t):P * (2 * k + t) + P], WO1[:, k, :],
                                  start=False, stop=k == KK - 1)
                last.then_inc(fin_ps, 1)

            def slot(i, u, s):
                h = 2 * i + u
                prev = prev_of(i, u, s)
                if s == 0:
                    if finds_maxima(i, u):
                        pe.wait_ge(opa_in[1 - u], 16 * 6 * (i + 1 + u))
                        pe.wait_ge(opa_rows, 2 * h + 4)
                    pe.wait_ge(opb_in[u], 16 * (i + 1))
                    pe.wait_ge(vs_ready, h + 1)
                for t in range(STEPS):
                    if finds_maxima(i, u):
                        for tile in tiles_at(s, t):
                            score_a(PER_HEAD * (h + 1), 1 - u, tile)
                    for tile in tiles_at(s, t, steps_b(s)):
                        score_b(h, u, tile)
                        for n in values_after(tile, lag_of(h)):
                            value(h, u, n)
                    if s == NC - 1 and t == STEPS - 2:
                        for k in range(PER_HEAD - lag_of(h), PER_HEAD - 1):
                            value(h, u, k)
                    if s == NC - 1 and t == STEPS - 1:
                        value(h, u, PER_HEAD - 1)
                    for n in ends_at(i, u, s, 1, t):
                        end_turn(n)
                    for n in ends_at(i, u, s, 4, t):
                        end_project(n)
                    if t == MAXT[s] and maxima_before(i, u, s):
                        bank7_read(i, u, s, t)
                        turn_maxima((s - 1) % 2, NC * h + s + NC)
                    if t == HEADS[s] and prev:
                        pe.wait_ge(u_ready, NC * h + s)
                        bank7_read(i, u, s, t)
                        heads_out(prev[2])
                    if finds_maxima(i, u):
                        e, half = expert_turn(i, u)
                        for unit, f, _, t_g, t_l, rate, _, _, _ in UNITS[s]:
                            for part, start in ((0, t_g), (1, t_l)):
                                for j in range(max(0, rate * (t - start)), max(0, min(6, rate * (t - start + 1)))):
                                    up(e, half, NC * (h + 1) + unit, unit, f, part, j)
                        for fill, buf, pair, t_f, _ in FILLS[s]:
                            if t == t_f:
                                pe.wait_ge(y_ready, NC * (h + 1) + 2 * buf + 2)
                                bank7_read(i, u, s, t)
                                down(e, buf, pair)

            pe.wait_ge(acc_init, NT // 2)
            pe.wait_ge(w1l_done, E)
            pe.wait_ge(a_reduced, PER_HEAD)
            pe.wait_ge(mt_copied, NC - 1)
            pe.wait_ge(ye_added, NC)
            slots_of_loop(slot, pe)
            end_turn(4)
            pe.wait_ge(u_ready, NC * H)
            pe.wait_ge(ye_added, NC * H)
            pe.wait_ge(o_normed, NC * H - 1)
            heads_out(NC - 1)
            for n in range(4, NT // 2):
                if n + 1 < NT // 2:
                    end_turn(n + 1)
                end_project(n)


def _rows(w):
    import numpy as np
    return np.ascontiguousarray(w.reshape(w.shape[0] // P, P, *w.shape[1:]).swapaxes(0, 1))


def _shape_constants():
    import numpy as np
    q, k = np.arange(P)[:, None], np.arange(P)[None, :]
    far = -float(2 ** 30)
    masks = np.stack([np.where(q > k, far, 0.0),
                      np.where(q < k, far, 0.0),
                      np.eye(P)], 1)
    pos = np.arange(S)
    high, low, one = pos // P * P, pos % P, np.ones(S)
    side_q = [one, -high, one, -low] * 3
    side_k = [high, one, low, one] * 3
    pos_rows = np.stack([side_q, side_k], 1).reshape(POS, 2, S)
    pick = np.zeros((POS, 2, 4), np.float32)
    for r in range(POS):
        pick[r, 0, r // 4 if r % 2 == 0 else 3] = 1
        pick[r, 1, r // 4 if r % 2 == 1 else 3] = 1
    sel = np.zeros((P, HD + 1), np.float32)
    for p in range(P):
        if p % 32 <= HD:
            sel[p, p % 32] = 1
    return pos_rows.astype(np.float32), pick, masks.astype(np.float32), np.eye(P, dtype=np.float32), sel


def kernel(L0_attn_x, L0_attn_W_qkv, L0_attn_W_out, L0_ffn_weight, L0_ffn_bias, L1_attn_qkv_w, L1_attn_qkv_b,
           L1_attn_out_w, L1_attn_out_b, L1_attn_alibi_slopes, L1_ffn_gate_w, L1_ffn_gate_b, L1_ffn_w1, L1_ffn_b1,
           L1_ffn_w2, L1_ffn_b2):
    import numpy as np
    import concourse.bacc as bacc
    from concourse.bass_utils import run_bass_kernel_spmd

    a = [np.asarray(v) for v in (L0_attn_x, L0_attn_W_qkv, L0_attn_W_out, L0_ffn_weight, L0_ffn_bias, L1_attn_qkv_w,
                                 L1_attn_qkv_b, L1_attn_out_w, L1_attn_out_b, L1_attn_alibi_slopes, L1_ffn_gate_w,
                                 L1_ffn_gate_b, L1_ffn_w1, L1_ffn_b1, L1_ffn_w2, L1_ffn_b2)]
    x, wqkv0, wout0, wf, bf, wqkv1, bqkv1, wout1, bout1, slopes, gw, gb, w1, b1, w2, b2 = a
    pos_rows, pick, masks, ident, sel = _shape_constants()
    w1v = w1.reshape(E, 2, P, 2, KK, P).transpose(5, 0, 3, 1, 4, 2).reshape(P, E * 1024)
    b1v = b1.reshape(E, 2, P, 2).transpose(2, 0, 3, 1)
    w2v = w2.reshape(E, D, KK, P).transpose(3, 0, 2, 1)
    arrays = dict(
        x=x, w_qkv0=_rows(wqkv0.T), w_out0=_rows(wout0.T), w_ffn=_rows(wf), b_ffn=bf[None],
        w_qkv1=_rows(wqkv1.T), b_qk1=bqkv1[:2 * D].reshape(4, P).T, b_v1=bqkv1[None, 2 * D:], w_out1=_rows(wout1.T),
        b_out1=bout1[None], slopes=slopes[None], pos_rows=pos_rows, pick=pick, masks=masks, ident=ident, sel=sel,
        gate_w=_rows(gw.T), gate_b=gb[None], w1=w1v, b1=b1v, w2=w2v, b2=b2)
    nc = bacc.Bacc("TRN2", target_bir_lowering=False, num_devices=1)
    ins, feed = {}, {}
    for name, v in arrays.items():
        v = np.ascontiguousarray(v)
        feed["in_" + name] = v
        ins[name] = nc.dram_tensor("in_" + name, v.shape, mybir.dt.from_np(v.dtype), kind="ExternalInput").ap()
    out = nc.dram_tensor("out_rows", (1, S, D), F32, kind="ExternalOutput").ap()
    build(nc, out=out, **ins)
    return run_bass_kernel_spmd(nc, [feed], core_ids=[0]).results[0]["out_rows"]
```
